# Optimizing a Trainium2 kernel written in Bass

```python
import numpy as np
import jax
import jax.numpy as jnp

def _softmax(x, axis=-1):
    return jax.nn.softmax(x, axis=axis)

def _gelu(x):
    return jax.nn.gelu(x, approximate=True)

def _silu(x):
    return jax.nn.silu(x)

def _sigmoid(x):
    return jax.nn.sigmoid(x)

def _layernorm(x, axis=-1, eps=1e-05):
    m = jnp.mean(x, axis=axis, keepdims=True)
    v = jnp.var(x, axis=axis, keepdims=True)
    return (x - m) / jnp.sqrt(v + eps)

def _scatter_add(tgt, idx, src, axis=0):
    return tgt.at[idx].add(src)

def _segment_sum(src, seg, n):
    return jax.ops.segment_sum(src, seg, n)
kernel_name = 'mk_xattn_ffn_d4_seqx_r8_7ad34a'

def setup_inputs(seed: int=0):
    np.random.seed(seed)
    _w = jnp.asarray

    def _rec_inputs():
        import jax
        import jax.numpy as jnp
        _rk = jax.random.key(seed)
        x = -0.0003929 + 0.9999 * jax.random.normal(jax.random.fold_in(_rk, 1), (8, 128, 512), jnp.float32)
        _lenS = 128 - jax.random.randint(jax.random.fold_in(_rk, 7), (8,), 0, max(1, 128 // 4) + 1, jnp.int32)
        _lenS2 = 128 - jax.random.randint(jax.random.fold_in(_rk, 8), (8,), 0, max(1, 128 // 4) + 1, jnp.int32)
        _ctx_4096P = jax.random.normal(jax.random.fold_in(_rk, 11), (8, 16, 512), jnp.float32)
        _ctx_4096c = jax.random.dirichlet(jax.random.fold_in(_rk, 511), 0.3 * jnp.ones((16,), jnp.float32), (8, 128))
        _ctx_4096t = jnp.einsum('bsk,bkd->bsd', _ctx_4096c, _ctx_4096P)
        _ctx_4096t = _ctx_4096t * jax.lax.rsqrt(jnp.mean(jnp.square(_ctx_4096t)) + 1e-12) * 0.953939
        ctx_4096 = 2.81802e-05 + 1.00001 * (_ctx_4096t + 0.3 * jax.random.normal(jax.random.fold_in(_rk, 611), (8, 128, 512), jnp.float32))
        _validS = jnp.arange(128)[None, :] < _lenS[:, None]
        _validS2 = jnp.arange(128)[None, :] < _lenS2[:, None]
        _causal = jnp.tril(jnp.ones((128, 128), dtype=bool))
        mask_1x1xSxS2_ff0 = jnp.where(jnp.ones((1, 1, 128, 128), dtype=bool), 0.0, -1000000000.0).astype(jnp.float32)
        return (x, ctx_4096, mask_1x1xSxS2_ff0)
    x, ctx_4096, mask_1x1xSxS2_ff0 = _rec_inputs()

    def _L0_xattn_setup():
        import jax, jax.numpy as jnp
        import numpy as np
        EMBED = 512
        NUM_Q = 32
        NUM_KV = 8
        GROUPS = NUM_Q // NUM_KV
        HEAD_DIM = EMBED // NUM_Q
        KV_DIM = HEAD_DIM * NUM_KV
        key = jax.random.key(seed)
        ks = jax.random.split(key, 12)
        B, S = (2, 256)
        s = 0.02
        return {'query': jax.random.normal(ks[0], (B, S, EMBED), jnp.float32), 'key': jax.random.normal(ks[1], (B, S, EMBED), jnp.float32), 'value': jax.random.normal(ks[2], (B, S, EMBED), jnp.float32), 'Wq': jax.random.normal(ks[3], (EMBED, EMBED), jnp.float32) * s, 'bq': jnp.zeros((EMBED,), jnp.float32), 'Wk': jax.random.normal(ks[4], (EMBED, KV_DIM), jnp.float32) * s, 'bk': jnp.zeros((KV_DIM,), jnp.float32), 'Wv': jax.random.normal(ks[5], (EMBED, KV_DIM), jnp.float32) * s, 'bv': jnp.zeros((KV_DIM,), jnp.float32), 'Wo': jax.random.normal(ks[6], (EMBED, EMBED), jnp.float32) * s, 'bo': jnp.zeros((EMBED,), jnp.float32)}
    _L0_xattn_all = _L0_xattn_setup()
    _L0_xattn_in = {k: v for k, v in _L0_xattn_all.items() if k in ('Wq', 'bq', 'Wk', 'bk', 'Wv', 'bv', 'Wo', 'bo')}
    del _L0_xattn_all

    def _L0_ffn_setup():
        import jax, jax.numpy as jnp
        import numpy as np
        B, S, IN, OUT = (4, 256, 512, 512)
        E, K, R = (8, 2, 16)
        CAP_FACTOR = 3.0
        ALPHA = 1.0 / R
        LN_EPS = 1e-05
        key = jax.random.key(seed)
        ks = jax.random.split(key, 6)
        return {'x': jax.random.normal(ks[0], (B, S, IN), dtype=jnp.float32), 'weight': jax.random.normal(ks[1], (OUT, IN), dtype=jnp.float32) * 0.02, 'lora_A': jax.random.normal(ks[2], (E, IN, R), dtype=jnp.float32) / np.sqrt(R), 'lora_B': jax.random.normal(ks[3], (E, R, OUT), dtype=jnp.float32) * 0.02, 'gw1': jax.random.normal(ks[4], (4 * E, IN), dtype=jnp.float32) * 0.02, 'gb1': jnp.zeros((4 * E,), dtype=jnp.float32), 'ln_gamma': jnp.ones((4 * E,), dtype=jnp.float32), 'ln_beta': jnp.zeros((4 * E,), dtype=jnp.float32), 'gw2': jax.random.normal(ks[5], (E, 4 * E), dtype=jnp.float32) * 0.02, 'gb2': jnp.zeros((E,), dtype=jnp.float32)}
    _L0_ffn_all = _L0_ffn_setup()
    _L0_ffn_in = {k: v for k, v in _L0_ffn_all.items() if k in ('weight', 'lora_A', 'lora_B', 'gw1', 'gb1', 'ln_gamma', 'ln_beta', 'gw2', 'gb2')}
    del _L0_ffn_all

    def _L1_xattn_setup():
        import jax, jax.numpy as jnp
        import numpy as np
        B, Q, K, D = (1, 128, 6404, 512)
        H, KVH, HD = (32, 8, 128)
        GROUPS = H // KVH
        EPS = 1e-05

        def _rmsnorm(x, w):
            xf = x.astype(jnp.float32)
            var = jnp.mean(xf * xf, axis=-1, keepdims=True)
            return (xf * jax.lax.rsqrt(var + EPS)).astype(x.dtype) * w
        key = jax.random.key(seed)
        ks = jax.random.split(key, 8)
        s = 0.02
        return {'hidden_states': jax.random.normal(ks[0], (B, Q, D), jnp.float32), 'cross_attention_states': jax.random.normal(ks[1], (B, K, D), jnp.float32), 'attention_mask': jnp.zeros((B, 1, Q, K), jnp.float32), 'Wq': jax.random.normal(ks[2], (H * HD, D), jnp.float32) * s, 'Wk': jax.random.normal(ks[3], (KVH * HD, D), jnp.float32) * s, 'Wv': jax.random.normal(ks[4], (KVH * HD, D), jnp.float32) * s, 'Wo': jax.random.normal(ks[5], (D, H * HD), jnp.float32) * s, 'q_norm_w': jnp.ones((HD,), jnp.float32), 'k_norm_w': jnp.ones((HD,), jnp.float32)}
    _L1_xattn_all = _L1_xattn_setup()
    _L1_xattn_in = {k: v for k, v in _L1_xattn_all.items() if k in ('Wq', 'Wk', 'Wv', 'Wo', 'q_norm_w', 'k_norm_w')}
    del _L1_xattn_all

    def _L1_ffn_setup():
        import jax, jax.numpy as jnp
        import numpy as np
        BATCH, TOK, DIM, OUT = (4, 256, 512, 512)
        E, R, TOP_K = (8, 16, 2)
        SCALING = 16.0 / R
        key = jax.random.key(seed)
        ks = jax.random.split(key, 6)
        return {'x': jax.random.normal(ks[0], (BATCH, TOK, DIM), dtype=jnp.float32), 'W_base': jax.random.normal(ks[1], (OUT, DIM), dtype=jnp.float32) / np.sqrt(DIM), 'b_base': jax.random.normal(ks[2], (OUT,), dtype=jnp.float32) * 0.01, 'W_gate': jax.random.normal(ks[3], (E, DIM), dtype=jnp.float32) * 0.01, 'A': jax.random.normal(ks[4], (E, R, DIM), dtype=jnp.float32) / np.sqrt(DIM), 'B': jax.random.normal(ks[5], (OUT, OUT // OUT * R * 0 + R), dtype=jnp.float32)[None].repeat(E, 0) * 0.0 + jax.random.normal(ks[5], (E, OUT, R), dtype=jnp.float32) * 0.02}
    _L1_ffn_all = _L1_ffn_setup()
    _L1_ffn_in = {k: v for k, v in _L1_ffn_all.items() if k in ('W_base', 'b_base', 'W_gate', 'A', 'B')}
    del _L1_ffn_all

    def _L2_xattn_setup():
        import jax, jax.numpy as jnp
        import numpy as np
        HID = 512
        NHEAD = 32
        NKV = 8
        HDIM = 128
        G = NHEAD // NKV
        key = jax.random.key(seed)
        ks = jax.random.split(key, 6)
        s = 0.02
        B, L = (2, 256)
        return {'query': jax.random.normal(ks[0], (B, L, HID), jnp.float32), 'kv': jax.random.normal(ks[1], (B, L, HID), jnp.float32), 'Wq': jax.random.normal(ks[2], (HID, NHEAD * HDIM), jnp.float32) * s, 'bq': jnp.zeros((NHEAD * HDIM,), jnp.float32), 'Wkv': jax.random.normal(ks[3], (HID, 2 * NKV * HDIM), jnp.float32) * s, 'bkv': jnp.zeros((2 * NKV * HDIM,), jnp.float32), 'Wo': jax.random.normal(ks[4], (NHEAD * HDIM, HID), jnp.float32) * s, 'bo': jnp.zeros((HID,), jnp.float32)}
    _L2_xattn_all = _L2_xattn_setup()
    _L2_xattn_in = {k: v for k, v in _L2_xattn_all.items() if k in ('Wq', 'bq', 'Wkv', 'bkv', 'Wo', 'bo')}
    del _L2_xattn_all

    def _L2_ffn_setup():
        import jax, jax.numpy as jnp
        import numpy as np
        IMAGE_START_POS = 34
        Q_START = IMAGE_START_POS + 72 + 1
        Q_END = -1
        LORA_ALPHA = 32
        LORA_RANK = 16
        SCALING = LORA_ALPHA / LORA_RANK
        key = jax.random.key(seed)
        ks = jax.random.split(key, 7)
        B_, S, D, O, E, R = (4, 256, 512, 512, 8, LORA_RANK)
        s = 0.02
        return {'x': jax.random.normal(ks[0], (B_, S, D), jnp.float32), 'W': jax.random.normal(ks[1], (O, D), jnp.float32) * s, 'b': jax.random.normal(ks[2], (O,), jnp.float32) * s, 'A': jax.random.normal(ks[3], (E, R, D), jnp.float32) * s, 'B': jax.random.normal(ks[4], (E, O, R), jnp.float32) * s, 'router_W': jax.random.normal(ks[5], (E, D), jnp.float32) * s, 'router_b': jax.random.normal(ks[6], (E,), jnp.float32) * s}
    _L2_ffn_all = _L2_ffn_setup()
    _L2_ffn_in = {k: v for k, v in _L2_ffn_all.items() if k in ('W', 'b', 'A', 'B', 'router_W', 'router_b')}
    del _L2_ffn_all

    def _L3_xattn_setup():
        import jax, jax.numpy as jnp
        import numpy as np
        N, C, S = (16, 64, 512)
        rng = jax.random.key(seed)
        k1, k2, k3 = jax.random.split(rng, 3)
        return {'key': jax.random.normal(k1, (N, C, S), dtype=jnp.float32), 'value': jax.random.normal(k2, (N, C, S), dtype=jnp.float32), 'query': jax.random.normal(k3, (N, C, S), dtype=jnp.float32)}
    _L3_xattn_all = _L3_xattn_setup()
    _L3_xattn_in = {k: v for k, v in _L3_xattn_all.items() if k in ()}
    del _L3_xattn_all

    def _L3_ffn_setup():
        import jax, jax.numpy as jnp
        import numpy as np
        K_TOP = 8
        key = jax.random.key(seed)
        k1, k2, k3 = jax.random.split(key, 3)
        B, S, H, E = (4, 512, 512, 64)
        hidden_states = jax.random.normal(k1, (B, S, H), dtype=jnp.float32)
        router_weight = jax.random.normal(k2, (E, H), dtype=jnp.float32)
        router_bias = jnp.zeros((E,), dtype=jnp.float32)
        expert_bias = jax.random.normal(k3, (E, H), dtype=jnp.float32) * 0.1
        return {'hidden_states': hidden_states, 'router_weight': router_weight, 'router_bias': router_bias, 'expert_bias': expert_bias}
    _L3_ffn_all = _L3_ffn_setup()
    _L3_ffn_in = {k: v for k, v in _L3_ffn_all.items() if k in ('router_weight', 'router_bias', 'expert_bias')}
    del _L3_ffn_all
    return {'x': x, 'ctx_4096': ctx_4096, 'mask_1x1xSxS2_ff0': mask_1x1xSxS2_ff0, 'L0_xattn_Wq': _L0_xattn_in['Wq'], 'L0_xattn_bq': _L0_xattn_in['bq'], 'L0_xattn_Wk': _L0_xattn_in['Wk'], 'L0_xattn_bk': _L0_xattn_in['bk'], 'L0_xattn_Wv': _L0_xattn_in['Wv'], 'L0_xattn_bv': _L0_xattn_in['bv'], 'L0_xattn_Wo': _L0_xattn_in['Wo'], 'L0_xattn_bo': _L0_xattn_in['bo'], 'L0_ffn_weight': _L0_ffn_in['weight'], 'L0_ffn_lora_A': _L0_ffn_in['lora_A'], 'L0_ffn_lora_B': _L0_ffn_in['lora_B'], 'L0_ffn_gw1': _L0_ffn_in['gw1'], 'L0_ffn_gb1': _L0_ffn_in['gb1'], 'L0_ffn_ln_gamma': _L0_ffn_in['ln_gamma'], 'L0_ffn_ln_beta': _L0_ffn_in['ln_beta'], 'L0_ffn_gw2': _L0_ffn_in['gw2'], 'L0_ffn_gb2': _L0_ffn_in['gb2'], 'L1_xattn_Wq': _L1_xattn_in['Wq'], 'L1_xattn_Wk': _L1_xattn_in['Wk'], 'L1_xattn_Wv': _L1_xattn_in['Wv'], 'L1_xattn_Wo': _L1_xattn_in['Wo'], 'L1_xattn_q_norm_w': _L1_xattn_in['q_norm_w'], 'L1_xattn_k_norm_w': _L1_xattn_in['k_norm_w'], 'L1_ffn_W_base': _L1_ffn_in['W_base'], 'L1_ffn_b_base': _L1_ffn_in['b_base'], 'L1_ffn_W_gate': _L1_ffn_in['W_gate'], 'L1_ffn_A': _L1_ffn_in['A'], 'L1_ffn_B': _L1_ffn_in['B'], 'L2_xattn_Wq': _L2_xattn_in['Wq'], 'L2_xattn_bq': _L2_xattn_in['bq'], 'L2_xattn_Wkv': _L2_xattn_in['Wkv'], 'L2_xattn_bkv': _L2_xattn_in['bkv'], 'L2_xattn_Wo': _L2_xattn_in['Wo'], 'L2_xattn_bo': _L2_xattn_in['bo'], 'L2_ffn_W': _L2_ffn_in['W'], 'L2_ffn_b': _L2_ffn_in['b'], 'L2_ffn_A': _L2_ffn_in['A'], 'L2_ffn_B': _L2_ffn_in['B'], 'L2_ffn_router_W': _L2_ffn_in['router_W'], 'L2_ffn_router_b': _L2_ffn_in['router_b'], 'L3_ffn_router_weight': _L3_ffn_in['router_weight'], 'L3_ffn_router_bias': _L3_ffn_in['router_bias'], 'L3_ffn_expert_bias': _L3_ffn_in['expert_bias']}

def reference(x, ctx_4096, mask_1x1xSxS2_ff0, L0_xattn_Wq, L0_xattn_bq, L0_xattn_Wk, L0_xattn_bk, L0_xattn_Wv, L0_xattn_bv, L0_xattn_Wo, L0_xattn_bo, L0_ffn_weight, L0_ffn_lora_A, L0_ffn_lora_B, L0_ffn_gw1, L0_ffn_gb1, L0_ffn_ln_gamma, L0_ffn_ln_beta, L0_ffn_gw2, L0_ffn_gb2, L1_xattn_Wq, L1_xattn_Wk, L1_xattn_Wv, L1_xattn_Wo, L1_xattn_q_norm_w, L1_xattn_k_norm_w, L1_ffn_W_base, L1_ffn_b_base, L1_ffn_W_gate, L1_ffn_A, L1_ffn_B, L2_xattn_Wq, L2_xattn_bq, L2_xattn_Wkv, L2_xattn_bkv, L2_xattn_Wo, L2_xattn_bo, L2_ffn_W, L2_ffn_b, L2_ffn_A, L2_ffn_B, L2_ffn_router_W, L2_ffn_router_b, L3_ffn_router_weight, L3_ffn_router_bias, L3_ffn_expert_bias):
    import jax
    import jax.numpy as jnp

    def _L0_xattn_ref(query, key, value, Wq, bq, Wk, bk, Wv, bv, Wo, bo):
        import jax, jax.numpy as jnp
        import numpy as np
        EMBED = 512
        NUM_Q = 32
        NUM_KV = 8
        GROUPS = NUM_Q // NUM_KV
        HEAD_DIM = EMBED // NUM_Q
        KV_DIM = HEAD_DIM * NUM_KV
        B, S, _ = query.shape
        Q = query @ Wq + bq
        K = key @ Wk + bk
        V = value @ Wv + bv
        Q = Q.reshape(B, S, NUM_KV, GROUPS, HEAD_DIM).transpose(0, 2, 3, 1, 4)
        K = K.reshape(B, S, NUM_KV, HEAD_DIM).transpose(0, 2, 1, 3)
        V = V.reshape(B, S, NUM_KV, HEAD_DIM).transpose(0, 2, 1, 3)
        scale = 1.0 / jnp.sqrt(jnp.asarray(HEAD_DIM, query.dtype))
        scores = jnp.einsum('bhgqd,bhkd->bhgqk', Q, K) * scale
        w = jax.nn.softmax(scores, axis=-1)
        y = jnp.einsum('bhgqk,bhkd->bhgqd', w, V)
        y = y.transpose(0, 3, 1, 2, 4).reshape(B, S, EMBED)
        return y @ Wo + bo

    def _L0_ffn_ref(x, weight, lora_A, lora_B, gw1, gb1, ln_gamma, ln_beta, gw2, gb2):
        import jax, jax.numpy as jnp
        import numpy as np
        B, S, IN, OUT = (4, 256, 512, 512)
        E, K, R = (8, 2, 16)
        CAP_FACTOR = 3.0
        ALPHA = 1.0 / R
        LN_EPS = 1e-05
        orig_shape = x.shape
        xf = x.reshape(-1, orig_shape[-1])
        N = xf.shape[0]
        capacity = int(CAP_FACTOR * N / E)
        h = xf @ gw1.T + gb1
        mu = jnp.mean(h, axis=-1, keepdims=True)
        var = jnp.mean((h - mu) ** 2, axis=-1, keepdims=True)
        h = (h - mu) * jax.lax.rsqrt(var + LN_EPS) * ln_gamma + ln_beta
        h = jax.nn.relu(h)
        gates = h @ gw2.T + gb2
        top_v, top_i = jax.lax.top_k(gates, K)
        top_g = jax.nn.softmax(top_v, axis=-1)
        onehot = (top_i[..., None] == jnp.arange(E)).astype(xf.dtype)
        counts = onehot.sum(axis=0)
        allowed = (counts <= capacity).astype(xf.dtype)
        w = jnp.einsum('nke,nk,ke->ne', onehot, top_g, allowed)
        main = xf @ weight.T
        tmp = jnp.einsum('ni,eir->enr', xf, lora_A)
        tmp = tmp * w.T[:, :, None]
        lora = jnp.einsum('enr,ero->no', tmp, lora_B) * ALPHA
        out = main + lora
        return out.reshape(*orig_shape[:-1], weight.shape[0])

    def _L1_xattn_ref(hidden_states, cross_attention_states, attention_mask, Wq, Wk, Wv, Wo, q_norm_w, k_norm_w):
        import jax, jax.numpy as jnp
        import numpy as np
        B, Q, K, D = (1, 128, 6404, 512)
        H, KVH, HD = (32, 8, 128)
        GROUPS = H // KVH
        EPS = 1e-05

        def _rmsnorm(x, w):
            xf = x.astype(jnp.float32)
            var = jnp.mean(xf * xf, axis=-1, keepdims=True)
            return (xf * jax.lax.rsqrt(var + EPS)).astype(x.dtype) * w
        bsz, q_len, _ = hidden_states.shape
        kv_len = cross_attention_states.shape[1]
        q = (hidden_states @ Wq.T).reshape(bsz, q_len, H, HD).transpose(0, 2, 1, 3)
        k = (cross_attention_states @ Wk.T).reshape(bsz, kv_len, KVH, HD).transpose(0, 2, 1, 3)
        v = (cross_attention_states @ Wv.T).reshape(bsz, kv_len, KVH, HD).transpose(0, 2, 1, 3)
        q = _rmsnorm(q, q_norm_w)
        k = jnp.repeat(k, GROUPS, axis=1)
        v = jnp.repeat(v, GROUPS, axis=1)
        k = _rmsnorm(k, k_norm_w)
        scale = 1.0 / np.sqrt(HD)
        scores = jnp.einsum('bhqd,bhkd->bhqk', q, k) * scale
        scores = scores + attention_mask[:, :, :, :kv_len]
        probs = jax.nn.softmax(scores.astype(jnp.float32), axis=-1).astype(q.dtype)
        out = jnp.einsum('bhqk,bhkd->bhqd', probs, v)
        out = out.transpose(0, 2, 1, 3).reshape(bsz, q_len, H * HD)
        return out @ Wo.T

    def _L1_ffn_ref(x, W_base, b_base, W_gate, A, B):
        import jax, jax.numpy as jnp
        import numpy as np
        BATCH, TOK, DIM, OUT = (4, 256, 512, 512)
        E, R, TOP_K = (8, 16, 2)
        SCALING = 16.0 / R
        result = jnp.einsum('bnd,od->bno', x, W_base) + b_base
        logits = jnp.einsum('bnd,ed->bne', x, W_gate)
        probs = jax.nn.softmax(logits.astype(jnp.float32), axis=-1)
        top_p, top_i = jax.lax.top_k(probs, TOP_K)
        top_p = top_p / jnp.sum(top_p, axis=-1, keepdims=True)
        top_p = top_p.astype(x.dtype)
        route_w = jnp.sum(jax.nn.one_hot(top_i, E, dtype=x.dtype) * top_p[..., None], axis=-2)
        h = jnp.einsum('bnd,erd->bner', x, A)
        hw = h * route_w[..., None]
        delta = jnp.einsum('bner,eor->bno', hw, B)
        return result + delta * SCALING

    def _L2_xattn_ref(query, kv, Wq, bq, Wkv, bkv, Wo, bo):
        import jax, jax.numpy as jnp
        import numpy as np
        HID = 512
        NHEAD = 32
        NKV = 8
        HDIM = 128
        G = NHEAD // NKV
        B, L, _ = query.shape
        Lk = kv.shape[1]
        scale = jnp.asarray(1.0 / np.sqrt(HDIM), query.dtype)
        q = (query @ Wq + bq).reshape(B, L, NKV, G, HDIM)
        k_, v_ = jnp.split(kv @ Wkv + bkv, 2, axis=-1)
        k = k_.reshape(B, Lk, NKV, HDIM)
        v = v_.reshape(B, Lk, NKV, HDIM)
        scores = jnp.einsum('blkgd,bmkd->bkglm', q, k) * scale
        attn = jax.nn.softmax(scores, axis=-1)
        o = jnp.einsum('bkglm,bmkd->blkgd', attn, v).reshape(B, L, NHEAD * HDIM)
        return o @ Wo + bo

    def _L2_ffn_ref(x, W, b, A, B, router_W, router_b):
        import jax, jax.numpy as jnp
        import numpy as np
        IMAGE_START_POS = 34
        Q_START = IMAGE_START_POS + 72 + 1
        Q_END = -1
        LORA_ALPHA = 32
        LORA_RANK = 16
        SCALING = LORA_ALPHA / LORA_RANK
        x_q = x[:, Q_START:Q_END, :]
        q = x_q.mean(axis=1)
        logits = q @ router_W.T + router_b
        routing = jax.nn.softmax(logits, axis=-1)
        base = x @ W.T + b
        t = jnp.einsum('bsd,erd->bser', x, A)
        lora = jnp.einsum('bser,eor,be->bso', t, B, routing) * SCALING
        return base + lora

    def _L3_xattn_ref(key, value, query):
        import jax, jax.numpy as jnp
        import numpy as np
        N, C, S = (16, 64, 512)
        KC = key.shape[1]
        sim = jnp.einsum('ncs,nds->ncd', key, query) * KC ** (-0.5)
        sim = jax.nn.softmax(sim, axis=1)
        context = jnp.einsum('ncd,nds->ncs', sim, value)
        return context

    def _L3_ffn_ref(hidden_states, router_weight, router_bias, expert_bias):
        import jax, jax.numpy as jnp
        import numpy as np
        K_TOP = 8
        B, S, H = hidden_states.shape
        E = router_weight.shape[0]
        T = B * S
        flat = hidden_states.reshape(T, H)
        logits = jnp.einsum('th,eh->te', flat, router_weight) + router_bias
        scores = jax.nn.softmax(logits, axis=-1)
        topk_w, topk_idx = jax.lax.top_k(scores, K_TOP)
        w_sum = topk_w.sum(axis=-1, keepdims=True)
        w_dense = jnp.zeros((T, E), dtype=scores.dtype).at[jnp.arange(T)[:, None], topk_idx].add(topk_w)
        bias_mix = jnp.einsum('te,eh->th', w_dense, expert_bias)
        out = flat * w_sum + bias_mix
        return out.reshape(B, S, H)
    x = x + _L0_xattn_ref(_layernorm(x, axis=-1), ctx_4096, ctx_4096, L0_xattn_Wq, L0_xattn_bq, L0_xattn_Wk, L0_xattn_bk, L0_xattn_Wv, L0_xattn_bv, L0_xattn_Wo, L0_xattn_bo)
    x = x + _L0_ffn_ref(_layernorm(x, axis=-1), L0_ffn_weight, L0_ffn_lora_A, L0_ffn_lora_B, L0_ffn_gw1, L0_ffn_gb1, L0_ffn_ln_gamma, L0_ffn_ln_beta, L0_ffn_gw2, L0_ffn_gb2)
    x = x + _L1_xattn_ref(_layernorm(x, axis=-1), ctx_4096, mask_1x1xSxS2_ff0, L1_xattn_Wq, L1_xattn_Wk, L1_xattn_Wv, L1_xattn_Wo, L1_xattn_q_norm_w, L1_xattn_k_norm_w)
    x = x + _L1_ffn_ref(_layernorm(x, axis=-1), L1_ffn_W_base, L1_ffn_b_base, L1_ffn_W_gate, L1_ffn_A, L1_ffn_B)
    x = x + _L2_xattn_ref(_layernorm(x, axis=-1), ctx_4096, L2_xattn_Wq, L2_xattn_bq, L2_xattn_Wkv, L2_xattn_bkv, L2_xattn_Wo, L2_xattn_bo)
    x = x + _L2_ffn_ref(_layernorm(x, axis=-1), L2_ffn_W, L2_ffn_b, L2_ffn_A, L2_ffn_B, L2_ffn_router_W, L2_ffn_router_b)
    x = x + _L3_xattn_ref(ctx_4096, ctx_4096, _layernorm(x, axis=-1))
    x = x + _L3_ffn_ref(_layernorm(x, axis=-1), L3_ffn_router_weight, L3_ffn_router_bias, L3_ffn_expert_bias)
    return x

_drawn_inputs = setup_inputs


def setup_inputs(seed=0):
    import zlib

    import numpy as np

    out = dict(_drawn_inputs(seed))
    spreads = {'L0_xattn_bq': (0.0, 0.8),
     'L0_xattn_bk': (0.0, 0.8),
     'L0_xattn_bv': (0.0, 0.1),
     'L0_xattn_bo': (0.0, 0.1),
     'L0_ffn_gb1': (0.0, 0.8),
     'L0_ffn_ln_gamma': (1.0, 0.6),
     'L0_ffn_ln_beta': (0.0, 0.8),
     'L0_ffn_gb2': (0.0, 0.635),
     'L1_xattn_q_norm_w': (1.0, 0.6),
     'L1_xattn_k_norm_w': (1.0, 0.6),
     'L2_xattn_bq': (0.0, 0.8),
     'L2_xattn_bkv': (0.0, 0.1),
     'L2_xattn_bo': (0.0, 0.1),
     'L3_ffn_router_bias': (0.0, 0.8)}
    factors = {'L0_xattn_Wq': 8.0,
     'L0_xattn_Wk': 7.849,
     'L0_ffn_lora_A': 6.234,
     'L0_ffn_lora_B': 6.332,
     'L0_ffn_gw1': 7.4,
     'L0_ffn_gw2': 7.1,
     'L1_ffn_b_base': 8.0,
     'L2_xattn_Wq': 5.853,
     'L2_ffn_b': 6.312,
     'L2_ffn_A': 5.095,
     'L2_ffn_B': 5.139,
     'L2_ffn_router_W': 8.0,
     'L2_ffn_router_b': 8.0}
    for name, (base, spread) in spreads.items():
        noise = np.random.default_rng([zlib.crc32(name.encode()), seed]).standard_normal(out[name].shape)
        drawn = base * np.exp(spread * noise) if base else spread * noise
        out[name] = jnp.asarray(drawn.astype(out[name].dtype))
    for name, factor in factors.items():
        out[name] = (out[name] * factor).astype(out[name].dtype)
    return out
```

```python
import concourse.bass as bass
from concourse import mybir
from contextlib import ExitStack

F32 = mybir.dt.float32
F32R = mybir.dt.float32r
ALU = mybir.AluOpType
ACT = mybir.ActivationFunctionType
AX = mybir.AxisListType

B = 8
S = 128
D = 512
KT = D // 128
BANK = 512
LN_EPS = 1e-5
NEVER = -3.0e38


def blk(i, width):
    return bass.ds(i * width, width)


def wait_from_one(eng, sem, value):
    if not (isinstance(value, int) and value <= 0):
        eng.wait_ge(sem, value)


def in_pairs(eng, front, back):
    front(0, 0)
    front(1, 1)
    back(0, 0)
    with eng.Fori(0, B // 2 - 1) as pair:
        i = pair * 2 + 1
        for n in (0, 1):
            front(i + n + 1, n)
            back(i + n, 1 - n)
    back(B - 1, 1)


def one_by_one(eng, step):
    step(0)
    with eng.Fori(1, B) as i:
        step(i)


def matmul_split(pe, out, lhs, rhs, start, stop):
    (lhs_hi, lhs_lo), (rhs_hi, rhs_lo) = lhs, rhs
    pe.matmul(out, lhs_lo, rhs_hi, start=start, stop=False)
    pe.matmul(out, lhs_hi, rhs_lo, start=False, stop=False)
    return pe.matmul(out, lhs_hi, rhs_hi, start=False, stop=stop)


def matmul_tiles(pe, out, lhs_tiles, rhs_tiles):
    n = len(lhs_tiles)
    for k in range(n):
        last = matmul_split(pe, out, lhs_tiles[k], rhs_tiles[k], k == 0, k == n - 1)
    return last


def minus(eng, out_lo, value, hi):
    return eng.tensor_tensor(out_lo, value, hi.bitcast(F32), ALU.subtract)


class Phase:

    def __init__(self, nc, ctx, tag):
        self.nc, self.ctx, self.tag, self.used = nc, ctx, tag, []
        ctx.callback(self.clear)

    def clear(self):
        self.nc.clear_and_free_semaphores(self.used)
        self.nc.all_engine_barrier()

    def sb(self, name, cols, dt=F32, rows=128):
        return self.ctx.enter_context(self.nc.sbuf_tensor(f"{self.tag}_{name}", [rows, cols], dt))

    def split(self, name, cols, rows=128):
        return (self.sb(name + "_hi", cols, F32R, rows), self.sb(name + "_lo", cols, F32R, rows))

    def sem(self, name):
        self.used.append(self.nc.alloc_semaphore(name=f"{self.tag}_{name}"))
        return self.used[-1]

    def sems(self, names):
        return {n: self.sem(n) for n in names.split()}



NORM_SEMS = "stats moments veps rstd xn xnT xT_hi xT_lo"


class NormBuffers:
    def __init__(self, ph):
        self.stats, self.moments = ph.sb("stats", 6), ph.sb("moments", 2)
        self.veps, self.rstd = ph.sb("veps", 1), ph.sb("rstd", 1)
        self.xn = ph.sb("xn", D)


def norm_vector(dve, s, t, x_i, xn, i):
    dve.bn_stats(t.stats[:, :], x_i).then_inc(s["stats"], 1)
    dve.drain()
    dve.bn_aggr(t.moments[:, :], t.stats[:, :]).then_inc(s["moments"], 1)
    dve.wait_ge(s["rstd"], i + 1)
    wait_from_one(dve, s["xnT"], i)
    dve.tensor_scalar(xn, x_i, t.moments[:, 0:1], t.rstd[:, 0:1], ALU.subtract, ALU.mult).then_inc(s["xn"], 1)


def norm_gpsimd(pool, C, s, t, i):
    pool.wait_ge(s["moments"], i + 1)
    wait_from_one(pool, s["xn"], i)
    pool.tensor_tensor(t.veps[:, :], t.moments[:, 1:2], C.ln_eps[:, 0:1], ALU.add).then_inc(s["veps"], 1)
    pool.wait_ge(s["veps"], i + 1)
    pool.tensor_tensor(t.rstd[:, :], t.veps[:, :], C.neg_half[:, 0:1], ALU.pow).then_inc(s["rstd"], 1)


def norm_tensor(pe, C, s, xn, bank, i):
    pe.wait_ge(s["xn"], i + 1)
    wait_from_one(pe, s["xT_lo"], i)
    for k in range(KT):
        last = pe.transpose(bank[:, k * 128:(k + 1) * 128], xn[:, k * 128:(k + 1) * 128], C.ident[:, :])
    last.then_inc(s["xnT"], 1)


def tiles_of(bank):
    return bank.rearrange("p (k t) -> p k t", k=KT)



def set_up(nc, C, x_dram):
    with ExitStack() as ctx:
        ph = Phase(nc, ctx, "setup")
        s = ph.sems("zeroed const loaded")
        block = ctx.enter_context(nc.Block())

        @block.sync
        def _(sp):
            with sp.Fori(0, B) as b:
                sp.dma_start(C.x[:, blk(b, D)], x_dram[bass.ds(b, 1)].rearrange("a p d -> p (a d)")).then_inc(s["loaded"], 16)
            sp.wait_ge(s["loaded"], 16 * B)

        @block.gpsimd
        def _(pool):
            pool.memset(C.ident[:, :], 0.0).then_inc(s["zeroed"], 1)
            pool.memset(C.neg_half[:, :], -0.5).then_inc(s["zeroed"], 1)
            pool.memset(C.ones[:, :], 1.0).then_inc(s["zeroed"], 1)
            pool.memset(C.ln_eps[:, :], LN_EPS).then_inc(s["zeroed"], 1)
            for e in range(8):
                pool.memset(C.falling[:, e:e + 1], float(8 - e)).then_inc(s["zeroed"], 1)
            pool.wait_ge(s["zeroed"], 12)
            pool.affine_select(out=C.ident[:, :], in_=C.ident[:, :], compare_op=ALU.not_equal, fill=1.0,
                               base=0, pattern=[[-1, 128]], channel_multiplier=1).then_inc(s["const"], 1)
            pool.wait_ge(s["const"], 1)



E = 8
R = 16
ER = E * R
GATE_HID = 32
CAPACITY = int(3.0 * B * S / E)
MEAN_FROM, MEAN_TO = 107, S - 1


def by_sequence(tile):
    return tile.rearrange("p (b c) -> p b c", b=B)


def along_last(v, n):
    return v.unsqueeze(2).to_broadcast([128, v.shape[1], n])


def along_sequences(v):
    return v.unsqueeze(1).to_broadcast([128, B, v.shape[1]])


def best_expert(link, dve, C, gates, onehot, best, rank):
    g3, o3 = by_sequence(gates), by_sequence(onehot)
    link(dve.tensor_reduce(best, g3, AX.X, ALU.max))
    link(dve.tensor_tensor(o3, g3, along_last(best, E), ALU.is_equal))
    link(dve.tensor_tensor(o3, o3, along_sequences(C.falling[:, :]), ALU.mult))
    link(dve.tensor_reduce(rank, o3, AX.X, ALU.max))
    link(dve.tensor_tensor(o3, o3, along_last(rank, E), ALU.is_equal))


class TopTwo:
    G = E
    N_ROWS = 0

    def __init__(self, ph, C, extra):
        self.C, self.extra = C, extra
        self.gates, self.first, self.second, self.rest = (
            ph.sb(n, B * E) for n in ("gates", "first", "second", "rest"))
        self.best, self.next, self.rank, self.share = (ph.sb(n, B) for n in ("best", "next", "rank", "share"))
        self.ratio = C.to_exp[:, 0:B]
        self.ahead, self.exped = ph.sem("ahead"), ph.sem("exped")
        self.route = self.first

    def load(self, sp, sem):
        pass

    def gpsimd(self, pool):
        pass

    def tensor(self, pe, bank):
        pass

    def scalar(self, act):
        act.wait_ge(self.ahead, 1)
        act.activation(self.ratio, self.ratio, ACT.Exp).then_inc(self.exped, 1)

    def pick(self, dve, link):
        best_expert(link, dve, self.C, self.gates[:, :], self.first[:, :], self.best[:, :], self.rank[:, :])
        link(dve.scalar_tensor_tensor(self.rest[:, :], self.first[:, :], NEVER, self.gates[:, :], ALU.mult, ALU.add))
        best_expert(link, dve, self.C, self.rest[:, :], self.second[:, :], self.next[:, :], self.rank[:, :])
        dve.tensor_tensor(self.ratio, self.next[:, :], self.best[:, :], ALU.subtract).then_inc(self.ahead, 1)
        dve.wait_ge(self.exped, 1)
        link(dve.tensor_scalar(self.share[:, :], self.ratio, 1.0, None, ALU.add))
        link(dve.reciprocal(self.share[:, :], self.share[:, :]))
        link(dve.tensor_tensor(self.ratio, self.ratio, self.share[:, :], ALU.mult))

    def weigh(self, dve, link):
        for onehot, w in ((self.first, self.share[:, :]), (self.second, self.ratio)):
            o3 = by_sequence(onehot[:, :])
            link(dve.tensor_tensor(o3, o3, along_last(w, E), ALU.mult))
        link(dve.tensor_tensor(self.first[:, :], self.first[:, :], self.second[:, :], ALU.add))

    def vector(self, dve, link, gate_out, bank, rows_loaded):
        link(dve.tensor_copy(by_sequence(self.gates[:, :]), gate_out))
        self.pick(dve, link)
        self.weigh(dve, link)


class GateNet(TopTwo):
    G = GATE_HID
    N_ROWS = 5

    def __init__(self, ph, C, extra):
        super().__init__(ph, C, extra)
        n = GATE_HID
        self.rows = [ph.sb(f"row{k}", w) for k, w in enumerate((n, n, n, E * n, E))]
        self.hid, self.dev = ph.sb("hid", B * n), ph.sb("dev", B * n)
        self.stat, self.inv = ph.sb("stat", B), ph.sb("inv", B)
        self.products = ph.sb("products", B * E * n)
        self.counts, self.allowed = ph.sb("counts", 2 * E), ph.sb("allowed", 2 * E)
        self.var, self.inverted, self.counted, self.summed = (
            ph.sem(n) for n in ("var", "inverted", "counted", "summed"))

    def load(self, sp, sem):
        for dst, src in zip(self.rows, self.extra):
            sp.dma_start(dst[:, :], src.partition_broadcast(128)).then_inc(sem, 16)

    def gpsimd(self, pool):
        pool.wait_ge(self.var, 1)
        pool.tensor_tensor(self.inv[:, :], self.stat[:, :], self.C.neg_half[:, 0:B], ALU.pow).then_inc(self.inverted, 1)

    def tensor(self, pe, bank):
        pe.wait_ge(self.counted, 1)
        pe.matmul(bank[:, 0:2 * E], self.C.ones[:, :], self.counts[:, :], start=True, stop=True).then_inc(self.summed, 1)

    def vector(self, dve, link, gate_out, bank, rows_loaded):
        b1, gamma, beta, w2, b2 = (r[:, :] for r in self.rows)
        hid, dev = by_sequence(self.hid[:, :]), by_sequence(self.dev[:, :])
        stat, n = self.stat[:, :], GATE_HID
        dve.wait_ge(rows_loaded, 16 * self.N_ROWS)
        link(dve.tensor_tensor(hid, gate_out, along_sequences(b1), ALU.add))
        link(dve.tensor_reduce(stat, hid, AX.X, ALU.add))
        link(dve.tensor_scalar(stat, stat, 1.0 / n, None, ALU.mult))
        link(dve.tensor_tensor(hid, hid, along_last(stat, n), ALU.subtract))
        link(dve.tensor_tensor(dev, hid, hid, ALU.mult))
        link(dve.tensor_reduce(stat, dev, AX.X, ALU.add))
        dve.tensor_scalar(stat, stat, 1.0 / n, LN_EPS, ALU.mult, ALU.add).then_inc(self.var, 1)
        dve.wait_ge(self.inverted, 1)
        link(dve.tensor_tensor(hid, hid, along_last(self.inv[:, :], n), ALU.mult))
        link(dve.tensor_tensor(hid, hid, along_sequences(gamma), ALU.mult))
        link(dve.tensor_tensor(hid, hid, along_sequences(beta), ALU.add))
        link(dve.tensor_scalar(self.hid[:, :], self.hid[:, :], 0.0, None, ALU.max))
        for b in range(B):
            p3 = self.products[:, b * E * n:(b + 1) * E * n].rearrange("p (e c) -> p e c", e=E)
            h3 = self.hid[:, b * n:(b + 1) * n].unsqueeze(1).to_broadcast([128, E, n])
            link(dve.tensor_tensor(p3, h3, w2.rearrange("p (e c) -> p e c", e=E), ALU.mult))
        link(dve.tensor_reduce(self.gates[:, :], self.products[:, :].rearrange("p (g c) -> p g c", c=n), AX.X, ALU.add))
        g3 = by_sequence(self.gates[:, :])
        link(dve.tensor_tensor(g3, g3, along_sequences(b2), ALU.add))
        self.pick(dve, link)
        link(dve.tensor_reduce(self.counts[:, 0:E], self.first[:, :].rearrange("p (b e) -> p e b", b=B), AX.X, ALU.add))
        dve.tensor_reduce(self.counts[:, E:2 * E], self.second[:, :].rearrange("p (b e) -> p e b", b=B), AX.X,
                          ALU.add).then_inc(self.counted, 1)
        dve.wait_ge(self.summed, 1)
        link(dve.tensor_scalar(self.allowed[:, :], bank[:, 0:2 * E], float(CAPACITY), None, ALU.is_le))
        for k, onehot in enumerate((self.first, self.second)):
            o3 = by_sequence(onehot[:, :])
            link(dve.tensor_tensor(o3, o3, along_sequences(self.allowed[:, k * E:(k + 1) * E]), ALU.mult))
        self.weigh(dve, link)


class MeanRoute:
    G = E
    N_ROWS = 1

    def __init__(self, ph, C, extra):
        self.C, self.extra = C, extra
        self.row, self.average = ph.sb("row", E), ph.sb("average", S)
        self.gates, self.route, self.most = ph.sb("gates", B * E), C.to_exp, ph.sb("most", B)
        self.masked, self.copied, self.averaged, self.below, self.exped = (
            ph.sem(n) for n in ("masked", "copied", "averaged", "below", "exped"))

    def load(self, sp, sem):
        sp.dma_start(self.row[:, :], self.extra[0].partition_broadcast(128)).then_inc(sem, 16)

    def gpsimd(self, pool):
        a = self.average[:, :]
        pool.memset(a, 1.0 / (MEAN_TO - MEAN_FROM)).then_inc(self.masked, 1)
        pool.wait_ge(self.masked, 1)
        pool.affine_select(out=a, in_=a, compare_op=ALU.is_ge, fill=0.0, base=-MEAN_FROM, pattern=[[0, S]],
                           channel_multiplier=1).then_inc(self.masked, 1)
        pool.wait_ge(self.masked, 2)
        pool.affine_select(out=a, in_=a, compare_op=ALU.is_ge, fill=0.0, base=MEAN_TO - 1, pattern=[[0, S]],
                           channel_multiplier=-1).then_inc(self.masked, 1)

    def tensor(self, pe, bank):
        pe.wait_ge(self.copied, 1)
        pe.wait_ge(self.masked, 3)
        pe.matmul(bank[:, 0:B * E], self.average[:, :], self.gates[:, :], start=True, stop=True).then_inc(self.averaged, 1)

    def scalar(self, act):
        act.wait_ge(self.below, 1)
        act.activation(self.route[:, :], self.route[:, :], ACT.Exp).then_inc(self.exped, 1)

    def vector(self, dve, link, gate_out, bank, rows_loaded):
        r3, most = by_sequence(self.route[:, :]), self.most[:, :]
        dve.tensor_copy(by_sequence(self.gates[:, :]), gate_out).then_inc(self.copied, 1)
        dve.wait_ge(rows_loaded, 16)
        dve.wait_ge(self.averaged, 1)
        link(dve.tensor_tensor(r3, by_sequence(bank[:, 0:B * E]), along_sequences(self.row[:, :]), ALU.add))
        link(dve.tensor_reduce(most, r3, AX.X, ALU.max))
        dve.tensor_tensor(r3, r3, along_last(most, E), ALU.subtract).then_inc(self.below, 1)
        dve.wait_ge(self.exped, 1)
        link(dve.tensor_reduce(most, r3, AX.X, ALU.add))
        link(dve.reciprocal(most, most))
        link(dve.tensor_tensor(r3, r3, along_last(most, E), ALU.mult))


def ffn_phase(nc, C, tag, Route, w_main, w_side, w_up, scale, bias=None, extra=None):
    SIDE = ER + Route.G
    with ExitStack() as ctx:
        ph = Phase(nc, ctx, tag)
        t = NormBuffers(ph)
        xT = [ph.split(f"xT{p}", D) for p in (0, 1)]
        raw = [ph.sb(n, c) for n, c in (("main_raw", KT * D), ("side_raw", KT * SIDE), ("up_raw", D))]
        main, side, up = (ph.split(n, c) for n, c in (("main", KT * D), ("side", KT * SIDE), ("up", D)))
        kept = ph.sb("kept", B * SIDE)
        bias_row = ph.sb("bias", D) if bias is not None else None
        routed = ph.sb("routed", ER)
        rT = [ph.split(f"rT{p}", S) for p in (0, 1)]
        s = ph.sems(NORM_SEMS + " loaded rows bias_loaded w_hi w_lo biased main_mm side_mm added kept"
                    " chain routed routedT rT_hi rT_lo up_mm summed_up")
        route = Route(ph, C, extra)
        bank_xT, bank_main, bank_side, bank_rT, bank_up, bank_route = (C.ps[:, blk(k, BANK)] for k in range(6))
        block = ctx.enter_context(nc.Block())

        def x_of(i):
            return C.x[:, blk(i, D)]

        def tiles(pair, n):
            return [tuple(h[:, k * n:(k + 1) * n] for h in pair) for k in range(KT)]

        @block.sync
        def _(sp):
            for dst, src in zip(raw, (w_main, w_side, w_up)):
                sp.dma_start(dst[:, :], src).then_inc(s["loaded"], 16)
            if bias is not None:
                sp.dma_start(bias_row[:, :], bias.partition_broadcast(128)).then_inc(s["bias_loaded"], 16)
            route.load(sp, s["rows"])

        @block.gpsimd
        def _(pool):
            def front(i, p):
                norm_gpsimd(pool, C, s, t, i)

            def back(i, p):
                if bias is not None:
                    pool.wait_ge(s["xn"], i + 1)
                    pool.tensor_tensor(x_of(i), x_of(i), bias_row[:, :], ALU.add).then_inc(s["biased"], 1)
            if bias is not None:
                pool.wait_ge(s["bias_loaded"], 16)
            in_pairs(pool, front, back)
            route.gpsimd(pool)

        @block.tensor
        def _(pe):
            def front(i, p):
                norm_tensor(pe, C, s, t.xn[:, :], bank_xT, i)

            def back(i, p):
                lhs = tiles(xT[p], S)
                pe.wait_ge(s["xT_lo"], i + 1)
                wait_from_one(pe, s["added"], i)
                matmul_tiles(pe, bank_main, lhs, tiles(main, D)).then_inc(s["main_mm"], 1)
                wait_from_one(pe, s["kept"], i)
                matmul_tiles(pe, bank_side[:, 0:SIDE], lhs, tiles(side, SIDE)).then_inc(s["side_mm"], 1)
            pe.wait_ge(s["w_lo"], 3)
            in_pairs(pe, front, back)
            route.tensor(pe, bank_route)

            def front2(i, p):
                pe.wait_ge(s["routed"], i + 1)
                wait_from_one(pe, s["rT_lo"], i)
                pe.transpose(bank_rT[:, 0:S], routed[:, :], C.ident[:, :]).then_inc(s["routedT"], 1)

            def back2(i, p):
                pe.wait_ge(s["rT_lo"], i + 1)
                wait_from_one(pe, s["summed_up"], i)
                matmul_tiles(pe, bank_up, [(rT[p][0][:, :], rT[p][1][:, :])],
                             [(up[0][:, :], up[1][:, :])]).then_inc(s["up_mm"], 1)
            in_pairs(pe, front2, back2)

        @block.scalar
        def _(act):
            act.wait_ge(s["loaded"], 48)
            for r, pair in zip(raw, (main, side, up)):
                act.activation(pair[0][:, :], r[:, :], ACT.Copy).then_inc(s["w_hi"], 1)

            def front(i, p):
                act.wait_ge(s["xnT"], i + 1)
                wait_from_one(act, s["side_mm"], i - 1)
                act.activation(xT[p][0][:, :], bank_xT, ACT.Copy).then_inc(s["xT_hi"], 1)
            in_pairs(act, front, lambda i, p: None)
            route.scalar(act)

            def front2(i, p):
                act.wait_ge(s["routedT"], i + 1)
                wait_from_one(act, s["up_mm"], i - 1)
                act.activation(rT[p][0][:, :], bank_rT[:, 0:S], ACT.Copy).then_inc(s["rT_hi"], 1)
            in_pairs(act, front2, lambda i, p: None)

        @block.vector
        def _(dve):
            n_link = [0]

            def link(ins):
                n_link[0] += 1
                ins.then_inc(s["chain"], 1)
                dve.wait_ge(s["chain"], n_link[0])

            for n, (r, pair) in enumerate(zip(raw, (main, side, up))):
                dve.wait_ge(s["w_hi"], n + 1)
                minus(dve, pair[1][:, :], r[:, :], pair[0][:, :]).then_inc(s["w_lo"], 1)

            def front(i, p):
                norm_vector(dve, s, t, x_of(i), t.xn[:, :], i)
                dve.wait_ge(s["xT_hi"], i + 1)
                minus(dve, xT[p][1][:, :], bank_xT, xT[p][0][:, :]).then_inc(s["xT_lo"], 1)

            def back(i, p):
                dve.wait_ge(s["main_mm"], i + 1)
                if bias is not None:
                    dve.wait_ge(s["biased"], i + 1)
                dve.tensor_tensor(x_of(i), x_of(i), bank_main, ALU.add).then_inc(s["added"], 1)
                dve.wait_ge(s["side_mm"], i + 1)
                dve.tensor_copy(kept[:, blk(i, SIDE)], bank_side[:, 0:SIDE]).then_inc(s["kept"], 1)
            in_pairs(dve, front, back)
            dve.wait_ge(s["kept"], B)
            dve.wait_ge(s["added"], B)
            route.vector(dve, link, by_sequence(kept[:, :])[:, :, ER:SIDE], bank_route, s["rows"])

            def front2(i, p):
                wait_from_one(dve, s["routedT"], i)
                dve.tensor_tensor(routed[:, :].rearrange("p (e r) -> p e r", e=E),
                                  kept[:, bass.ds(i * SIDE, ER)].rearrange("p (e r) -> p e r", e=E),
                                  along_last(route.route[:, blk(i, E)], R), ALU.mult).then_inc(s["routed"], 1)
                dve.wait_ge(s["rT_hi"], i + 1)
                minus(dve, rT[p][1][:, :], bank_rT[:, 0:S], rT[p][0][:, :]).then_inc(s["rT_lo"], 1)

            def back2(i, p):
                dve.wait_ge(s["up_mm"], i + 1)
                dve.scalar_tensor_tensor(x_of(i), bank_up, scale, x_of(i), ALU.mult, ALU.add).then_inc(s["summed_up"], 1)
            in_pairs(dve, front2, back2)



HQ = 4
HD = 128
GROUPS = 8
UNIT = 4
CHUNK = KT * HD
QK_EPS = 1e-5


def context_transposed(nc, C, cT_dram):
    with ExitStack() as ctx:
        ph = Phase(nc, ctx, "cT")
        raw = ph.sb("raw", KT * B * S)
        s = ph.sems("loaded hi lo")
        block = ctx.enter_context(nc.Block())

        @block.sync
        def _(sp):
            for k in range(KT):
                sp.dma_start(raw[:, blk(k, B * S)], cT_dram[:, blk(k, B * S)]).then_inc(s["loaded"], 16)
                sp.wait_ge(s["loaded"], 16 * (k + 1))

        @block.scalar
        def _(act):
            for k in range(KT):
                act.wait_ge(s["loaded"], 16 * (k + 1))
                act.activation(C.cT[0][:, blk(k, B * S)], raw[:, blk(k, B * S)], ACT.Copy).then_inc(s["hi"], 1)

        @block.vector
        def _(dve):
            for k in range(KT):
                dve.wait_ge(s["hi"], k + 1)
                minus(dve, C.cT[1][:, blk(k, B * S)], raw[:, blk(k, B * S)], C.cT[0][:, blk(k, B * S)]).then_inc(s["lo"], 1)


def norm_all(nc, C, tag, xT, bias=None):
    with ExitStack() as ctx:
        ph = Phase(nc, ctx, tag)
        t = NormBuffers(ph)
        s = ph.sems(NORM_SEMS + " bias_loaded biased")
        bias_row = ph.sb("bias", D) if bias is not None else None
        bank = C.ps[:, 0:BANK]
        block = ctx.enter_context(nc.Block())

        def xT_of(half, i):
            return half[:, :].rearrange("p (k t) -> p k t", k=KT)[:, :, blk(i, S)]

        @block.sync
        def _(sp):
            if bias is not None:
                sp.dma_start(bias_row[:, :], bias.partition_broadcast(128)).then_inc(s["bias_loaded"], 16)

        @block.gpsimd
        def _(pool):
            def step(i):
                norm_gpsimd(pool, C, s, t, i)
                if bias is not None:
                    pool.wait_ge(s["xn"], i + 1)
                    pool.tensor_tensor(C.x[:, blk(i, D)], C.x[:, blk(i, D)], bias_row[:, :], ALU.add).then_inc(s["biased"], 1)
            if bias is not None:
                pool.wait_ge(s["bias_loaded"], 16)
            one_by_one(pool, step)

        @block.tensor
        def _(pe):
            one_by_one(pe, lambda i: norm_tensor(pe, C, s, t.xn[:, :], bank, i))

        @block.scalar
        def _(act):
            def step(i):
                act.wait_ge(s["xnT"], i + 1)
                act.activation(xT_of(xT[0], i), tiles_of(bank), ACT.Copy).then_inc(s["xT_hi"], 1)
            one_by_one(act, step)

        @block.vector
        def _(dve):
            def step(i):
                norm_vector(dve, s, t, C.x[:, blk(i, D)], t.xn[:, :], i)
                dve.wait_ge(s["xT_hi"], i + 1)
                minus(dve, xT_of(xT[1], i), tiles_of(bank), xT_of(xT[0], i)).then_inc(s["xT_lo"], 1)
            one_by_one(dve, step)


def attention_phase(nc, C, tag, wkv, wq, wo, q_norm=None, k_norm=None, mask=None, bq=None, bk=None, bv=None, bo=None):
    normed = q_norm is not None
    with ExitStack() as ctx:
        ph = Phase(nc, ctx, tag)
        xT = ph.split("xT", KT * B * S)
        norm_all(nc, C, tag + "n", xT, bo)
        raw = [ph.sb(f"raw{k}", CHUNK) for k in (0, 1)]
        wk_s, wq_s = ph.split("wk", CHUNK), ph.split("wq", HQ * CHUNK)
        wv_s, wo_s = ph.split("wv", 2 * CHUNK), ph.split("wo", 2 * HQ * D)
        kT, qT = [ph.split(f"kT{p}", UNIT * S) for p in (0, 1)], [ph.split(f"qT{p}", HQ * UNIT * S) for p in (0, 1)]
        v_s = [ph.split(f"v{p}", HD) for p in (0, 1)]
        probs, pT, oT = ph.sb("probs", HQ * S), ph.split("pT", HQ * S), ph.split("oT", HQ * S)
        neg_max, total = ph.sb("neg_max", HQ), ph.sb("total", HQ)
        s = ph.sems("raw_in0 raw_in1 chunk_hi wo_hi split0 split1 columns k_mm k_hi k_lo kn q_mm q32 q_hi q_lo v_mm v_hi v_lo"
                    " s_mm raw_max neg_max exped inverse probs pT_mm pT_hi pT_lo av_mm o32 oT_hi oT_lo o_mm added")
        kn = ph.sb("kn", UNIT * S)
        if normed:
            squares, k_squares = ph.sb("squares", UNIT * S), ph.sb("k_squares", UNIT * S)
            k_scale, k_diagonal = ph.sb("k_scale", UNIT), k_squares
            mask_t, weight, q_col, eps = ph.sb("mask", S), ph.sb("weight", 1), ph.sb("q_col", 1), ph.sb("eps", 1)
            q_scale = [ph.sb(f"q_scale{p}", HQ * UNIT) for p in (0, 1)]
            sn = ph.sems("weight eps squares qs_mm q_eps q_scale k_squares k_copied k_eps k_scale k_diagonal kb_mm masked")
        else:
            q32, o32 = ph.sb("q32", UNIT * S), ph.sb("o32", HQ * S)
            bq_cols, bk_cols, bv_cols = ph.sb("bq_cols", GROUPS * HQ), ph.sb("bk_cols", GROUPS), ph.sb("bv_cols", GROUPS)
        bank_k, bank_q, bank_v, bank_s0, bank_s1, bank_pT, bank_o, bank_out = (C.ps[:, blk(k, BANK)] for k in range(8))
        bank_s = (bank_s0, bank_s1)
        q_sums, k_sums = bank_v[:, 2 * HD:2 * HD + UNIT], bank_v[:, 2 * HD + UNIT:2 * HD + 2 * UNIT]
        SCALE = HD ** -0.5
        KEYS_AT = 2
        block = ctx.enter_context(nc.Block())

        def head(tile, h, width=128):
            return tile[:, h * width:(h + 1) * width]

        def heads(tile):
            return tile.rearrange("p (h c) -> p h c", h=HQ)

        def ahead(g, b, n):
            return (g + (b + n) // B, (b + n) % B)

        def number(g, b):
            return g * B + b

        def steps(eng, step):
            for b in range(B):
                step(0, b)
            with eng.Fori(1, GROUPS - 2) as g:
                for b in range(B):
                    step(g, b)
            for g in (GROUPS - 2, GROUPS - 1):
                for b in range(B):
                    step(g, b)

        def exists(g):
            return not (isinstance(g, int) and g >= GROUPS)

        V_CHUNK, K_CHUNK, Q_CHUNK, O_CHUNK, CHUNKS = 0, 1, 2, 6, 10

        def nth(g, c):
            return g * (CHUNKS // 2) + c // 2 + 1

        def chunk_in(eng, g, c):
            eng.wait_ge(s[f"raw_in{c % 2}"], 16 * nth(g, c))

        def chunk_split(eng, g, c):
            eng.wait_ge(s[f"split{c % 2}"], nth(g, c))

        @block.sync
        def _(sp):
            def load_chunk(g, c):
                wait_from_one(sp, s[f"split{c % 2}"], nth(g, c) - 1)
                src = (wkv[bass.ds(g, 1), c] if c < Q_CHUNK else wq[bass.ds(g, 1), c - Q_CHUNK] if c < O_CHUNK
                       else wo[bass.ds(g, 1), c - O_CHUNK])
                sp.dma_start(raw[c % 2][:, :], src.rearrange("a p c -> p (a c)")).then_inc(s[f"raw_in{c % 2}"], 16)

            if normed:
                sp.dma_start(weight[:, :], k_norm).then_inc(s["columns"], 16)
                sp.dma_start(q_col[:, :], q_norm).then_inc(s["columns"], 16)
                sp.dma_start(mask_t[:, :], mask).then_inc(s["columns"], 16)
            else:
                for dst, src in ((bq_cols, bq), (bk_cols, bk), (bv_cols, bv)):
                    sp.dma_start(dst[:, :], src).then_inc(s["columns"], 16)
            for g in range(GROUPS):
                for c in range(CHUNKS):
                    load_chunk(g, c)

        @block.gpsimd
        def _(pool):
            if normed:
                pool.memset(eps[:, :], HD * QK_EPS).then_inc(sn["eps"], 1)
                pool.wait_ge(sn["eps"], 1)

            def split_chunk(g, c):
                pair, at = ((wv_s, (g % 2) * CHUNK) if c == V_CHUNK else (wk_s, 0) if c == K_CHUNK
                            else (wq_s, (c - Q_CHUNK) * CHUNK))
                hi, lo = (h[:, bass.ds(at, CHUNK)] for h in pair)
                chunk_in(pool, g, c)
                pool.tensor_tensor(hi, raw[c % 2][:, :], C.ones[:, 0:1].to_broadcast([128, CHUNK]), ALU.mult).then_inc(s["chunk_hi"], 1)
                pool.wait_ge(s["chunk_hi"], O_CHUNK * g + c + 1)
                minus(pool, lo, raw[c % 2][:, :], hi).then_inc(s[f"split{c % 2}"], 1)

            def normalise(t):
                pool.wait_ge(s["inverse"], t + 1)
                pool.tensor_tensor(heads(probs[:, :]), heads(probs[:, :]), along_last(total[:, :], S), ALU.mult).then_inc(s["probs"], 1)

            def query_scale(P, unit, h):
                pool.wait_ge(sn["q_eps"], P + 1)
                out = q_scale[unit][:, h * UNIT:(h + 1) * UNIT]
                pool.tensor_tensor(out, out, C.neg_half[:, 0:UNIT], ALU.pow).then_inc(sn["q_scale"], 1)

            def key_scale(u):
                pool.wait_ge(sn["k_eps"], u + 1)
                pool.tensor_tensor(k_scale[:, :], k_scale[:, :], C.neg_half[:, 0:UNIT], ALU.pow).then_inc(sn["k_scale"], 1)
            if normed:
                for P in range(UNIT):
                    query_scale(P, 0, P)
                    if P == 0:
                        key_scale(0)
            normalise(0)
            split_chunk(1, V_CHUNK)
            pool.wait_ge(s["q_mm"], UNIT + 1)
            split_chunk(1, K_CHUNK)
            split_chunk(1, Q_CHUNK)

            def step(g, b):
                t = number(g, b)
                gp, bp = ahead(g, b, 5)
                if normed and exists(ahead(g, b, 4)[0]):
                    query_scale(t + 4, (b + 4) // UNIT % 2, (b + 4) % UNIT)
                    if (b + 4) % UNIT == 0:
                        key_scale(g * 2 + (b + 4) // UNIT)
                if exists(gp + 1):
                    if bp == 3:
                        pool.wait_ge(s["v_mm"], t + 2)
                        split_chunk(gp + 1, V_CHUNK)
                    if bp == 4:
                        pool.wait_ge(s["q_mm"], t + 6)
                        split_chunk(gp + 1, K_CHUNK)
                    if bp >= 4:
                        pool.wait_ge(s["q_mm"], t + 6)
                        split_chunk(gp + 1, Q_CHUNK + bp - 4)
                if exists(ahead(g, b, 1)[0]):
                    normalise(t + 1)
            steps(pool, step)

        @block.tensor
        def _(pe):
            def project(P, g, b):
                unit, h = b // UNIT, b % UNIT
                if h == 0:
                    if b == 0:
                        chunk_split(pe, g, K_CHUNK)
                    wait_from_one(pe, s["kn"], g * 2 + unit)
                    matmul_tiles(pe, bank_k, [tuple(head(x, k) for x in wk_s) for k in range(KT)],
                                 tokens(C.cT, unit)).then_inc(s["k_mm"], 1)
                if unit == 0:
                    chunk_split(pe, g, Q_CHUNK + h)
                wait_from_one(pe, s["q_lo"], P)
                matmul_tiles(pe, bank_q, [tuple(head(x, h * KT + k) for x in wq_s) for k in range(KT)],
                             tokens(xT, unit)).then_inc(s["q_mm"], 1)

            def tokens(pair, unit):
                return [tuple(x[:, k * B * S + unit * UNIT * S:k * B * S + (unit + 1) * UNIT * S] for x in pair) for k in range(KT)]

            def sums(P, g, b, n_v):
                pe.wait_ge(sn["squares"], P + 1)
                wait_from_one(pe, sn["q_eps"], P)
                wait_from_one(pe, s["v_lo"], n_v)
                for j in range(UNIT):
                    last = pe.matmul(q_sums[:, j:j + 1], head(squares, j), C.ones[:, 0:1], start=True, stop=True)
                if b % UNIT == 0:
                    pe.wait_ge(sn["k_squares"], g * 2 + b // UNIT + 1)
                    for j in range(UNIT):
                        last = pe.matmul(k_sums[:, j:j + 1], head(k_squares, j), C.ones[:, 0:1], start=True, stop=True)
                last.then_inc(sn["qs_mm"], 1)
                if b % UNIT == 1:
                    pe.wait_ge(sn["k_diagonal"], g * 2 + b // UNIT + 1)
                    pe.wait_ge(sn["k_copied"], g * 2 + b // UNIT + 1)
                    pe.matmul(bank_k, C.ones[:, :], k_diagonal[:, :], start=True, stop=True).then_inc(sn["kb_mm"], 1)

            def scores(t, g, b):
                unit, j = b // UNIT, b % UNIT
                if j == 0:
                    pe.wait_ge(s["k_lo"], g * 2 + unit + 1)
                    pe.wait_ge(s["q_lo"], UNIT * (g * 2 + unit + 1))
                wait_from_one(pe, sn["masked"] if normed else s["exped"], HQ * (t - 1))
                for h in range(HQ):
                    last = matmul_split(pe, head(bank_s[b % 2], h), tuple(head(x, h * UNIT + j) for x in qT[unit]),
                                        tuple(head(x, j) for x in kT[unit]), True, True)
                last.then_inc(s["s_mm"], 1)

            def values(t, g, b):
                if b == 0:
                    chunk_split(pe, g, V_CHUNK)
                wait_from_one(pe, s["v_lo"], t)
                if normed and exists(ahead(g, b, 3)[0]):
                    wait_from_one(pe, sn["q_eps"], t + UNIT)
                turn = g % 2 if isinstance(g, int) else pe.snap(g % 2)
                matmul_tiles(pe, bank_v[:, 0:HD], [tuple(x[:, k * B * S + b * S:k * B * S + (b + 1) * S] for x in C.cT)
                                                   for k in range(KT)],
                             [tuple(x[:, bass.ds(turn * CHUNK + k * HD, HD)] for x in wv_s) for k in range(KT)])\
                    .then_inc(s["v_mm"], 1)

            def project_out(t, g, b):
                pe.wait_ge(s["oT_lo"], t + 1)
                if b == 0:
                    for h in (HQ - 2, HQ - 1):
                        chunk_split(pe, g, O_CHUNK + h)
                wait_from_one(pe, s["added"], t)
                turn = g % 2 if isinstance(g, int) else pe.snap(g % 2)
                matmul_tiles(pe, bank_out, [tuple(head(x, h) for x in oT) for h in range(HQ)],
                             [tuple(x[:, bass.ds(turn * (HQ * D) + h * D, D)] for x in wo_s) for h in range(HQ)])\
                    .then_inc(s["o_mm"], 1)
            for P in range(UNIT + 1):
                project(P, 0, P)
                if normed and P < UNIT:
                    sums(P, 0, P, 0)
            scores(0, 0, 0)
            values(0, 0, 0)
            if normed:
                sums(UNIT, 0, UNIT, 1)

            def step(g, b):
                t = number(g, b)
                next_item, piece = ahead(g, b, 1), ahead(g, b, 5)
                if exists(next_item[0]):
                    scores(t + 1, *next_item)
                if exists(piece[0]):
                    project(t + 5, *piece)
                pe.wait_ge(s["probs"], t + 1)
                wait_from_one(pe, s["pT_lo"], t)
                for h in range(HQ):
                    last = pe.transpose(head(bank_pT, h), head(probs, h), C.ident[:, :])
                last.then_inc(s["pT_mm"], 1)
                if exists(next_item[0]):
                    values(t + 1, *next_item)
                if not (isinstance(t, int) and t == 0):
                    project_out(t - 1, *ahead(g, b, -1))
                pe.wait_ge(s["pT_lo"], t + 1)
                pe.wait_ge(s["v_lo"], t + 1)
                wait_from_one(pe, s["oT_lo"], t)
                matmul_split(pe, bank_o, tuple(x[:, :] for x in v_s[b % 2]), tuple(x[:, :] for x in pT),
                             True, True).then_inc(s["av_mm"], 1)
                if normed and exists(piece[0]):
                    sums(t + 5, *piece, t + 2)
            steps(pe, step)
            project_out(GROUPS * B - 1, GROUPS - 1, B - 1)

        @block.scalar
        def _(act):
            def split_first(c):
                chunk_in(act, 0, c)
                hi = wv_s[0] if c == V_CHUNK else wk_s[0] if c == K_CHUNK else wq_s[0][:, (c - Q_CHUNK) * CHUNK:(c - Q_CHUNK + 1) * CHUNK]
                act.activation(hi[:, 0:CHUNK], raw[c % 2][:, :], ACT.Copy).then_inc(s["chunk_hi"], 1)

            def split_wo(g, h):
                chunk_in(act, g, O_CHUNK + h)
                wait_from_one(act, s["o_mm"], B * (g - 1))
                hi = wo_s[0][:, bass.ds((g % 2) * (HQ * D) + h * D, D)]
                act.activation(hi, raw[h % 2][:, :], ACT.Copy).then_inc(s["wo_hi"], 1)

            def keys(u):
                if normed:
                    act.wait_ge(s["k_mm"], u + 1)
                    wait_from_one(act, s["kn"], u)
                    act.activation(k_squares[:, :], bank_k, ACT.Square).then_inc(sn["k_squares"], 1)

            def split_keys(u, unit):
                act.wait_ge(s["kn"], u + 1)
                wait_from_one(act, s["s_mm"], UNIT * (u - 1))
                act.activation(kT[unit][0][:, :], kn[:, :], ACT.Copy).then_inc(s["k_hi"], 1)

            def queries(P, g, b):
                unit, h = b // UNIT, b % UNIT
                act.wait_ge(s["q_mm"] if normed else s["q32"], P + 1)
                if h == 0:
                    wait_from_one(act, s["s_mm"], UNIT * (g * 2 + unit - 1))
                out = head(qT[unit][0], h, UNIT * S)
                if normed:
                    act.activation(out, bank_q, ACT.Copy).then_inc(s["q_hi"], 1)
                    wait_from_one(act, sn["qs_mm"], P)
                    act.activation(squares[:, :], bank_q, ACT.Square).then_inc(sn["squares"], 1)
                else:
                    act.activation(out, q32[:, :], ACT.Copy).then_inc(s["q_hi"], 1)

            def exps(t, b):
                act.wait_ge(s["neg_max"], t + 1)
                if not normed:
                    wait_from_one(act, s["pT_mm"], t)
                src = probs if normed else bank_s[b % 2]
                for h in range(HQ):
                    act.activation(head(probs, h), head(src, h), ACT.Exp, bias=neg_max[:, h:h + 1],
                                   scale=1.0 if normed else SCALE, accum_out=total[:, h:h + 1]).then_inc(s["exped"], 1)

            def split_v(t, b):
                act.wait_ge(s["v_mm"], t + 1)
                wait_from_one(act, s["av_mm"], t - 1)
                act.activation(v_s[b % 2][0][:, :], bank_v[:, 0:HD], ACT.Copy).then_inc(s["v_hi"], 1)

            def split_oT(t):
                act.wait_ge(s["av_mm"] if normed else s["o32"], t + 1)
                wait_from_one(act, s["o_mm"], t)
                act.activation(oT[0][:, :], bank_o if normed else o32[:, :], ACT.Copy).then_inc(s["oT_hi"], 1)
            for c in range(O_CHUNK):
                split_first(c)
                if c >= Q_CHUNK:
                    P = c - Q_CHUNK
                    if P == 0:
                        keys(0)
                    queries(P, 0, P)
                    if P == KEYS_AT:
                        split_keys(0, 0)
            keys(1)
            queries(UNIT, 0, UNIT)
            for h in range(HQ):
                split_wo(0, h)
            split_v(0, 0)
            exps(0, 0)

            def step(g, b):
                t = number(g, b)
                gp, bp = piece = ahead(g, b, 5)
                if not (isinstance(t, int) and t == 0):
                    split_oT(t - 1)
                if exists(gp):
                    u = gp * 2 + bp // UNIT
                    if bp % UNIT == 0:
                        keys(u)
                    if bp % UNIT == KEYS_AT:
                        split_keys(u, bp // UNIT)
                    queries(t + 5, gp, bp)
                act.wait_ge(s["pT_mm"], t + 1)
                wait_from_one(act, s["av_mm"], t)
                act.activation(pT[0][:, :], bank_pT, ACT.Copy).then_inc(s["pT_hi"], 1)
                if exists(ahead(g, b, 1)[0]):
                    split_v(t + 1, (b + 1) % B)
                    exps(t + 1, (b + 1) % B)
                if 3 <= b < 3 + HQ and exists(g + 1):
                    split_wo(g + 1, b - 3)
            steps(act, step)
            split_oT(GROUPS * B - 1)

        @block.vector
        def _(dve):
            def split_first(c):
                dve.wait_ge(s["chunk_hi"], c + 1)
                at = (c - Q_CHUNK) * CHUNK if c >= Q_CHUNK else 0
                hi, lo = (x[:, at:at + CHUNK] for x in (wv_s if c == V_CHUNK else wk_s if c == K_CHUNK else wq_s))
                minus(dve, lo, raw[c % 2][:, :], hi).then_inc(s[f"split{c % 2}"], 1)

            def split_wo(g, h):
                dve.wait_ge(s["wo_hi"], HQ * g + h + 1)
                hi, lo = (x[:, bass.ds((g % 2) * (HQ * D) + h * D, D)] for x in wo_s)
                minus(dve, lo, raw[h % 2][:, :], hi).then_inc(s[f"split{h % 2}"], 1)

            def keys(u, g, b):
                if normed:
                    dve.wait_ge(sn["k_squares"], u + 1)
                    wait_from_one(dve, s["k_lo"], u)
                    dve.tensor_copy(kn[:, :], bank_k).then_inc(sn["k_copied"], 1)
                else:
                    dve.wait_ge(s["k_mm"], u + 1)
                    wait_from_one(dve, s["k_lo"], u)
                    dve.tensor_scalar(kn[:, :], bank_k, bk_cols[:, bass.ds(g, 1)], None, ALU.add).then_inc(s["kn"], 1)

            def key_eps(u):
                dve.wait_ge(sn["qs_mm"], UNIT * u + 1)
                dve.tensor_scalar(k_scale[:, :], k_sums, HD * QK_EPS, None, ALU.add).then_inc(sn["k_eps"], 1)

            def key_diagonal(u):
                dve.wait_ge(sn["k_scale"], u + 1)
                dve.tensor_tensor(k_diagonal[:, :].rearrange("p (j t) -> p j t", j=UNIT), along_last(k_scale[:, :], S),
                                  C.ident[:, :].unsqueeze(1).to_broadcast([128, UNIT, S]), ALU.mult).then_inc(sn["k_diagonal"], 1)

            def scale_keys(u):
                dve.wait_ge(sn["kb_mm"], u + 1)
                dve.wait_ge(sn["k_copied"], u + 1)
                dve.scalar_tensor_tensor(kn[:, :], kn[:, :], weight[:, 0:1], bank_k, ALU.mult, ALU.mult).then_inc(s["kn"], 1)

            def split_keys(u, unit):
                dve.wait_ge(s["k_hi"], u + 1)
                minus(dve, kT[unit][1][:, :], kn[:, :], kT[unit][0][:, :]).then_inc(s["k_lo"], 1)

            def queries(P, g, b):
                unit, h = b // UNIT, b % UNIT
                hi, lo = (head(x, h, UNIT * S) for x in qT[unit])
                if normed:
                    dve.wait_ge(sn["squares"], P + 1)
                    minus(dve, lo, bank_q, hi).then_inc(s["q_lo"], 1)
                else:
                    dve.wait_ge(s["q_hi"], P + 1)
                    minus(dve, lo, q32[:, :], hi).then_inc(s["q_lo"], 1)

            def bias_queries(P, g, h):
                dve.wait_ge(s["q_mm"], P + 1)
                wait_from_one(dve, s["q_lo"], P)
                dve.tensor_scalar(q32[:, :], bank_q, bq_cols[:, bass.ds(g * HQ + h, 1)], None, ALU.add).then_inc(s["q32"], 1)

            def query_eps(P, g, b):
                unit, h = b // UNIT, b % UNIT
                dve.wait_ge(sn["qs_mm"], P + 1)
                if h == 0:
                    wait_from_one(dve, sn["masked"], HQ * UNIT * (g * 2 + unit - 1))
                dve.tensor_scalar(q_scale[unit][:, h * UNIT:(h + 1) * UNIT], q_sums, HD * QK_EPS, None, ALU.add).then_inc(sn["q_eps"], 1)

            def add_mask(t, b):
                unit, j = b // UNIT, b % UNIT
                dve.wait_ge(s["s_mm"], t + 1)
                if j == 0:
                    pieces = t + UNIT
                    dve.wait_ge(sn["q_scale"], pieces)
                wait_from_one(dve, s["pT_mm"], t)
                for h in range(HQ):
                    at = h * UNIT + j
                    dve.scalar_tensor_tensor(head(probs, h), head(bank_s[b % 2], h), q_scale[unit][:, at:at + 1], mask_t[:, :],
                                             ALU.mult, ALU.add).then_inc(sn["masked"], 1)

            def maximum(t, b):
                wait_from_one(dve, s["exped"], HQ * t)
                if normed:
                    dve.wait_ge(sn["masked"], HQ * (t + 1))
                    dve.tensor_reduce(neg_max[:, :], heads(probs[:, :]), AX.X, ALU.max, negate=True).then_inc(s["neg_max"], 1)
                else:
                    dve.wait_ge(s["s_mm"], t + 1)
                    dve.tensor_reduce(neg_max[:, :], heads(bank_s[b % 2]), AX.X, ALU.max).then_inc(s["raw_max"], 1)
                    dve.wait_ge(s["raw_max"], t + 1)
                    dve.tensor_scalar(neg_max[:, :], neg_max[:, :], -SCALE, None, ALU.mult).then_inc(s["neg_max"], 1)

            def invert(t):
                dve.wait_ge(s["exped"], HQ * (t + 1))
                dve.reciprocal(total[:, :], total[:, :]).then_inc(s["inverse"], 1)

            def split_v(t, b):
                dve.wait_ge(s["v_hi"], t + 1)
                minus(dve, v_s[b % 2][1][:, :], bank_v[:, 0:HD], v_s[b % 2][0][:, :]).then_inc(s["v_lo"], 1)

            def split_oT(t):
                dve.wait_ge(s["oT_hi"], t + 1)
                minus(dve, oT[1][:, :], bank_o if normed else o32[:, :], oT[0][:, :]).then_inc(s["oT_lo"], 1)

            def bias_out(t, g):
                dve.wait_ge(s["av_mm"], t + 1)
                wait_from_one(dve, s["oT_lo"], t)
                dve.tensor_scalar(o32[:, :], bank_o, bv_cols[:, bass.ds(g, 1)], None, ALU.add).then_inc(s["o32"], 1)

            def add_out(t, b):
                dve.wait_ge(s["o_mm"], t + 1)
                x_b = C.x[:, blk(b, D)]
                dve.tensor_tensor(x_b, x_b, bank_out, ALU.add).then_inc(s["added"], 1)
            dve.wait_ge(s["columns"], 48)
            if normed:
                dve.scalar_tensor_tensor(weight[:, :], weight[:, :], HD ** 0.5, q_col[:, :], ALU.mult, ALU.mult).then_inc(sn["weight"], 1)
                dve.wait_ge(sn["weight"], 1)
            for c in range(O_CHUNK):
                split_first(c)
                if c >= Q_CHUNK:
                    P = c - Q_CHUNK
                    if P == 0:
                        keys(0, 0, 0)
                    if not normed:
                        bias_queries(P, 0, P)
                    queries(P, 0, P)
                    if P == KEYS_AT and not normed:
                        split_keys(0, 0)
                    if normed:
                        if P == 0:
                            key_eps(0)
                        query_eps(P, 0, P)
                        if P == 1:
                            key_diagonal(0)
                        if P == KEYS_AT:
                            scale_keys(0)
                            split_keys(0, 0)
            keys(1, 0, UNIT)
            if not normed:
                bias_queries(UNIT, 0, 0)
            queries(UNIT, 0, UNIT)
            for h in range(HQ):
                split_wo(0, h)
            if normed:
                add_mask(0, 0)
            maximum(0, 0)
            split_v(0, 0)
            invert(0)

            def step(g, b):
                t = number(g, b)
                gp, bp = ahead(g, b, 5)
                u = gp * 2 + bp // UNIT
                before = ahead(g, b, 4)
                if not (isinstance(t, int) and t == 0):
                    if not normed:
                        bias_out(t - 1, ahead(g, b, -1)[0])
                    split_oT(t - 1)
                if normed and exists(before[0]):
                    if before[1] % UNIT == 0:
                        key_eps(before[0] * 2 + before[1] // UNIT)
                    query_eps(t + 4, *before)
                if exists(gp):
                    if bp % UNIT == 0:
                        keys(u, gp, bp)
                    if normed and bp % UNIT == 2:
                        scale_keys(u)
                    if not normed:
                        bias_queries(t + 5, gp, bp % UNIT)
                    queries(t + 5, gp, bp)
                    if normed and bp % UNIT == 1:
                        key_diagonal(u)
                    if bp % UNIT == KEYS_AT:
                        split_keys(u, bp // UNIT)
                more = exists(ahead(g, b, 1)[0])
                if normed and more:
                    add_mask(t + 1, (b + 1) % B)
                if not normed and more:
                    maximum(t + 1, (b + 1) % B)
                dve.wait_ge(s["pT_hi"], t + 1)
                minus(dve, pT[1][:, :], bank_pT, pT[0][:, :]).then_inc(s["pT_lo"], 1)
                if more:
                    split_v(t + 1, (b + 1) % B)
                    if normed:
                        maximum(t + 1, (b + 1) % B)
                    invert(t + 1)
                if not (isinstance(t, int) and t == 0):
                    add_out(t - 1, (b - 1) % B)
                if 3 <= b < 3 + HQ and exists(g + 1):
                    split_wo(g + 1, b - 3)
            steps(dve, step)
            if not normed:
                bias_out(GROUPS * B - 1, GROUPS - 1)
            split_oT(GROUPS * B - 1)
            add_out(GROUPS * B - 1, B - 1)



H0 = 32
KV0 = 8
HD0 = 16
ROUNDS = 4
RH = H0 // ROUNDS
QUERIES_PER_KV = H0 // KV0
KVD0 = KV0 * HD0


def attention_small_heads(nc, C, wq, wkv, wo, bkv, bq, bo, cT):
    with ExitStack() as ctx:
        ph = Phase(nc, ctx, "a0")
        t = NormBuffers(ph)
        xT = [ph.split(f"xT{p}", D) for p in (0, 1)]
        cT_raw = [ph.sb(f"cT_raw{p}", D) for p in (0, 1)]
        cT_s = [ph.split(f"cT{p}", D) for p in (0, 1)]
        raw = [ph.sb(n, c) for n, c in (("wkv_raw", KT * 2 * KVD0), ("wq_raw", KT * D), ("wo_raw", KT * D))]
        wkv_s, wq_s, wo_s = (ph.split(n, c) for n, c in (("wkv", KT * 2 * KVD0), ("wq", KT * D), ("wo", KT * D)))
        bkv_row, bq_row, bo_row = ph.sb("bkv", 2 * KVD0), ph.sb("bq", D), ph.sb("bo", D)
        kv, q, k_wide = ph.sb("kv", 2 * KVD0), ph.sb("q", D), ph.sb("k_wide", D)
        v_s, qT, k2 = ph.split("v", KVD0), ph.split("qT", D), ph.split("k2", 2 * D)
        keep = ph.sb("keep", 2)
        neg_max, total = ph.sb("neg_max", H0), ph.sb("total", H0)
        raw_max = ph.sb("raw_max", H0)
        probs = [ph.sb(f"probs{r}", RH * S) for r in (0, 1)]
        pT = [ph.split(f"pT{r}", RH * S) for r in (0, 1)]
        o, oT = ph.sb("o", D), ph.split("oT", D)
        s = ph.sems(NORM_SEMS + " w_in rows_in c_in keep w_hi w_lo biased cT_hi cT_lo kv_mm q_mm kv q k_wide v_split"
                    " kT_mm k2_hi k2_lo qT_mm qT_hi qT_lo even_mm s_mm raw_max neg_max exped pT_mm pT_hi pT_lo av_mm inverse"
                    " o oT_mm oT_hi oT_lo o_mm added")
        bank = [C.ps[:, blk(k, BANK)] for k in range(8)]
        bank_s = [C.ps[:, 2 * BANK * r:2 * BANK * (r + 1)] for r in (0, 1)]
        bank_pT = C.ps[:, 4 * BANK:6 * BANK]
        bank_av, bank_misc = bank[6], bank[7]
        SCALE = HD0 ** -0.5
        block = ctx.enter_context(nc.Block())

        def x_of(i):
            return C.x[:, blk(i, D)]

        def tiles(pair, n):
            return [tuple(h[:, k * n:(k + 1) * n] for h in pair) for k in range(KT)]

        @block.sync
        def _(sp):
            for dst, src in zip(raw, (wkv, wq, wo)):
                sp.dma_start(dst[:, :], src).then_inc(s["w_in"], 16)
            for dst, src in zip((bkv_row, bq_row, bo_row), (bkv, bq, bo)):
                sp.dma_start(dst[:, :], src.partition_broadcast(128)).then_inc(s["rows_in"], 16)

            for i in range(B):
                wait_from_one(sp, s["cT_lo"], i - 1)
                wait_from_one(sp, s["c_in"], 16 * i)
                sp.dma_start(cT_raw[i % 2][:, :], cT[i]).then_inc(s["c_in"], 16)

        @block.gpsimd
        def _(pool):
            def front(i, p):
                norm_gpsimd(pool, C, s, t, i)
                pool.wait_ge(s["cT_hi"], i + 1)
                minus(pool, cT_s[p][1][:, :], cT_raw[p][:, :], cT_s[p][0][:, :]).then_inc(s["cT_lo"], 1)

            def back(i, p):
                pool.wait_ge(s["xn"], i + 1)
                pool.tensor_tensor(x_of(i), x_of(i), bo_row[:, :], ALU.add).then_inc(s["biased"], 1)
                pool.wait_ge(s["kv"], i + 1)
                wait_from_one(pool, s["kT_mm"], i)
                pool.tensor_tensor(k_wide[:, :].rearrange("p (k g d) -> p k g d", k=KV0, g=QUERIES_PER_KV),
                                   kv[:, 0:KVD0].rearrange("p (k d) -> p k d", k=KV0).unsqueeze(2).to_broadcast(
                                       [128, KV0, QUERIES_PER_KV, HD0]),
                                   C.ones[:, :].rearrange("p (k d) -> p k d", k=KV0).unsqueeze(2).to_broadcast(
                                       [128, KV0, QUERIES_PER_KV, HD0]), ALU.mult).then_inc(s["k_wide"], 1)
                wait_from_one(pool, s["av_mm"], ROUNDS * i)
                v = kv[:, KVD0:2 * KVD0]
                pool.tensor_tensor(v_s[0][:, :], v, C.ones[:, :], ALU.mult).then_inc(s["v_split"], 1)
                pool.wait_ge(s["v_split"], 2 * i + 1)
                minus(pool, v_s[1][:, :], v, v_s[0][:, :]).then_inc(s["v_split"], 1)
            pool.wait_ge(s["rows_in"], 48)
            in_pairs(pool, front, back)

        @block.tensor
        def _(pe):
            def front(i, p):
                wait_from_one(pe, s["oT_lo"], i - 1)
                norm_tensor(pe, C, s, t.xn[:, :], bank_misc, i)

            def back(i, p):
                wait_from_one(pe, s["added"], i)
                pe.wait_ge(s["cT_lo"], i + 1)
                matmul_tiles(pe, bank_av[:, 0:2 * KVD0], tiles(cT_s[p], S), tiles(wkv_s, 2 * KVD0)).then_inc(s["kv_mm"], 1)
                pe.wait_ge(s["xT_lo"], min(i + 2, B) if isinstance(i, int) else i + 2)
                matmul_tiles(pe, bank_misc, tiles(xT[p], S), tiles(wq_s, D)).then_inc(s["q_mm"], 1)
                pe.wait_ge(s["k_wide"], i + 1)
                wait_from_one(pe, s["pT_lo"], ROUNDS * i)
                for k in range(KT):
                    last = pe.transpose(bank[5][:, k * 128:(k + 1) * 128], k_wide[:, k * 128:(k + 1) * 128], C.ident[:, :])
                last.then_inc(s["kT_mm"], 1)
                pe.wait_ge(s["q"], i + 1)
                for k in range(KT):
                    last = pe.transpose(bank[4][:, k * 128:(k + 1) * 128], q[:, k * 128:(k + 1) * 128], C.ident[:, :])
                last.then_inc(s["qT_mm"], 1)

                def scores(r):
                    if r >= 2:
                        pe.wait_ge(s["exped"], RH * (ROUNDS * i + r - 1))
                    for a in (0, 2, 1, 3):
                        rows = slice(32 * a, 32 * a + 32)
                        if a == 1:
                            pe.wait_ge(s["even_mm"], ROUNDS * i + r + 1)
                        last = matmul_split(pe, bank_s[r % 2][:, a * 2 * S:(a + 1) * 2 * S],
                                            tuple(h[rows, r * 128:(r + 1) * 128] for h in qT),
                                            tuple(h[rows, r * 2 * S:(r + 1) * 2 * S] for h in k2), True, True)
                        if a == 2:
                            last.then_inc(s["even_mm"], 1)
                    last.then_inc(s["s_mm"], 1)

                def turn(r):
                    pe.wait_ge(s["exped"], RH * (ROUNDS * i + r + 1))
                    if r > 0:
                        pe.wait_ge(s["pT_lo"], ROUNDS * i + r)
                    for h in range(RH):
                        last = pe.transpose(bank_pT[:, h * S:(h + 1) * S], probs[r % 2][:, h * S:(h + 1) * S], C.ident[:, :])
                    last.then_inc(s["pT_mm"], 1)

                def mix(r):
                    pe.wait_ge(s["pT_lo"], ROUNDS * i + r + 1)
                    if r == 0:
                        pe.wait_ge(s["v_split"], 2 * (i + 1))
                    for h in range(RH):
                        at, k = (r * RH + h) * HD0, (r * RH + h) // QUERIES_PER_KV * HD0
                        last = matmul_split(pe, bank_av[:, at:at + HD0], tuple(x[:, h * S:(h + 1) * S] for x in pT[r % 2]),
                                            tuple(x[:, k:k + HD0] for x in v_s), True, True)
                    last.then_inc(s["av_mm"], 1)
                pe.wait_ge(s["k2_lo"], 2 * (i + 1))
                pe.wait_ge(s["qT_lo"], i + 1)
                scores(0)
                scores(1)
                turn(0)
                scores(2)
                turn(1)
                mix(0)
                scores(3)
                turn(2)
                mix(1)
                turn(3)
                mix(2)
                mix(3)
                pe.wait_ge(s["o"], i + 1)
                for k in range(KT):
                    last = pe.transpose(bank_misc[:, k * 128:(k + 1) * 128], o[:, k * 128:(k + 1) * 128], C.ident[:, :])
                last.then_inc(s["oT_mm"], 1)
                pe.wait_ge(s["oT_lo"], i + 1)
                matmul_tiles(pe, bank_av, tiles(oT, S), tiles(wo_s, D)).then_inc(s["o_mm"], 1)
            pe.wait_ge(s["w_lo"], 3)
            in_pairs(pe, front, back)

        @block.scalar
        def _(act):
            act.wait_ge(s["w_in"], 48)
            for r, pair in zip(raw, (wkv_s, wq_s, wo_s)):
                act.activation(pair[0][:, :], r[:, :], ACT.Copy).then_inc(s["w_hi"], 1)
            act.wait_ge(s["keep"], 1)

            def front(i, p):
                act.wait_ge(s["c_in"], 16 * (i + 1))
                wait_from_one(act, s["kv_mm"], i - 1)
                act.activation(cT_s[p][0][:, :], cT_raw[p][:, :], ACT.Copy).then_inc(s["cT_hi"], 1)
                act.wait_ge(s["xnT"], i + 1)
                wait_from_one(act, s["q_mm"], i - 1)
                act.activation(xT[p][0][:, :], bank_misc, ACT.Copy).then_inc(s["xT_hi"], 1)

            def back(i, p):
                act.wait_ge(s["kT_mm"], i + 1)
                wait_from_one(act, s["s_mm"], ROUNDS * i)
                for c in (0, 1):
                    out = k2[0][:, :].rearrange("p (r c t) -> p r c t", r=ROUNDS, c=2)[:, :, c, :]
                    act.activation(out, tiles_of(bank[5]), ACT.Copy, scale=keep[:, c:c + 1]).then_inc(s["k2_hi"], 1)
                act.wait_ge(s["qT_mm"], i + 1)
                act.activation(qT[0][:, :], bank[4], ACT.Copy).then_inc(s["qT_hi"], 1)

                def exps(r):
                    act.wait_ge(s["neg_max"], ROUNDS * i + r + 1)
                    wait_from_one(act, s["pT_mm"], ROUNDS * i + max(r - 1, 0))
                    if r == 0:
                        wait_from_one(act, s["o"], i)
                    for h in range(RH):
                        k = r * RH + h
                        act.activation(probs[r % 2][:, h * S:(h + 1) * S], bank_s[r % 2][:, h * S:(h + 1) * S], ACT.Exp,
                                       bias=neg_max[:, k:k + 1], scale=SCALE, accum_out=total[:, k:k + 1]).then_inc(s["exped"], 1)

                def split(r):
                    act.wait_ge(s["pT_mm"], ROUNDS * i + r + 1)
                    wait_from_one(act, s["av_mm"], ROUNDS * i + max(r - 1, 0))
                    act.activation(pT[r % 2][0][:, :], bank_pT, ACT.Copy).then_inc(s["pT_hi"], 1)
                exps(0)
                for r in range(1, ROUNDS):
                    exps(r)
                    split(r - 1)
                split(ROUNDS - 1)
                act.wait_ge(s["oT_mm"], i + 1)
                wait_from_one(act, s["o_mm"], i)
                act.activation(oT[0][:, :], bank_misc, ACT.Copy).then_inc(s["oT_hi"], 1)
            in_pairs(act, front, back)

        @block.vector
        def _(dve):
            dve.tensor_reduce(keep[:, :], C.ident[:, :].rearrange("p (a c r) -> p c a r", c=2, r=HD0), AX.XY,
                              ALU.add).then_inc(s["keep"], 1)
            for n, (r, pair) in enumerate(zip(raw, (wkv_s, wq_s, wo_s))):
                dve.wait_ge(s["w_hi"], n + 1)
                minus(dve, pair[1][:, :], r[:, :], pair[0][:, :]).then_inc(s["w_lo"], 1)
            dve.wait_ge(s["rows_in"], 48)
            dve.wait_ge(s["keep"], 1)

            def front(i, p):
                norm_vector(dve, s, t, x_of(i), t.xn[:, :], i)
                dve.wait_ge(s["xT_hi"], i + 1)
                minus(dve, xT[p][1][:, :], bank_misc, xT[p][0][:, :]).then_inc(s["xT_lo"], 1)

            def back(i, p):
                dve.wait_ge(s["kv_mm"], i + 1)
                wait_from_one(dve, s["v_split"], 2 * i)
                dve.tensor_tensor(kv[:, :], bank_av[:, 0:2 * KVD0], bkv_row[:, :], ALU.add).then_inc(s["kv"], 1)
                dve.wait_ge(s["q_mm"], i + 1)
                wait_from_one(dve, s["qT_mm"], i)
                dve.tensor_tensor(q[:, :], bank_misc, bq_row[:, :], ALU.add).then_inc(s["q"], 1)
                dve.wait_ge(s["k2_hi"], 2 * (i + 1))
                for c in (0, 1):
                    lo, hi = (h[:, :].rearrange("p (r c t) -> p r c t", r=ROUNDS, c=2)[:, :, c, :] for h in (k2[1], k2[0]))
                    dve.scalar_tensor_tensor(lo, tiles_of(bank[5]), keep[:, c:c + 1], hi.bitcast(F32), ALU.mult,
                                             ALU.subtract).then_inc(s["k2_lo"], 1)
                dve.wait_ge(s["qT_hi"], i + 1)
                minus(dve, qT[1][:, :], bank[4], qT[0][:, :]).then_inc(s["qT_lo"], 1)

                def maxima(r):
                    n = ROUNDS * i + r + 1
                    dve.wait_ge(s["s_mm"], n)
                    of_round = slice(r * RH, (r + 1) * RH)
                    dve.tensor_reduce(raw_max[:, of_round], bank_s[r % 2].rearrange("p (h t) -> p h t", h=RH), AX.X,
                                      ALU.max).then_inc(s["raw_max"], 1)
                    dve.wait_ge(s["raw_max"], n)
                    dve.tensor_scalar(neg_max[:, of_round], raw_max[:, of_round], -SCALE, None, ALU.mult).then_inc(s["neg_max"], 1)

                def split(r):
                    dve.wait_ge(s["pT_hi"], ROUNDS * i + r + 1)
                    minus(dve, pT[r % 2][1][:, :], bank_pT, pT[r % 2][0][:, :]).then_inc(s["pT_lo"], 1)
                maxima(0)
                maxima(1)
                split(0)
                maxima(2)
                split(1)
                maxima(3)
                split(2)
                dve.wait_ge(s["exped"], RH * ROUNDS * (i + 1))
                dve.reciprocal(total[:, :], total[:, :]).then_inc(s["inverse"], 1)
                split(3)
                dve.wait_ge(s["av_mm"], ROUNDS * (i + 1))
                dve.wait_ge(s["inverse"], i + 1)
                wait_from_one(dve, s["oT_mm"], i)
                dve.tensor_tensor(o[:, :].rearrange("p (h d) -> p h d", h=H0), bank_av.rearrange("p (h d) -> p h d", h=H0),
                                  along_last(total[:, :], HD0), ALU.mult).then_inc(s["o"], 1)
                dve.wait_ge(s["oT_hi"], i + 1)
                minus(dve, oT[1][:, :], bank_misc, oT[0][:, :]).then_inc(s["oT_lo"], 1)
                dve.wait_ge(s["o_mm"], i + 1)
                dve.wait_ge(s["biased"], i + 1)
                dve.tensor_tensor(x_of(i), x_of(i), bank_av, ALU.add).then_inc(s["added"], 1)
            in_pairs(dve, front, back)



def attention_transposed(nc, C, context):
    with ExitStack() as ctx:
        ph = Phase(nc, ctx, "a3")
        t = NormBuffers(ph)
        xT = [ph.split(f"xT{p}", D) for p in (0, 1)]
        c_raw = [ph.sb(f"c_raw{p}", D) for p in (0, 1)]
        c_s = [ph.split(f"c{p}", D) for p in (0, 1)]
        probs = [ph.sb(f"probs{p}", S) for p in (0, 1)]
        total = [ph.sb(f"total{p}", 1) for p in (0, 1)]
        raw_max, neg_max = ph.sb("raw_max", 1), ph.sb("neg_max", 1)
        p_s = [ph.split(f"p{p}", S) for p in (0, 1)]
        s = ph.sems(NORM_SEMS + " c_in c_hi c_lo s_mm raw_max neg_max exped inverse probs p_hi p_lo o_mm added")
        bank_xT, bank_out = C.ps[:, 0:BANK], C.ps[:, 3 * BANK:4 * BANK]
        bank_s = [C.ps[:, (1 + p) * BANK:(1 + p) * BANK + S] for p in (0, 1)]
        SCALE = S ** -0.5
        block = ctx.enter_context(nc.Block())

        def x_of(i):
            return C.x[:, blk(i, D)]

        @block.sync
        def _(sp):
            for i in range(B):
                wait_from_one(sp, s["c_lo"], i - 1)
                wait_from_one(sp, s["c_in"], 16 * i)
                sp.dma_start(c_raw[i % 2][:, :], context[i]).then_inc(s["c_in"], 16)

        @block.gpsimd
        def _(pool):
            def front(i, p):
                norm_gpsimd(pool, C, s, t, i)
                pool.wait_ge(s["c_hi"], i + 1)
                minus(pool, c_s[p][1][:, :], c_raw[p][:, :], c_s[p][0][:, :]).then_inc(s["c_lo"], 1)
            in_pairs(pool, front, lambda i, p: None)

        @block.tensor
        def _(pe):
            def front(i, p):
                norm_tensor(pe, C, s, t.xn[:, :], bank_xT, i)
                pe.wait_ge(s["xT_lo"], i + 1)
                wait_from_one(pe, s["exped"], i - 1)
                lhs = [tuple(h[:, k * S:(k + 1) * S] for h in xT[p]) for k in range(KT)]
                rhs = [tuple(h[:, bass.ds(i * S + k * B * S, S)] for h in C.cT) for k in range(KT)]
                matmul_tiles(pe, bank_s[p], lhs, rhs).then_inc(s["s_mm"], 1)

            def back(i, p):
                pe.wait_ge(s["p_lo"], i + 1)
                pe.wait_ge(s["c_lo"], i + 1)
                wait_from_one(pe, s["added"], i)
                matmul_split(pe, bank_out, tuple(h[:, :] for h in p_s[p]), tuple(h[:, :] for h in c_s[p]),
                             True, True).then_inc(s["o_mm"], 1)
            in_pairs(pe, front, back)

        @block.scalar
        def _(act):
            def front(i, p):
                act.wait_ge(s["c_in"], 16 * (i + 1))
                wait_from_one(act, s["o_mm"], i - 1)
                act.activation(c_s[p][0][:, :], c_raw[p][:, :], ACT.Copy).then_inc(s["c_hi"], 1)
                act.wait_ge(s["xnT"], i + 1)
                wait_from_one(act, s["s_mm"], i - 1)
                act.activation(xT[p][0][:, :], bank_xT, ACT.Copy).then_inc(s["xT_hi"], 1)
                act.wait_ge(s["neg_max"], i + 1)
                wait_from_one(act, s["p_lo"], i - 1)
                act.activation(probs[p][:, :], bank_s[p], ACT.Exp, bias=neg_max[:, 0:1], scale=SCALE,
                               accum_out=total[p][:, :]).then_inc(s["exped"], 1)

            def back(i, p):
                act.wait_ge(s["probs"], i + 1)
                wait_from_one(act, s["o_mm"], i)
                act.activation(p_s[p][0][:, :], probs[p][:, :], ACT.Copy).then_inc(s["p_hi"], 1)
            in_pairs(act, front, back)

        @block.vector
        def _(dve):
            def front(i, p):
                norm_vector(dve, s, t, x_of(i), t.xn[:, :], i)
                dve.wait_ge(s["xT_hi"], i + 1)
                minus(dve, xT[p][1][:, :], bank_xT, xT[p][0][:, :]).then_inc(s["xT_lo"], 1)
                dve.wait_ge(s["s_mm"], i + 1)
                dve.tensor_reduce(raw_max[:, :], bank_s[p], AX.X, ALU.max).then_inc(s["raw_max"], 1)
                dve.wait_ge(s["raw_max"], i + 1)
                wait_from_one(dve, s["exped"], i)
                dve.tensor_scalar(neg_max[:, :], raw_max[:, :], -SCALE, None, ALU.mult).then_inc(s["neg_max"], 1)

            def back(i, p):
                dve.wait_ge(s["exped"], i + 1)
                dve.reciprocal(total[p][:, :], total[p][:, :]).then_inc(s["inverse"], 1)
                dve.wait_ge(s["inverse"], i + 1)
                dve.tensor_scalar(probs[p][:, :], probs[p][:, :], total[p][:, 0:1], None, ALU.mult).then_inc(s["probs"], 1)
                dve.wait_ge(s["p_hi"], i + 1)
                minus(dve, p_s[p][1][:, :], probs[p][:, :], p_s[p][0][:, :]).then_inc(s["p_lo"], 1)
                dve.wait_ge(s["o_mm"], i + 1)
                dve.tensor_tensor(x_of(i), x_of(i), bank_out, ALU.add).then_inc(s["added"], 1)
            in_pairs(dve, front, back)


E3 = 64
TOP = 8


def bias_experts(nc, C, w_router, router_bias, expert_bias, out):
    with ExitStack() as ctx:
        ph = Phase(nc, ctx, "f3")
        t = NormBuffers(ph)
        xT = [ph.split(f"xT{p}", D) for p in (0, 1)]
        xn_all = ph.sb("xn_all", B * D)
        router_raw, router = ph.sb("router_raw", KT * E3), ph.split("router", KT * E3)
        eb_raw, eb = ph.sb("eb_raw", D, rows=E3), ph.split("eb", D, rows=E3)
        row = ph.sb("row", E3)
        scores, most = ph.sb("scores", B * E3), ph.sb("most", B)
        current, rest, top = ph.sb("current", E3), ph.sb("rest", E3), ph.sb("top", TOP)
        w_sum = [ph.sb(f"w_sum{p}", 1) for p in (0, 1)]
        taken = ph.sb("taken", 128)
        wT = [ph.split(f"wT{p}", S, rows=E3) for p in (0, 1)]
        delta = ph.sb("delta", D)
        s = ph.sems(NORM_SEMS + " w_in row_in w_hi w_lo xn_kept logits_mm scores chain below exped padded current"
                    " top taken w_sum takenT wT_hi wT_lo up_mm delta added stored")
        bank_xT, bank_l, bank_wT, bank_up = (C.ps[:, blk(k, BANK)] for k in range(4))
        block = ctx.enter_context(nc.Block())

        def x_of(i):
            return C.x[:, blk(i, D)]

        def nothing(i, p):
            pass

        @block.sync
        def _(sp):
            sp.dma_start(router_raw[:, :], w_router).then_inc(s["w_in"], 16)
            sp.dma_start(eb_raw[:, :], expert_bias).then_inc(s["w_in"], 16)
            sp.dma_start(row[:, :], router_bias.partition_broadcast(128)).then_inc(s["row_in"], 16)
            with sp.Fori(0, B) as i:
                sp.wait_ge(s["added"], i + 1)
                sp.dma_start(out[bass.ds(i, 1)].rearrange("a p d -> p (a d)"), x_of(i)).then_inc(s["stored"], 16)
            sp.wait_ge(s["stored"], 16 * B)

        @block.gpsimd
        def _(pool):
            pool.memset(taken[:, E3:128], 0.0).then_inc(s["padded"], 1)
            in_pairs(pool, lambda i, p: norm_gpsimd(pool, C, s, t, i), nothing)

        @block.tensor
        def _(pe):
            pe.wait_ge(s["w_lo"], 2)

            def back(i, p):
                pe.wait_ge(s["xT_lo"], i + 1)
                wait_from_one(pe, s["scores"], i)
                matmul_tiles(pe, bank_l[:, 0:E3], [tuple(h[:, k * S:(k + 1) * S] for h in xT[p]) for k in range(KT)],
                             [tuple(h[:, k * E3:(k + 1) * E3] for h in router) for k in range(KT)]).then_inc(s["logits_mm"], 1)

            in_pairs(pe, lambda i, p: norm_tensor(pe, C, s, t.xn[:, :], bank_xT, i), back)
            pe.wait_ge(s["padded"], 1)

            def front2(i, p):
                pe.wait_ge(s["taken"], i + 1)
                wait_from_one(pe, s["wT_lo"], i)
                pe.transpose(bank_wT[:, 0:S], taken[:, :], C.ident[:, :]).then_inc(s["takenT"], 1)

            def back2(i, p):
                pe.wait_ge(s["wT_lo"], i + 1)
                wait_from_one(pe, s["delta"], i)
                matmul_split(pe, bank_up, tuple(h[:, :] for h in wT[p]), tuple(h[:, :] for h in eb), True, True)\
                    .then_inc(s["up_mm"], 1)
            in_pairs(pe, front2, back2)

        @block.scalar
        def _(act):
            act.wait_ge(s["w_in"], 32)
            act.activation(router[0][:, :], router_raw[:, :], ACT.Copy).then_inc(s["w_hi"], 1)
            act.activation(eb[0][:, :], eb_raw[:, :], ACT.Copy).then_inc(s["w_hi"], 1)

            def front(i, p):
                act.wait_ge(s["xn"], i + 1)
                act.activation(xn_all[:, blk(i, D)], t.xn[:, :], ACT.Copy).then_inc(s["xn_kept"], 1)
                act.wait_ge(s["xnT"], i + 1)
                wait_from_one(act, s["logits_mm"], i - 1)
                act.activation(xT[p][0][:, :], bank_xT, ACT.Copy).then_inc(s["xT_hi"], 1)
            in_pairs(act, front, nothing)
            act.wait_ge(s["below"], 1)
            act.activation(scores[:, :], scores[:, :], ACT.Exp).then_inc(s["exped"], 1)

            def front2(i, p):
                act.wait_ge(s["takenT"], i + 1)
                wait_from_one(act, s["up_mm"], i - 1)
                act.activation(wT[p][0][:, :], bank_wT[0:E3, 0:S], ACT.Copy).then_inc(s["wT_hi"], 1)
            in_pairs(act, front2, nothing)

        @block.vector
        def _(dve):
            n_link = [0]

            def link(ins):
                n_link[0] += 1
                ins.then_inc(s["chain"], 1)
                dve.wait_ge(s["chain"], n_link[0])
            dve.wait_ge(s["w_hi"], 1)
            minus(dve, router[1][:, :], router_raw[:, :], router[0][:, :]).then_inc(s["w_lo"], 1)
            dve.wait_ge(s["w_hi"], 2)
            minus(dve, eb[1][:, :], eb_raw[:, :], eb[0][:, :]).then_inc(s["w_lo"], 1)
            dve.wait_ge(s["row_in"], 16)

            def front(i, p):
                wait_from_one(dve, s["xn_kept"], i)
                norm_vector(dve, s, t, x_of(i), t.xn[:, :], i)
                dve.wait_ge(s["xT_hi"], i + 1)
                minus(dve, xT[p][1][:, :], bank_xT, xT[p][0][:, :]).then_inc(s["xT_lo"], 1)

            def back(i, p):
                dve.wait_ge(s["logits_mm"], i + 1)
                dve.tensor_tensor(scores[:, blk(i, E3)], bank_l[:, 0:E3], row[:, :], ALU.add).then_inc(s["scores"], 1)
            in_pairs(dve, front, back)
            dve.wait_ge(s["scores"], B)
            s3 = by_sequence(scores[:, :])
            link(dve.tensor_reduce(most[:, :], s3, AX.X, ALU.max))
            dve.tensor_tensor(s3, s3, along_last(most[:, :], E3), ALU.subtract).then_inc(s["below"], 1)
            dve.wait_ge(s["exped"], 1)
            link(dve.tensor_reduce(most[:, :], s3, AX.X, ALU.add))
            link(dve.reciprocal(most[:, :], most[:, :]))
            link(dve.tensor_tensor(s3, s3, along_last(most[:, :], E3), ALU.mult))
            dve.wait_ge(s["xn_kept"], B)

            def front2(i, p):
                dve.tensor_copy(current[:, :], scores[:, blk(i, E3)]).then_inc(s["current"], 1)
                dve.drain()
                dve.max(top[:, :], current[:, :])
                dve.drain()
                dve.match_replace(rest[:, :], top[:, :], current[:, :], 0.0).then_inc(s["top"], 1)
                dve.wait_ge(s["top"], i + 1)
                wait_from_one(dve, s["takenT"], i)
                dve.tensor_tensor(taken[:, 0:E3], current[:, :], rest[:, :], ALU.subtract).then_inc(s["taken"], 1)
                dve.tensor_reduce(w_sum[p][:, :], top[:, :], AX.X, ALU.add).then_inc(s["w_sum"], 1)
                dve.wait_ge(s["wT_hi"], i + 1)
                minus(dve, wT[p][1][:, :], bank_wT[0:E3, 0:S], wT[p][0][:, :]).then_inc(s["wT_lo"], 1)

            def back2(i, p):
                dve.wait_ge(s["up_mm"], i + 1)
                dve.wait_ge(s["w_sum"], i + 1)
                wait_from_one(dve, s["added"], i)
                dve.scalar_tensor_tensor(delta[:, :], xn_all[:, blk(i, D)], w_sum[p][:, 0:1], bank_up, ALU.mult,
                                         ALU.add).then_inc(s["delta"], 1)
                dve.wait_ge(s["delta"], i + 1)
                dve.tensor_tensor(x_of(i), x_of(i), delta[:, :], ALU.add).then_inc(s["added"], 1)
            in_pairs(dve, front2, back2)



class Core:

    def __init__(self, nc, ctx):
        def sb(name, cols):
            return ctx.enter_context(nc.sbuf_tensor(name, [128, cols], F32))
        self.x = sb("x", B * D)
        self.ident, self.ones, self.neg_half = sb("ident", 128), sb("ones", 128), sb("neg_half", 8)
        self.ln_eps, self.falling = sb("ln_eps", 1), sb("falling", E)
        self.to_exp = sb("to_exp", B * E)
        self.ps = ctx.enter_context(nc.psum_tensor("ps", [128, 8 * BANK], F32))


def build(nc, A, out):
    with ExitStack() as ctx:
        def sb(name, cols, dt=F32):
            return ctx.enter_context(nc.sbuf_tensor(name, [128, cols], dt))
        C = Core(nc, ctx)
        set_up(nc, C, A["x"])
        attention_small_heads(nc, C, A["L0_wq"], A["L0_wkv"], A["L0_wo"], A["L0_bkv"], A["L0_xattn_bq"],
                              A["L0_xattn_bo"], A["cT_by_sequence"])
        ffn_phase(nc, C, "f0", GateNet, A["L0_main"], A["L0_side"], A["L0_up"], 1.0 / R,
                  extra=[A[n] for n in ("L0_ffn_gb1", "L0_ffn_ln_gamma", "L0_ffn_ln_beta", "L0_gw2", "L0_ffn_gb2")])
        C.cT = tuple(sb(f"cT_{h}", KT * B * S, F32R) for h in ("hi", "lo"))
        context_transposed(nc, C, A["cT"])
        attention_phase(nc, C, "a1", A["L1_wkv"], A["L1_wq"], A["L1_wo"], q_norm=A["L1_xattn_q_norm_w"],
                        k_norm=A["L1_xattn_k_norm_w"], mask=A["mask"])
        ffn_phase(nc, C, "f1", TopTwo, A["L1_main"], A["L1_side"], A["L1_up"], 1.0, bias=A["L1_ffn_b_base"])
        attention_phase(nc, C, "a2", A["L2_wkv"], A["L2_wq"], A["L2_wo"], bq=A["L2_bq"], bk=A["L2_bk"],
                        bv=A["L2_bv"], bo=A["L2_xattn_bo"])
        ffn_phase(nc, C, "f2", MeanRoute, A["L2_main"], A["L2_side"], A["L2_up"], 2.0, bias=A["L2_ffn_b"],
                  extra=[A["L2_ffn_router_b"]])
        attention_transposed(nc, C, A["context"])
        bias_experts(nc, C, A["L3_router"], A["L3_ffn_router_bias"], A["L3_ffn_expert_bias"], out)


def kernel(**inputs):
    import numpy as np
    import concourse.bacc as bacc
    from concourse.bass_utils import run_bass_kernel_spmd

    def tiled(w):
        return np.ascontiguousarray(w.reshape(KT, 128, -1).transpose(1, 0, 2).reshape(128, -1))

    I = {k: np.asarray(v) for k, v in inputs.items()}
    A = {"x": I["x"]}
    for n, main, a, gate, up in (
            ("L0", I["L0_ffn_weight"].T, I["L0_ffn_lora_A"].transpose(1, 0, 2).reshape(D, ER), I["L0_ffn_gw1"].T,
             I["L0_ffn_lora_B"].reshape(ER, D)),
            ("L1", I["L1_ffn_W_base"].T, I["L1_ffn_A"].reshape(ER, D).T, I["L1_ffn_W_gate"].T,
             I["L1_ffn_B"].transpose(0, 2, 1).reshape(ER, D)),
            ("L2", I["L2_ffn_W"].T, I["L2_ffn_A"].reshape(ER, D).T, I["L2_ffn_router_W"].T,
             I["L2_ffn_B"].transpose(0, 2, 1).reshape(ER, D))):
        A[n + "_main"] = tiled(main)
        A[n + "_side"] = tiled(np.concatenate([a, gate], axis=1))
        A[n + "_up"] = np.ascontiguousarray(up)
    A["L0_gw2"] = I["L0_ffn_gw2"].reshape(-1)
    for n in ("L0_ffn_gb1", "L0_ffn_ln_gamma", "L0_ffn_ln_beta", "L0_ffn_gb2", "L1_ffn_b_base", "L2_ffn_b",
              "L2_ffn_router_b"):
        A[n] = I[n]

    A["L0_wq"], A["L0_wo"] = tiled(I["L0_xattn_Wq"]), tiled(I["L0_xattn_Wo"])
    A["L0_wkv"] = tiled(np.concatenate([I["L0_xattn_Wk"], I["L0_xattn_Wv"]], axis=1))
    A["L0_bkv"] = np.concatenate([I["L0_xattn_bk"], I["L0_xattn_bv"]])
    A["cT_by_sequence"] = I["ctx_4096"].reshape(B, S, KT, 128).transpose(0, 3, 2, 1).reshape(B, 128, D)
    A["context"] = I["ctx_4096"]
    A["L3_router"] = tiled(I["L3_ffn_router_weight"].T)
    for n in ("L0_xattn_bq", "L0_xattn_bo", "L3_ffn_router_bias", "L3_ffn_expert_bias"):
        A[n] = I[n]

    A["cT"] = tiled(I["ctx_4096"].reshape(B * S, D).T)
    A["mask"] = I["mask_1x1xSxS2_ff0"].reshape(S, S)

    def heads_apart(w, n):
        return w.reshape(KT, 128, GROUPS, n, HD).transpose(2, 3, 1, 0, 4).reshape(GROUPS, n, 128, CHUNK)

    def v_and_k(k, v):
        return np.concatenate([heads_apart(v, 1), heads_apart(k, 1)], axis=1)

    def columns(b):
        return b.reshape(-1, HD).T
    A["L1_wq"] = heads_apart(I["L1_xattn_Wq"].T, HQ)
    A["L1_wkv"] = v_and_k(I["L1_xattn_Wk"].T, I["L1_xattn_Wv"].T)
    A["L1_wo"] = I["L1_xattn_Wo"].T.reshape(GROUPS, HQ, HD, D)
    A["L1_xattn_q_norm_w"], A["L1_xattn_k_norm_w"] = columns(I["L1_xattn_q_norm_w"]), columns(I["L1_xattn_k_norm_w"])
    A["L2_wq"] = heads_apart(I["L2_xattn_Wq"], HQ)
    wkv, bkv = I["L2_xattn_Wkv"], I["L2_xattn_bkv"]
    A["L2_wkv"] = v_and_k(wkv[:, :GROUPS * HD], wkv[:, GROUPS * HD:])
    A["L2_wo"] = I["L2_xattn_Wo"].reshape(GROUPS, HQ, HD, D)
    A["L2_bq"], A["L2_bk"], A["L2_bv"] = columns(I["L2_xattn_bq"]), columns(bkv[:GROUPS * HD]), columns(bkv[GROUPS * HD:])
    for n in ("L2_xattn_bo",):
        A[n] = I[n]

    nc = bacc.Bacc("TRN2", target_bir_lowering=False, num_devices=1)
    A = {n: np.ascontiguousarray(a) for n, a in A.items()}
    aps = {n: nc.dram_tensor(f"in_{n}", a.shape, mybir.dt.from_np(a.dtype), kind="ExternalInput").ap() for n, a in A.items()}
    out = nc.dram_tensor("out", (B, S, D), F32, kind="ExternalOutput").ap()
    build(nc, aps, out)
    return run_bass_kernel_spmd(nc, [{f"in_{n}": a for n, a in A.items()}], core_ids=[0]).results[0]["out"]
```

```python
import concourse.bass as bass
from concourse import mybir
from contextlib import ExitStack

F32 = mybir.dt.float32
F32R = mybir.dt.float32r
ALU = mybir.AluOpType
ACT = mybir.ActivationFunctionType
AX = mybir.AxisListType

B = 8
S = 128
D = 512
KT = D // 128
BANK = 512
LN_EPS = 1e-5
NEVER = -3.0e38


def blk(i, width):
    return bass.ds(i * width, width)


def wait_from_one(eng, sem, value):
    if not (isinstance(value, int) and value <= 0):
        eng.wait_ge(sem, value)


def in_pairs(eng, front, back):
    front(0, 0)
    front(1, 1)
    back(0, 0)
    with eng.Fori(0, B // 2 - 2) as pair:
        i = pair * 2 + 1
        for n in (0, 1):
            front(i + n + 1, n)
            back(i + n, 1 - n)
    for i in (B - 2, B - 1):
        front(i, i % 2)
        back(i - 1, (i - 1) % 2)
    back(B - 1, 1)


def one_by_one(eng, step):
    step(0)
    with eng.Fori(1, B - 1) as i:
        step(i)
    step(B - 1)


def matmul_split(pe, out, lhs, rhs, start, stop):
    (lhs_hi, lhs_lo), (rhs_hi, rhs_lo) = lhs, rhs
    pe.matmul(out, lhs_lo, rhs_hi, start=start, stop=False)
    pe.matmul(out, lhs_hi, rhs_lo, start=False, stop=False)
    return pe.matmul(out, lhs_hi, rhs_hi, start=False, stop=stop)


def matmul_tiles(pe, out, lhs_tiles, rhs_tiles):
    n = len(lhs_tiles)
    for k in range(n):
        last = matmul_split(pe, out, lhs_tiles[k], rhs_tiles[k], k == 0, k == n - 1)
    return last


def minus(eng, out_lo, value, hi):
    return eng.tensor_tensor(out_lo, value, hi.bitcast(F32), ALU.subtract)


class Phase:

    def __init__(self, nc, ctx, tag):
        self.nc, self.ctx, self.tag, self.used = nc, ctx, tag, []
        ctx.callback(self.clear)

    def clear(self):
        self.nc.clear_and_free_semaphores(self.used)
        self.nc.all_engine_barrier()

    def sb(self, name, cols, dt=F32, rows=128):
        return self.ctx.enter_context(self.nc.sbuf_tensor(f"{self.tag}_{name}", [rows, cols], dt))

    def split(self, name, cols, rows=128):
        return (self.sb(name + "_hi", cols, F32R, rows), self.sb(name + "_lo", cols, F32R, rows))

    def sem(self, name):
        self.used.append(self.nc.alloc_semaphore(name=f"{self.tag}_{name}"))
        return self.used[-1]

    def sems(self, names):
        return {n: self.sem(n) for n in names.split()}



NORM_SEMS = "stats moments veps rstd xn xnT xT_hi xT_lo"


class NormBuffers:
    def __init__(self, ph):
        self.stats, self.moments = ph.sb("stats", B * 6), ph.sb("moments", B * 2)
        self.veps, self.rstd = ph.sb("veps", B), ph.sb("rstd", B)
        self.xn = ph.sb("xn", D)


def moments_vector(dve, C, s, t):
    with dve.Fori(0, B) as i:
        dve.bn_stats(t.stats[:, blk(i, 6)], C.x[:, blk(i, D)]).then_inc(s["stats"], 1)
    dve.drain()
    for i in range(B):
        dve.bn_aggr(t.moments[:, 2 * i:2 * i + 2], t.stats[:, 6 * i:6 * i + 6]).then_inc(s["moments"], 1)
    dve.wait_ge(s["rstd"], 1)
    norm_vector(dve, C, s, t, 0)


def norm_vector(dve, C, s, t, i):
    wait_from_one(dve, s["xnT"], i)
    dve.tensor_scalar(t.xn[:, :], C.x[:, blk(i, D)], t.moments[:, blk(i * 2, 1)], t.rstd[:, blk(i, 1)], ALU.subtract,
                      ALU.mult).then_inc(s["xn"], 1)


def next_norm_vector(dve, C, s, t, i):
    if not (isinstance(i, int) and i == B - 1):
        norm_vector(dve, C, s, t, i + 1)


def norm_gpsimd(pool, C, s, t):
    pool.wait_ge(s["moments"], B)
    variance = t.moments[:, :].rearrange("p (b c) -> p b c", c=2)[:, :, 1]
    pool.tensor_tensor(t.veps[:, :], variance, C.ln_eps[:, 0:1].to_broadcast([128, B]), ALU.add).then_inc(s["veps"], 1)
    pool.wait_ge(s["veps"], 1)
    pool.tensor_tensor(t.rstd[:, :], t.veps[:, :], C.neg_half[:, 0:B], ALU.pow).then_inc(s["rstd"], 1)


def norm_tensor(pe, C, s, xn, bank, i):
    pe.wait_ge(s["xn"], i + 1)
    wait_from_one(pe, s["xT_lo"], i)
    for k in range(KT):
        last = pe.transpose(bank[:, k * 128:(k + 1) * 128], xn[:, k * 128:(k + 1) * 128], C.ident[:, :])
    last.then_inc(s["xnT"], 1)


def tiles_of(bank):
    return bank.rearrange("p (k t) -> p k t", k=KT)



def set_up(nc, C, x_dram):
    with ExitStack() as ctx:
        ph = Phase(nc, ctx, "setup")
        s = ph.sems("zeroed const loaded")
        block = ctx.enter_context(nc.Block())

        @block.sync
        def _(sp):
            with sp.Fori(0, B) as b:
                sp.dma_start(C.x[:, blk(b, D)], x_dram[bass.ds(b, 1)].rearrange("a p d -> p (a d)")).then_inc(s["loaded"], 16)
            sp.wait_ge(s["loaded"], 16 * B)

        @block.gpsimd
        def _(pool):
            pool.memset(C.ident[:, :], 0.0).then_inc(s["zeroed"], 1)
            pool.memset(C.neg_half[:, :], -0.5).then_inc(s["zeroed"], 1)
            pool.memset(C.ones[:, :], 1.0).then_inc(s["zeroed"], 1)
            pool.memset(C.ln_eps[:, :], LN_EPS).then_inc(s["zeroed"], 1)
            for e in range(8):
                pool.memset(C.falling[:, e:e + 1], float(8 - e)).then_inc(s["zeroed"], 1)
            pool.wait_ge(s["zeroed"], 12)
            pool.affine_select(out=C.ident[:, :], in_=C.ident[:, :], compare_op=ALU.not_equal, fill=1.0,
                               base=0, pattern=[[-1, 128]], channel_multiplier=1).then_inc(s["const"], 1)
            pool.wait_ge(s["const"], 1)



E = 8
R = 16
ER = E * R
GATE_HID = 32
CAPACITY = int(3.0 * B * S / E)
MEAN_FROM, MEAN_TO = 107, S - 1


def by_sequence(tile):
    return tile.rearrange("p (b c) -> p b c", b=B)


def along_last(v, n):
    return v.unsqueeze(2).to_broadcast([128, v.shape[1], n])


def along_sequences(v):
    return v.unsqueeze(1).to_broadcast([128, B, v.shape[1]])


def best_expert(link, dve, C, gates, onehot, best, rank):
    g3, o3 = by_sequence(gates), by_sequence(onehot)
    link(dve.tensor_reduce(best, g3, AX.X, ALU.max))
    link(dve.tensor_tensor(o3, g3, along_last(best, E), ALU.is_equal))
    link(dve.tensor_tensor(o3, o3, along_sequences(C.falling[:, :]), ALU.mult))
    link(dve.tensor_reduce(rank, o3, AX.X, ALU.max))
    link(dve.tensor_tensor(o3, o3, along_last(rank, E), ALU.is_equal))


class TopTwo:
    G = E
    N_ROWS = 0

    def __init__(self, ph, C, extra):
        self.C, self.extra = C, extra
        self.gates, self.first, self.second, self.rest = (
            ph.sb(n, B * E) for n in ("gates", "first", "second", "rest"))
        self.best, self.next, self.rank, self.share = (ph.sb(n, B) for n in ("best", "next", "rank", "share"))
        self.ratio = C.to_exp[:, 0:B]
        self.ahead, self.exped = ph.sem("ahead"), ph.sem("exped")
        self.route = self.first

    def load(self, sp, sem):
        pass

    def gpsimd(self, pool):
        pass

    def tensor(self, pe, bank):
        pass

    def scalar(self, act):
        act.wait_ge(self.ahead, 1)
        act.activation(self.ratio, self.ratio, ACT.Exp).then_inc(self.exped, 1)

    def pick(self, dve, link):
        best_expert(link, dve, self.C, self.gates[:, :], self.first[:, :], self.best[:, :], self.rank[:, :])
        link(dve.scalar_tensor_tensor(self.rest[:, :], self.first[:, :], NEVER, self.gates[:, :], ALU.mult, ALU.add))
        best_expert(link, dve, self.C, self.rest[:, :], self.second[:, :], self.next[:, :], self.rank[:, :])
        dve.tensor_tensor(self.ratio, self.next[:, :], self.best[:, :], ALU.subtract).then_inc(self.ahead, 1)
        dve.wait_ge(self.exped, 1)
        link(dve.tensor_scalar(self.share[:, :], self.ratio, 1.0, None, ALU.add))
        link(dve.reciprocal(self.share[:, :], self.share[:, :]))
        link(dve.tensor_tensor(self.ratio, self.ratio, self.share[:, :], ALU.mult))

    def weigh(self, dve, link):
        for onehot, w in ((self.first, self.share[:, :]), (self.second, self.ratio)):
            o3 = by_sequence(onehot[:, :])
            link(dve.tensor_tensor(o3, o3, along_last(w, E), ALU.mult))
        link(dve.tensor_tensor(self.first[:, :], self.first[:, :], self.second[:, :], ALU.add))

    def vector(self, dve, link, gate_out, bank, rows_loaded):
        link(dve.tensor_copy(by_sequence(self.gates[:, :]), gate_out))
        self.pick(dve, link)
        self.weigh(dve, link)


class GateNet(TopTwo):
    G = GATE_HID
    N_ROWS = 5

    def __init__(self, ph, C, extra):
        super().__init__(ph, C, extra)
        n = GATE_HID
        self.rows = [ph.sb(f"row{k}", w) for k, w in enumerate((n, n, n, E * n, E))]
        self.hid, self.dev = ph.sb("hid", B * n), ph.sb("dev", B * n)
        self.stat, self.inv = ph.sb("stat", B), ph.sb("inv", B)
        self.products = ph.sb("products", B * E * n)
        self.counts, self.allowed = ph.sb("counts", 2 * E), ph.sb("allowed", 2 * E)
        self.var, self.inverted, self.counted, self.summed = (
            ph.sem(n) for n in ("var", "inverted", "counted", "summed"))

    def load(self, sp, sem):
        for dst, src in zip(self.rows, self.extra):
            sp.dma_start(dst[:, :], src.partition_broadcast(128)).then_inc(sem, 16)

    def gpsimd(self, pool):
        pool.wait_ge(self.var, 1)
        pool.tensor_tensor(self.inv[:, :], self.stat[:, :], self.C.neg_half[:, 0:B], ALU.pow).then_inc(self.inverted, 1)

    def tensor(self, pe, bank):
        pe.wait_ge(self.counted, 1)
        pe.matmul(bank[:, 0:2 * E], self.C.ones[:, :], self.counts[:, :], start=True, stop=True).then_inc(self.summed, 1)

    def vector(self, dve, link, gate_out, bank, rows_loaded):
        b1, gamma, beta, w2, b2 = (r[:, :] for r in self.rows)
        hid, dev = by_sequence(self.hid[:, :]), by_sequence(self.dev[:, :])
        stat, n = self.stat[:, :], GATE_HID
        dve.wait_ge(rows_loaded, 16 * self.N_ROWS)
        link(dve.tensor_tensor(hid, gate_out, along_sequences(b1), ALU.add))
        link(dve.tensor_reduce(stat, hid, AX.X, ALU.add))
        link(dve.tensor_scalar(stat, stat, 1.0 / n, None, ALU.mult))
        link(dve.tensor_tensor(hid, hid, along_last(stat, n), ALU.subtract))
        link(dve.tensor_tensor(dev, hid, hid, ALU.mult))
        link(dve.tensor_reduce(stat, dev, AX.X, ALU.add))
        dve.tensor_scalar(stat, stat, 1.0 / n, LN_EPS, ALU.mult, ALU.add).then_inc(self.var, 1)
        dve.wait_ge(self.inverted, 1)
        link(dve.tensor_tensor(hid, hid, along_last(self.inv[:, :], n), ALU.mult))
        link(dve.tensor_tensor(hid, hid, along_sequences(gamma), ALU.mult))
        link(dve.tensor_tensor(hid, hid, along_sequences(beta), ALU.add))
        link(dve.tensor_scalar(self.hid[:, :], self.hid[:, :], 0.0, None, ALU.max))
        for b in range(B):
            p3 = self.products[:, b * E * n:(b + 1) * E * n].rearrange("p (e c) -> p e c", e=E)
            h3 = self.hid[:, b * n:(b + 1) * n].unsqueeze(1).to_broadcast([128, E, n])
            link(dve.tensor_tensor(p3, h3, w2.rearrange("p (e c) -> p e c", e=E), ALU.mult))
        link(dve.tensor_reduce(self.gates[:, :], self.products[:, :].rearrange("p (g c) -> p g c", c=n), AX.X, ALU.add))
        g3 = by_sequence(self.gates[:, :])
        link(dve.tensor_tensor(g3, g3, along_sequences(b2), ALU.add))
        self.pick(dve, link)
        link(dve.tensor_reduce(self.counts[:, 0:E], self.first[:, :].rearrange("p (b e) -> p e b", b=B), AX.X, ALU.add))
        dve.tensor_reduce(self.counts[:, E:2 * E], self.second[:, :].rearrange("p (b e) -> p e b", b=B), AX.X,
                          ALU.add).then_inc(self.counted, 1)
        dve.wait_ge(self.summed, 1)
        link(dve.tensor_scalar(self.allowed[:, :], bank[:, 0:2 * E], float(CAPACITY), None, ALU.is_le))
        for k, onehot in enumerate((self.first, self.second)):
            o3 = by_sequence(onehot[:, :])
            link(dve.tensor_tensor(o3, o3, along_sequences(self.allowed[:, k * E:(k + 1) * E]), ALU.mult))
        self.weigh(dve, link)


class MeanRoute:
    G = E
    N_ROWS = 1

    def __init__(self, ph, C, extra):
        self.C, self.extra = C, extra
        self.row, self.average = ph.sb("row", E), ph.sb("average", S)
        self.gates, self.route, self.most = ph.sb("gates", B * E), C.to_exp, ph.sb("most", B)
        self.masked, self.copied, self.averaged, self.below, self.exped = (
            ph.sem(n) for n in ("masked", "copied", "averaged", "below", "exped"))

    def load(self, sp, sem):
        sp.dma_start(self.row[:, :], self.extra[0].partition_broadcast(128)).then_inc(sem, 16)

    def gpsimd(self, pool):
        a = self.average[:, :]
        pool.memset(a, 1.0 / (MEAN_TO - MEAN_FROM)).then_inc(self.masked, 1)
        pool.wait_ge(self.masked, 1)
        pool.affine_select(out=a, in_=a, compare_op=ALU.is_ge, fill=0.0, base=-MEAN_FROM, pattern=[[0, S]],
                           channel_multiplier=1).then_inc(self.masked, 1)
        pool.wait_ge(self.masked, 2)
        pool.affine_select(out=a, in_=a, compare_op=ALU.is_ge, fill=0.0, base=MEAN_TO - 1, pattern=[[0, S]],
                           channel_multiplier=-1).then_inc(self.masked, 1)

    def tensor(self, pe, bank):
        pe.wait_ge(self.copied, 1)
        pe.wait_ge(self.masked, 3)
        pe.matmul(bank[:, 0:B * E], self.average[:, :], self.gates[:, :], start=True, stop=True).then_inc(self.averaged, 1)

    def scalar(self, act):
        act.wait_ge(self.below, 1)
        act.activation(self.route[:, :], self.route[:, :], ACT.Exp).then_inc(self.exped, 1)

    def vector(self, dve, link, gate_out, bank, rows_loaded):
        r3, most = by_sequence(self.route[:, :]), self.most[:, :]
        dve.tensor_copy(by_sequence(self.gates[:, :]), gate_out).then_inc(self.copied, 1)
        dve.wait_ge(rows_loaded, 16)
        dve.wait_ge(self.averaged, 1)
        link(dve.tensor_tensor(r3, by_sequence(bank[:, 0:B * E]), along_sequences(self.row[:, :]), ALU.add))
        link(dve.tensor_reduce(most, r3, AX.X, ALU.max))
        dve.tensor_tensor(r3, r3, along_last(most, E), ALU.subtract).then_inc(self.below, 1)
        dve.wait_ge(self.exped, 1)
        link(dve.tensor_reduce(most, r3, AX.X, ALU.add))
        link(dve.reciprocal(most, most))
        link(dve.tensor_tensor(r3, r3, along_last(most, E), ALU.mult))


def ffn_phase(nc, C, tag, Route, w_main, w_side, w_up, scale, bias=None, extra=None):
    SIDE = ER + Route.G
    with ExitStack() as ctx:
        ph = Phase(nc, ctx, tag)
        t = NormBuffers(ph)
        xT = [ph.split(f"xT{p}", D) for p in (0, 1)]
        raw = [ph.sb(n, c) for n, c in (("main_raw", KT * D), ("side_raw", KT * SIDE), ("up_raw", D))]
        main, side, up = (ph.split(n, c) for n, c in (("main", KT * D), ("side", KT * SIDE), ("up", D)))
        kept = ph.sb("kept", B * SIDE)
        bias_row = ph.sb("bias", D) if bias is not None else None
        routed, rT = ph.sb("routed", B * ER), ph.split("rT", B * S)
        s = ph.sems(NORM_SEMS + " loaded rows bias_loaded w_hi w_lo biased main_mm side_mm added kept"
                    " chain routed routedT rT_hi rT_lo up_mm summed_up")
        route = Route(ph, C, extra)
        bank_xT, bank_main, bank_side, bank_route = (C.ps[:, blk(k, BANK)] for k in range(4))
        bank_rT, bank_up = ([C.ps[:, blk(k + p, BANK)] for p in (0, 1)] for k in (4, 6))
        block = ctx.enter_context(nc.Block())

        def x_of(i):
            return C.x[:, blk(i, D)]

        def tiles(pair, n):
            return [tuple(h[:, k * n:(k + 1) * n] for h in pair) for k in range(KT)]

        @block.sync
        def _(sp):
            for dst, src in zip(raw, (w_main, w_side, w_up)):
                sp.dma_start(dst[:, :], src).then_inc(s["loaded"], 16)
            if bias is not None:
                sp.dma_start(bias_row[:, :], bias.partition_broadcast(128)).then_inc(s["bias_loaded"], 16)
            route.load(sp, s["rows"])

        @block.gpsimd
        def _(pool):
            norm_gpsimd(pool, C, s, t)
            if bias is not None:
                pool.wait_ge(s["bias_loaded"], 16)
                with pool.Fori(0, B) as i:
                    pool.wait_ge(s["xn"], i + 1)
                    pool.tensor_tensor(x_of(i), x_of(i), bias_row[:, :], ALU.add).then_inc(s["biased"], 1)
            route.gpsimd(pool)

        @block.tensor
        def _(pe):
            def front(i, p):
                norm_tensor(pe, C, s, t.xn[:, :], bank_xT, i)

            def back(i, p):
                lhs = tiles(xT[p], S)
                pe.wait_ge(s["xT_lo"], i + 1)
                wait_from_one(pe, s["added"], i)
                matmul_tiles(pe, bank_main, lhs, tiles(main, D)).then_inc(s["main_mm"], 1)
                wait_from_one(pe, s["kept"], i)
                matmul_tiles(pe, bank_side[:, 0:SIDE], lhs, tiles(side, SIDE)).then_inc(s["side_mm"], 1)
            pe.wait_ge(s["w_lo"], 3)
            in_pairs(pe, front, back)
            route.tensor(pe, bank_route)

            for h in (0, 1):
                pe.wait_ge(s["routed"], h + 1)
                for j in range(B // 2):
                    last = pe.transpose(bank_rT[h][:, j * S:(j + 1) * S], routed[:, (h * (B // 2) + j) * ER:][:, 0:ER],
                                        C.ident[:, :])
                last.then_inc(s["routedT"], 1)
            for i in range(B):
                if i % (B // 2) == 0:
                    pe.wait_ge(s["rT_lo"], i // (B // 2) + 1)
                wait_from_one(pe, s["summed_up"], i - 1)
                matmul_split(pe, bank_up[i % 2], tuple(x[:, i * S:(i + 1) * S] for x in rT),
                             (up[0][:, :], up[1][:, :]), True, True).then_inc(s["up_mm"], 1)

        @block.scalar
        def _(act):
            act.wait_ge(s["loaded"], 48)
            for r, pair in zip(raw, (main, side, up)):
                act.activation(pair[0][:, :], r[:, :], ACT.Copy).then_inc(s["w_hi"], 1)

            def front(i, p):
                act.wait_ge(s["xnT"], i + 1)
                wait_from_one(act, s["side_mm"], i - 1)
                act.activation(xT[p][0][:, :], bank_xT, ACT.Copy).then_inc(s["xT_hi"], 1)
            in_pairs(act, front, lambda i, p: None)
            route.scalar(act)

            for h in (0, 1):
                act.wait_ge(s["routedT"], h + 1)
                act.activation(rT[0][:, h * BANK:(h + 1) * BANK], bank_rT[h], ACT.Copy).then_inc(s["rT_hi"], 1)

        @block.vector
        def _(dve):
            n_link = [0]

            def link(ins):
                n_link[0] += 1
                ins.then_inc(s["chain"], 1)
                dve.wait_ge(s["chain"], n_link[0])

            moments_vector(dve, C, s, t)
            for n, (r, pair) in enumerate(zip(raw, (main, side, up))):
                dve.wait_ge(s["w_hi"], n + 1)
                minus(dve, pair[1][:, :], r[:, :], pair[0][:, :]).then_inc(s["w_lo"], 1)

            def front(i, p):
                dve.wait_ge(s["xT_hi"], i + 1)
                minus(dve, xT[p][1][:, :], bank_xT, xT[p][0][:, :]).then_inc(s["xT_lo"], 1)
                next_norm_vector(dve, C, s, t, i)

            def back(i, p):
                dve.wait_ge(s["main_mm"], i + 1)
                if bias is not None:
                    dve.wait_ge(s["biased"], i + 1)
                dve.tensor_tensor(x_of(i), x_of(i), bank_main, ALU.add).then_inc(s["added"], 1)
                dve.wait_ge(s["side_mm"], i + 1)
                dve.tensor_copy(kept[:, blk(i, SIDE)], bank_side[:, 0:SIDE]).then_inc(s["kept"], 1)
            in_pairs(dve, front, back)
            dve.wait_ge(s["kept"], B)
            dve.wait_ge(s["added"], B)
            route.vector(dve, link, by_sequence(kept[:, :])[:, :, ER:SIDE], bank_route, s["rows"])

            for h in (0, 1):
                part = slice(h * (B // 2), (h + 1) * (B // 2))
                dve.tensor_tensor(by_sequence(routed[:, :])[:, part].rearrange("p b (e r) -> p b e r", e=E),
                                  by_sequence(kept[:, :])[:, part, 0:ER].rearrange("p b (e r) -> p b e r", e=E),
                                  by_sequence(route.route[:, :])[:, part].unsqueeze(3).to_broadcast([128, B // 2, E, R]),
                                  ALU.mult).then_inc(s["routed"], 1)
            for h in (0, 1):
                at = slice(h * BANK, (h + 1) * BANK)
                dve.wait_ge(s["rT_hi"], h + 1)
                minus(dve, rT[1][:, at], bank_rT[h], rT[0][:, at]).then_inc(s["rT_lo"], 1)
            for i in range(B):
                dve.wait_ge(s["up_mm"], i + 1)
                dve.scalar_tensor_tensor(x_of(i), bank_up[i % 2], scale, x_of(i), ALU.mult, ALU.add).then_inc(s["summed_up"], 1)



HQ = 4
HD = 128
GROUPS = 8
UNIT = 4
CHUNK = KT * HD
QK_EPS = 1e-5


def context_transposed(nc, C, cT_dram):
    with ExitStack() as ctx:
        ph = Phase(nc, ctx, "cT")
        raw = ph.sb("raw", KT * B * S)
        s = ph.sems("loaded hi lo")
        block = ctx.enter_context(nc.Block())

        @block.sync
        def _(sp):
            for k in range(KT):
                sp.dma_start(raw[:, blk(k, B * S)], cT_dram[:, blk(k, B * S)]).then_inc(s["loaded"], 16)
                sp.wait_ge(s["loaded"], 16 * (k + 1))

        @block.scalar
        def _(act):
            for k in range(KT):
                act.wait_ge(s["loaded"], 16 * (k + 1))
                act.activation(C.cT[0][:, blk(k, B * S)], raw[:, blk(k, B * S)], ACT.Copy).then_inc(s["hi"], 1)

        @block.vector
        def _(dve):
            for k in range(KT):
                dve.wait_ge(s["hi"], k + 1)
                minus(dve, C.cT[1][:, blk(k, B * S)], raw[:, blk(k, B * S)], C.cT[0][:, blk(k, B * S)]).then_inc(s["lo"], 1)


def norm_all(nc, C, tag, xT, bias=None):
    with ExitStack() as ctx:
        ph = Phase(nc, ctx, tag)
        t = NormBuffers(ph)
        s = ph.sems(NORM_SEMS + " bias_loaded biased")
        bias_row = ph.sb("bias", D) if bias is not None else None
        bank = C.ps[:, 0:BANK]
        block = ctx.enter_context(nc.Block())

        def xT_of(half, i):
            return half[:, :].rearrange("p (k t) -> p k t", k=KT)[:, :, blk(i, S)]

        @block.sync
        def _(sp):
            if bias is not None:
                sp.dma_start(bias_row[:, :], bias.partition_broadcast(128)).then_inc(s["bias_loaded"], 16)

        @block.gpsimd
        def _(pool):
            norm_gpsimd(pool, C, s, t)
            if bias is not None:
                pool.wait_ge(s["bias_loaded"], 16)
                with pool.Fori(0, B) as i:
                    pool.wait_ge(s["xn"], i + 1)
                    pool.tensor_tensor(C.x[:, blk(i, D)], C.x[:, blk(i, D)], bias_row[:, :], ALU.add).then_inc(s["biased"], 1)

        @block.tensor
        def _(pe):
            one_by_one(pe, lambda i: norm_tensor(pe, C, s, t.xn[:, :], bank, i))

        @block.scalar
        def _(act):
            def step(i):
                act.wait_ge(s["xnT"], i + 1)
                act.activation(xT_of(xT[0], i), tiles_of(bank), ACT.Copy).then_inc(s["xT_hi"], 1)
            one_by_one(act, step)

        @block.vector
        def _(dve):
            def step(i):
                next_norm_vector(dve, C, s, t, i)
                dve.wait_ge(s["xT_hi"], i + 1)
                minus(dve, xT_of(xT[1], i), tiles_of(bank), xT_of(xT[0], i)).then_inc(s["xT_lo"], 1)
            moments_vector(dve, C, s, t)
            one_by_one(dve, step)


def attention_phase(nc, C, tag, wkv, wq, wo, q_norm=None, k_norm=None, mask=None, bq=None, bk=None, bv=None, bo=None):
    normed = q_norm is not None
    with ExitStack() as ctx:
        ph = Phase(nc, ctx, tag)
        xT = ph.split("xT", KT * B * S)
        norm_all(nc, C, tag + "n", xT, bo)
        raw = [ph.sb(f"raw{k}", CHUNK) for k in (0, 1)]
        wk_s, wq_s = ph.split("wk", CHUNK), ph.split("wq", HQ * CHUNK)
        wv_s, wo_s = ph.split("wv", 2 * CHUNK), ph.split("wo", 2 * HQ * D)
        kT, qT = [ph.split(f"kT{p}", UNIT * S) for p in (0, 1)], [ph.split(f"qT{p}", HQ * UNIT * S) for p in (0, 1)]
        v_s = [ph.split(f"v{p}", HD) for p in (0, 1)]
        probs, pT, oT = ph.sb("probs", HQ * S), ph.split("pT", HQ * S), ph.split("oT", HQ * S)
        neg_max, total = ph.sb("neg_max", HQ), ph.sb("total", HQ)
        s = ph.sems("raw_in0 raw_in1 chunk_hi wo_hi split0 split1 columns k_mm k_hi k_lo kn q_mm q32 q_hi q_lo v_mm v_hi v_lo"
                    " s_mm raw_max neg_max exped inverse probs pT_mm pT_hi pT_lo av_mm o32 oT_hi oT_lo o_mm added")
        kn = ph.sb("kn", UNIT * S)
        if normed:
            squares, k_squares = ph.sb("squares", UNIT * S), ph.sb("k_squares", UNIT * S)
            k_scale, k_diagonal = ph.sb("k_scale", UNIT), k_squares
            mask_t, weight, q_col, eps = ph.sb("mask", S), ph.sb("weight", 1), ph.sb("q_col", 1), ph.sb("eps", 1)
            q_scale = [ph.sb(f"q_scale{p}", HQ * UNIT) for p in (0, 1)]
            sn = ph.sems("weight eps squares qs_mm q_eps q_scale k_squares k_copied k_eps k_scale k_diagonal kb_mm masked")
        else:
            q32, o32 = ph.sb("q32", UNIT * S), ph.sb("o32", HQ * S)
            bq_cols, bk_cols, bv_cols = ph.sb("bq_cols", GROUPS * HQ), ph.sb("bk_cols", GROUPS), ph.sb("bv_cols", GROUPS)
        bank_k, bank_q, bank_v, bank_s0, bank_s1, bank_pT, bank_o, bank_out = (C.ps[:, blk(k, BANK)] for k in range(8))
        bank_s = (bank_s0, bank_s1)
        q_sums, k_sums = bank_v[:, 2 * HD:2 * HD + UNIT], bank_v[:, 2 * HD + UNIT:2 * HD + 2 * UNIT]
        SCALE = HD ** -0.5
        KEYS_AT = 2
        block = ctx.enter_context(nc.Block())

        def head(tile, h, width=128):
            return tile[:, h * width:(h + 1) * width]

        def heads(tile):
            return tile.rearrange("p (h c) -> p h c", h=HQ)

        def ahead(g, b, n):
            return (g + (b + n) // B, (b + n) % B)

        def number(g, b):
            return g * B + b

        def steps(eng, step):
            for b in range(B):
                step(0, b)
            with eng.Fori(1, GROUPS - 2) as g:
                for b in range(B):
                    step(g, b)
            for g in (GROUPS - 2, GROUPS - 1):
                for b in range(B):
                    step(g, b)

        def exists(g):
            return not (isinstance(g, int) and g >= GROUPS)

        V_CHUNK, K_CHUNK, Q_CHUNK, O_CHUNK, CHUNKS = 0, 1, 2, 6, 10

        def nth(g, c):
            return g * (CHUNKS // 2) + c // 2 + 1

        def chunk_in(eng, g, c):
            eng.wait_ge(s[f"raw_in{c % 2}"], 16 * nth(g, c))

        def chunk_split(eng, g, c):
            eng.wait_ge(s[f"split{c % 2}"], nth(g, c))

        @block.sync
        def _(sp):
            def load_chunk(g, c):
                wait_from_one(sp, s[f"split{c % 2}"], nth(g, c) - 1)
                src = (wkv[bass.ds(g, 1), c] if c < Q_CHUNK else wq[bass.ds(g, 1), c - Q_CHUNK] if c < O_CHUNK
                       else wo[bass.ds(g, 1), c - O_CHUNK])
                sp.dma_start(raw[c % 2][:, :], src.rearrange("a p c -> p (a c)")).then_inc(s[f"raw_in{c % 2}"], 16)

            if normed:
                sp.dma_start(weight[:, :], k_norm).then_inc(s["columns"], 16)
                sp.dma_start(q_col[:, :], q_norm).then_inc(s["columns"], 16)
                sp.dma_start(mask_t[:, :], mask).then_inc(s["columns"], 16)
            else:
                for dst, src in ((bq_cols, bq), (bk_cols, bk), (bv_cols, bv)):
                    sp.dma_start(dst[:, :], src).then_inc(s["columns"], 16)
            for g in range(GROUPS):
                for c in range(CHUNKS):
                    load_chunk(g, c)

        @block.gpsimd
        def _(pool):
            if normed:
                pool.memset(eps[:, :], HD * QK_EPS).then_inc(sn["eps"], 1)
                pool.wait_ge(sn["eps"], 1)

            def split_chunk(g, c):
                pair, at = ((wv_s, (g % 2) * CHUNK) if c == V_CHUNK else (wk_s, 0) if c == K_CHUNK
                            else (wq_s, (c - Q_CHUNK) * CHUNK))
                hi, lo = (h[:, bass.ds(at, CHUNK)] for h in pair)
                chunk_in(pool, g, c)
                pool.tensor_tensor(hi, raw[c % 2][:, :], C.ones[:, 0:1].to_broadcast([128, CHUNK]), ALU.mult).then_inc(s["chunk_hi"], 1)
                pool.wait_ge(s["chunk_hi"], O_CHUNK * g + c + 1)
                minus(pool, lo, raw[c % 2][:, :], hi).then_inc(s[f"split{c % 2}"], 1)

            def normalise(t):
                pool.wait_ge(s["inverse"], t + 1)
                pool.tensor_tensor(heads(probs[:, :]), heads(probs[:, :]), along_last(total[:, :], S), ALU.mult).then_inc(s["probs"], 1)

            def query_scale(P, unit, h):
                pool.wait_ge(sn["q_eps"], P + 1)
                out = q_scale[unit][:, h * UNIT:(h + 1) * UNIT]
                pool.tensor_tensor(out, out, C.neg_half[:, 0:UNIT], ALU.pow).then_inc(sn["q_scale"], 1)

            def key_scale(u):
                pool.wait_ge(sn["k_eps"], u + 1)
                pool.tensor_tensor(k_scale[:, :], k_scale[:, :], C.neg_half[:, 0:UNIT], ALU.pow).then_inc(sn["k_scale"], 1)
            if normed:
                for P in range(UNIT):
                    query_scale(P, 0, P)
                    if P == 0:
                        key_scale(0)
            normalise(0)
            split_chunk(1, V_CHUNK)
            pool.wait_ge(s["q_mm"], UNIT + 1)
            split_chunk(1, K_CHUNK)
            split_chunk(1, Q_CHUNK)

            def step(g, b):
                t = number(g, b)
                gp, bp = ahead(g, b, 5)
                if normed and exists(ahead(g, b, 4)[0]):
                    query_scale(t + 4, (b + 4) // UNIT % 2, (b + 4) % UNIT)
                    if (b + 4) % UNIT == 0:
                        key_scale(g * 2 + (b + 4) // UNIT)
                if exists(gp + 1):
                    if bp == 3:
                        pool.wait_ge(s["v_mm"], t + 2)
                        split_chunk(gp + 1, V_CHUNK)
                    if bp == 4:
                        pool.wait_ge(s["q_mm"], t + 6)
                        split_chunk(gp + 1, K_CHUNK)
                    if bp >= 4:
                        pool.wait_ge(s["q_mm"], t + 6)
                        split_chunk(gp + 1, Q_CHUNK + bp - 4)
                if exists(ahead(g, b, 1)[0]):
                    normalise(t + 1)
            steps(pool, step)

        @block.tensor
        def _(pe):
            def project(P, g, b):
                unit, h = b // UNIT, b % UNIT
                if h == 0:
                    if b == 0:
                        chunk_split(pe, g, K_CHUNK)
                    wait_from_one(pe, s["kn"], g * 2 + unit)
                    matmul_tiles(pe, bank_k, [tuple(head(x, k) for x in wk_s) for k in range(KT)],
                                 tokens(C.cT, unit)).then_inc(s["k_mm"], 1)
                if unit == 0:
                    chunk_split(pe, g, Q_CHUNK + h)
                wait_from_one(pe, s["q_lo"], P)
                matmul_tiles(pe, bank_q, [tuple(head(x, h * KT + k) for x in wq_s) for k in range(KT)],
                             tokens(xT, unit)).then_inc(s["q_mm"], 1)

            def tokens(pair, unit):
                return [tuple(x[:, k * B * S + unit * UNIT * S:k * B * S + (unit + 1) * UNIT * S] for x in pair) for k in range(KT)]

            def sums(P, g, b, n_v):
                pe.wait_ge(sn["squares"], P + 1)
                wait_from_one(pe, sn["q_eps"], P)
                wait_from_one(pe, s["v_lo"], n_v)
                for j in range(UNIT):
                    last = pe.matmul(q_sums[:, j:j + 1], head(squares, j), C.ones[:, 0:1], start=True, stop=True)
                if b % UNIT == 0:
                    pe.wait_ge(sn["k_squares"], g * 2 + b // UNIT + 1)
                    for j in range(UNIT):
                        last = pe.matmul(k_sums[:, j:j + 1], head(k_squares, j), C.ones[:, 0:1], start=True, stop=True)
                last.then_inc(sn["qs_mm"], 1)
                if b % UNIT == 1:
                    pe.wait_ge(sn["k_diagonal"], g * 2 + b // UNIT + 1)
                    pe.wait_ge(sn["k_copied"], g * 2 + b // UNIT + 1)
                    pe.matmul(bank_k, C.ones[:, :], k_diagonal[:, :], start=True, stop=True).then_inc(sn["kb_mm"], 1)

            def scores(t, g, b):
                unit, j = b // UNIT, b % UNIT
                if j == 0:
                    pe.wait_ge(s["k_lo"], g * 2 + unit + 1)
                    pe.wait_ge(s["q_lo"], UNIT * (g * 2 + unit + 1))
                wait_from_one(pe, sn["masked"] if normed else s["exped"], HQ * (t - 1))
                for h in range(HQ):
                    last = matmul_split(pe, head(bank_s[b % 2], h), tuple(head(x, h * UNIT + j) for x in qT[unit]),
                                        tuple(head(x, j) for x in kT[unit]), True, True)
                last.then_inc(s["s_mm"], 1)

            def values(t, g, b):
                if b == 0:
                    chunk_split(pe, g, V_CHUNK)
                wait_from_one(pe, s["v_lo"], t)
                if normed and exists(ahead(g, b, 3)[0]):
                    wait_from_one(pe, sn["q_eps"], t + UNIT)
                turn = g % 2 if isinstance(g, int) else pe.snap(g % 2)
                matmul_tiles(pe, bank_v[:, 0:HD], [tuple(x[:, k * B * S + b * S:k * B * S + (b + 1) * S] for x in C.cT)
                                                   for k in range(KT)],
                             [tuple(x[:, bass.ds(turn * CHUNK + k * HD, HD)] for x in wv_s) for k in range(KT)])\
                    .then_inc(s["v_mm"], 1)

            def project_out(t, g, b):
                pe.wait_ge(s["oT_lo"], t + 1)
                if b == 0:
                    for h in (HQ - 2, HQ - 1):
                        chunk_split(pe, g, O_CHUNK + h)
                wait_from_one(pe, s["added"], t)
                turn = g % 2 if isinstance(g, int) else pe.snap(g % 2)
                matmul_tiles(pe, bank_out, [tuple(head(x, h) for x in oT) for h in range(HQ)],
                             [tuple(x[:, bass.ds(turn * (HQ * D) + h * D, D)] for x in wo_s) for h in range(HQ)])\
                    .then_inc(s["o_mm"], 1)
            for P in range(UNIT + 1):
                project(P, 0, P)
                if normed and P < UNIT:
                    sums(P, 0, P, 0)
            scores(0, 0, 0)
            values(0, 0, 0)
            if normed:
                sums(UNIT, 0, UNIT, 1)

            def step(g, b):
                t = number(g, b)
                next_item, piece = ahead(g, b, 1), ahead(g, b, 5)
                if exists(next_item[0]):
                    scores(t + 1, *next_item)
                if exists(piece[0]):
                    project(t + 5, *piece)
                pe.wait_ge(s["probs"], t + 1)
                wait_from_one(pe, s["pT_lo"], t)
                for h in range(HQ):
                    last = pe.transpose(head(bank_pT, h), head(probs, h), C.ident[:, :])
                last.then_inc(s["pT_mm"], 1)
                if exists(next_item[0]):
                    values(t + 1, *next_item)
                if not (isinstance(t, int) and t == 0):
                    project_out(t - 1, *ahead(g, b, -1))
                pe.wait_ge(s["pT_lo"], t + 1)
                pe.wait_ge(s["v_lo"], t + 1)
                wait_from_one(pe, s["oT_lo"], t)
                matmul_split(pe, bank_o, tuple(x[:, :] for x in v_s[b % 2]), tuple(x[:, :] for x in pT),
                             True, True).then_inc(s["av_mm"], 1)
                if normed and exists(piece[0]):
                    sums(t + 5, *piece, t + 2)
            steps(pe, step)
            project_out(GROUPS * B - 1, GROUPS - 1, B - 1)

        @block.scalar
        def _(act):
            def split_first(c):
                chunk_in(act, 0, c)
                hi = wv_s[0] if c == V_CHUNK else wk_s[0] if c == K_CHUNK else wq_s[0][:, (c - Q_CHUNK) * CHUNK:(c - Q_CHUNK + 1) * CHUNK]
                act.activation(hi[:, 0:CHUNK], raw[c % 2][:, :], ACT.Copy).then_inc(s["chunk_hi"], 1)

            def split_wo(g, h):
                chunk_in(act, g, O_CHUNK + h)
                wait_from_one(act, s["o_mm"], B * (g - 1))
                hi = wo_s[0][:, bass.ds((g % 2) * (HQ * D) + h * D, D)]
                act.activation(hi, raw[h % 2][:, :], ACT.Copy).then_inc(s["wo_hi"], 1)

            def keys(u):
                if normed:
                    act.wait_ge(s["k_mm"], u + 1)
                    wait_from_one(act, s["kn"], u)
                    act.activation(k_squares[:, :], bank_k, ACT.Square).then_inc(sn["k_squares"], 1)

            def split_keys(u, unit):
                act.wait_ge(s["kn"], u + 1)
                wait_from_one(act, s["s_mm"], UNIT * (u - 1))
                act.activation(kT[unit][0][:, :], kn[:, :], ACT.Copy).then_inc(s["k_hi"], 1)

            def queries(P, g, b):
                unit, h = b // UNIT, b % UNIT
                act.wait_ge(s["q_mm"] if normed else s["q32"], P + 1)
                if h == 0:
                    wait_from_one(act, s["s_mm"], UNIT * (g * 2 + unit - 1))
                out = head(qT[unit][0], h, UNIT * S)
                if normed:
                    act.activation(out, bank_q, ACT.Copy).then_inc(s["q_hi"], 1)
                    wait_from_one(act, sn["qs_mm"], P)
                    act.activation(squares[:, :], bank_q, ACT.Square).then_inc(sn["squares"], 1)
                else:
                    act.activation(out, q32[:, :], ACT.Copy).then_inc(s["q_hi"], 1)

            def exps(t, b):
                act.wait_ge(s["neg_max"], t + 1)
                if not normed:
                    wait_from_one(act, s["pT_mm"], t)
                src = probs if normed else bank_s[b % 2]
                for h in range(HQ):
                    act.activation(head(probs, h), head(src, h), ACT.Exp, bias=neg_max[:, h:h + 1],
                                   scale=1.0 if normed else SCALE, accum_out=total[:, h:h + 1]).then_inc(s["exped"], 1)

            def split_v(t, b):
                act.wait_ge(s["v_mm"], t + 1)
                wait_from_one(act, s["av_mm"], t - 1)
                act.activation(v_s[b % 2][0][:, :], bank_v[:, 0:HD], ACT.Copy).then_inc(s["v_hi"], 1)

            def split_oT(t):
                act.wait_ge(s["av_mm"] if normed else s["o32"], t + 1)
                wait_from_one(act, s["o_mm"], t)
                act.activation(oT[0][:, :], bank_o if normed else o32[:, :], ACT.Copy).then_inc(s["oT_hi"], 1)
            for c in range(O_CHUNK):
                split_first(c)
                if c >= Q_CHUNK:
                    P = c - Q_CHUNK
                    if P == 0:
                        keys(0)
                    queries(P, 0, P)
                    if P == KEYS_AT:
                        split_keys(0, 0)
            keys(1)
            queries(UNIT, 0, UNIT)
            for h in range(HQ):
                split_wo(0, h)
            split_v(0, 0)
            exps(0, 0)

            def step(g, b):
                t = number(g, b)
                gp, bp = piece = ahead(g, b, 5)
                if not (isinstance(t, int) and t == 0):
                    split_oT(t - 1)
                if exists(gp):
                    u = gp * 2 + bp // UNIT
                    if bp % UNIT == 0:
                        keys(u)
                    if bp % UNIT == KEYS_AT:
                        split_keys(u, bp // UNIT)
                    queries(t + 5, gp, bp)
                act.wait_ge(s["pT_mm"], t + 1)
                wait_from_one(act, s["av_mm"], t)
                act.activation(pT[0][:, :], bank_pT, ACT.Copy).then_inc(s["pT_hi"], 1)
                if exists(ahead(g, b, 1)[0]):
                    split_v(t + 1, (b + 1) % B)
                    exps(t + 1, (b + 1) % B)
                if 3 <= b < 3 + HQ and exists(g + 1):
                    split_wo(g + 1, b - 3)
            steps(act, step)
            split_oT(GROUPS * B - 1)

        @block.vector
        def _(dve):
            def split_first(c):
                dve.wait_ge(s["chunk_hi"], c + 1)
                at = (c - Q_CHUNK) * CHUNK if c >= Q_CHUNK else 0
                hi, lo = (x[:, at:at + CHUNK] for x in (wv_s if c == V_CHUNK else wk_s if c == K_CHUNK else wq_s))
                minus(dve, lo, raw[c % 2][:, :], hi).then_inc(s[f"split{c % 2}"], 1)

            def split_wo(g, h):
                dve.wait_ge(s["wo_hi"], HQ * g + h + 1)
                hi, lo = (x[:, bass.ds((g % 2) * (HQ * D) + h * D, D)] for x in wo_s)
                minus(dve, lo, raw[h % 2][:, :], hi).then_inc(s[f"split{h % 2}"], 1)

            def keys(u, g, b):
                if normed:
                    dve.wait_ge(sn["k_squares"], u + 1)
                    wait_from_one(dve, s["k_lo"], u)
                    dve.tensor_copy(kn[:, :], bank_k).then_inc(sn["k_copied"], 1)
                else:
                    dve.wait_ge(s["k_mm"], u + 1)
                    wait_from_one(dve, s["k_lo"], u)
                    dve.tensor_scalar(kn[:, :], bank_k, bk_cols[:, bass.ds(g, 1)], None, ALU.add).then_inc(s["kn"], 1)

            def key_eps(u):
                dve.wait_ge(sn["qs_mm"], UNIT * u + 1)
                dve.tensor_scalar(k_scale[:, :], k_sums, HD * QK_EPS, None, ALU.add).then_inc(sn["k_eps"], 1)

            def key_diagonal(u):
                dve.wait_ge(sn["k_scale"], u + 1)
                dve.tensor_tensor(k_diagonal[:, :].rearrange("p (j t) -> p j t", j=UNIT), along_last(k_scale[:, :], S),
                                  C.ident[:, :].unsqueeze(1).to_broadcast([128, UNIT, S]), ALU.mult).then_inc(sn["k_diagonal"], 1)

            def scale_keys(u):
                dve.wait_ge(sn["kb_mm"], u + 1)
                dve.wait_ge(sn["k_copied"], u + 1)
                dve.scalar_tensor_tensor(kn[:, :], kn[:, :], weight[:, 0:1], bank_k, ALU.mult, ALU.mult).then_inc(s["kn"], 1)

            def split_keys(u, unit):
                dve.wait_ge(s["k_hi"], u + 1)
                minus(dve, kT[unit][1][:, :], kn[:, :], kT[unit][0][:, :]).then_inc(s["k_lo"], 1)

            def queries(P, g, b):
                unit, h = b // UNIT, b % UNIT
                hi, lo = (head(x, h, UNIT * S) for x in qT[unit])
                if normed:
                    dve.wait_ge(sn["squares"], P + 1)
                    minus(dve, lo, bank_q, hi).then_inc(s["q_lo"], 1)
                else:
                    dve.wait_ge(s["q_hi"], P + 1)
                    minus(dve, lo, q32[:, :], hi).then_inc(s["q_lo"], 1)

            def bias_queries(P, g, h):
                dve.wait_ge(s["q_mm"], P + 1)
                wait_from_one(dve, s["q_lo"], P)
                dve.tensor_scalar(q32[:, :], bank_q, bq_cols[:, bass.ds(g * HQ + h, 1)], None, ALU.add).then_inc(s["q32"], 1)

            def query_eps(P, g, b):
                unit, h = b // UNIT, b % UNIT
                dve.wait_ge(sn["qs_mm"], P + 1)
                if h == 0:
                    wait_from_one(dve, sn["masked"], HQ * UNIT * (g * 2 + unit - 1))
                dve.tensor_scalar(q_scale[unit][:, h * UNIT:(h + 1) * UNIT], q_sums, HD * QK_EPS, None, ALU.add).then_inc(sn["q_eps"], 1)

            def add_mask(t, b):
                unit, j = b // UNIT, b % UNIT
                dve.wait_ge(s["s_mm"], t + 1)
                if j == 0:
                    pieces = t + UNIT
                    dve.wait_ge(sn["q_scale"], pieces)
                wait_from_one(dve, s["pT_mm"], t)
                for h in range(HQ):
                    at = h * UNIT + j
                    dve.scalar_tensor_tensor(head(probs, h), head(bank_s[b % 2], h), q_scale[unit][:, at:at + 1], mask_t[:, :],
                                             ALU.mult, ALU.add).then_inc(sn["masked"], 1)

            def maximum(t, b):
                wait_from_one(dve, s["exped"], HQ * t)
                if normed:
                    dve.wait_ge(sn["masked"], HQ * (t + 1))
                    dve.tensor_reduce(neg_max[:, :], heads(probs[:, :]), AX.X, ALU.max, negate=True).then_inc(s["neg_max"], 1)
                else:
                    dve.wait_ge(s["s_mm"], t + 1)
                    dve.tensor_reduce(neg_max[:, :], heads(bank_s[b % 2]), AX.X, ALU.max).then_inc(s["raw_max"], 1)
                    dve.wait_ge(s["raw_max"], t + 1)
                    dve.tensor_scalar(neg_max[:, :], neg_max[:, :], -SCALE, None, ALU.mult).then_inc(s["neg_max"], 1)

            def invert(t):
                dve.wait_ge(s["exped"], HQ * (t + 1))
                dve.reciprocal(total[:, :], total[:, :]).then_inc(s["inverse"], 1)

            def split_v(t, b):
                dve.wait_ge(s["v_hi"], t + 1)
                minus(dve, v_s[b % 2][1][:, :], bank_v[:, 0:HD], v_s[b % 2][0][:, :]).then_inc(s["v_lo"], 1)

            def split_oT(t):
                dve.wait_ge(s["oT_hi"], t + 1)
                minus(dve, oT[1][:, :], bank_o if normed else o32[:, :], oT[0][:, :]).then_inc(s["oT_lo"], 1)

            def bias_out(t, g):
                dve.wait_ge(s["av_mm"], t + 1)
                wait_from_one(dve, s["oT_lo"], t)
                dve.tensor_scalar(o32[:, :], bank_o, bv_cols[:, bass.ds(g, 1)], None, ALU.add).then_inc(s["o32"], 1)

            def add_out(t, b):
                dve.wait_ge(s["o_mm"], t + 1)
                x_b = C.x[:, blk(b, D)]
                dve.tensor_tensor(x_b, x_b, bank_out, ALU.add).then_inc(s["added"], 1)
            dve.wait_ge(s["columns"], 48)
            if normed:
                dve.scalar_tensor_tensor(weight[:, :], weight[:, :], HD ** 0.5, q_col[:, :], ALU.mult, ALU.mult).then_inc(sn["weight"], 1)
                dve.wait_ge(sn["weight"], 1)
            for c in range(O_CHUNK):
                split_first(c)
                if c >= Q_CHUNK:
                    P = c - Q_CHUNK
                    if P == 0:
                        keys(0, 0, 0)
                    if not normed:
                        bias_queries(P, 0, P)
                    queries(P, 0, P)
                    if P == KEYS_AT and not normed:
                        split_keys(0, 0)
                    if normed:
                        if P == 0:
                            key_eps(0)
                        query_eps(P, 0, P)
                        if P == 1:
                            key_diagonal(0)
                        if P == KEYS_AT:
                            scale_keys(0)
                            split_keys(0, 0)
            keys(1, 0, UNIT)
            if not normed:
                bias_queries(UNIT, 0, 0)
            queries(UNIT, 0, UNIT)
            for h in range(HQ):
                split_wo(0, h)
            if normed:
                add_mask(0, 0)
            maximum(0, 0)
            split_v(0, 0)
            invert(0)

            def step(g, b):
                t = number(g, b)
                gp, bp = ahead(g, b, 5)
                u = gp * 2 + bp // UNIT
                before = ahead(g, b, 4)
                if not (isinstance(t, int) and t == 0):
                    if not normed:
                        bias_out(t - 1, ahead(g, b, -1)[0])
                    split_oT(t - 1)
                if normed and exists(before[0]):
                    if before[1] % UNIT == 0:
                        key_eps(before[0] * 2 + before[1] // UNIT)
                    query_eps(t + 4, *before)
                if exists(gp):
                    if bp % UNIT == 0:
                        keys(u, gp, bp)
                    if normed and bp % UNIT == 2:
                        scale_keys(u)
                    if not normed:
                        bias_queries(t + 5, gp, bp % UNIT)
                    queries(t + 5, gp, bp)
                    if normed and bp % UNIT == 1:
                        key_diagonal(u)
                    if bp % UNIT == KEYS_AT:
                        split_keys(u, bp // UNIT)
                more = exists(ahead(g, b, 1)[0])
                if normed and more:
                    add_mask(t + 1, (b + 1) % B)
                if not normed and more:
                    maximum(t + 1, (b + 1) % B)
                dve.wait_ge(s["pT_hi"], t + 1)
                minus(dve, pT[1][:, :], bank_pT, pT[0][:, :]).then_inc(s["pT_lo"], 1)
                if more:
                    split_v(t + 1, (b + 1) % B)
                    if normed:
                        maximum(t + 1, (b + 1) % B)
                    invert(t + 1)
                if not (isinstance(t, int) and t == 0):
                    add_out(t - 1, (b - 1) % B)
                if 3 <= b < 3 + HQ and exists(g + 1):
                    split_wo(g + 1, b - 3)
            steps(dve, step)
            if not normed:
                bias_out(GROUPS * B - 1, GROUPS - 1)
            split_oT(GROUPS * B - 1)
            add_out(GROUPS * B - 1, B - 1)



HD0 = 16
KV0 = 8
SETS = 4
ROUNDS = KV0 // 2
RH = 2 * SETS
RW = RH * S


def project_small_heads(nc, C, q32, k32, v32, wkv, wq, bk, bq, bv, bo):
    with ExitStack() as ctx:
        ph = Phase(nc, ctx, "p0")
        xT = ph.split("xT", KT * B * S)
        norm_all(nc, C, "p0n", xT, bo)
        raw, w_s = ph.sb("raw", (2 + SETS) * CHUNK), ph.split("w", (2 + SETS) * CHUNK)
        bk_col, bq_cols, bv_row = ph.sb("bk", 1), ph.sb("bq", SETS), ph.sb("bv", S)
        s = ph.sems("w_in bias_in w_hi w_lo mm taken")
        banks = [C.ps[:, blk(k, BANK)] for k in range(4)]
        block = ctx.enter_context(nc.Block())
        K_CHUNK, V_CHUNK, Q_CHUNK = 0, 1, 2
        products = [(K_CHUNK, h) for h in (0, 1)] + [(V_CHUNK, b) for b in range(B)] + \
            [(Q_CHUNK + n, h) for n in range(SETS) for h in (0, 1)]

        def chunk(tile, c):
            return tile[:, c * CHUNK:(c + 1) * CHUNK]

        @block.sync
        def _(sp):
            for c in range(2 + SETS):
                src = wkv[c] if c < Q_CHUNK else wq[c - Q_CHUNK]
                sp.dma_start(chunk(raw, c), src).then_inc(s["w_in"], 16)
                sp.wait_ge(s["w_in"], 16 * (c + 1))
                if c == 0:
                    sp.dma_start(bk_col[:, :], bk).then_inc(s["bias_in"], 16)
                    sp.dma_start(bq_cols[:, :], bq).then_inc(s["bias_in"], 16)
                    sp.dma_start(bv_row[:, :], bv.partition_broadcast(128)).then_inc(s["bias_in"], 16)

        @block.scalar
        def _(act):
            for c in range(2 + SETS):
                act.wait_ge(s["w_in"], 16 * (c + 1))
                act.activation(chunk(w_s[0], c), chunk(raw, c), ACT.Copy).then_inc(s["w_hi"], 1)

        @block.tensor
        def _(pe):
            for n, (c, part) in enumerate(products):
                pe.wait_ge(s["w_lo"], c + 1)
                wait_from_one(pe, s["taken"], n - 3)
                if c == V_CHUNK:
                    lhs = [tuple(x[:, k * B * S + part * S:k * B * S + (part + 1) * S] for x in C.cT) for k in range(KT)]
                    rhs = [tuple(chunk(x, c)[:, k * S:(k + 1) * S] for x in w_s) for k in range(KT)]
                    out = banks[n % 4][:, 0:S]
                else:
                    lhs = [tuple(chunk(x, c)[:, k * S:(k + 1) * S] for x in w_s) for k in range(KT)]
                    moving = C.cT if c == K_CHUNK else xT
                    rhs = [tuple(x[:, k * B * S + part * BANK:k * B * S + (part + 1) * BANK] for x in moving) for k in range(KT)]
                    out = banks[n % 4]
                matmul_tiles(pe, out, lhs, rhs).then_inc(s["mm"], 1)

        @block.vector
        def _(dve):
            for c in range(2 + SETS):
                dve.wait_ge(s["w_hi"], c + 1)
                minus(dve, chunk(w_s[1], c), chunk(raw, c), chunk(w_s[0], c)).then_inc(s["w_lo"], 1)
            dve.wait_ge(s["bias_in"], 48)
            for n, (c, part) in enumerate(products):
                dve.wait_ge(s["mm"], n + 1)
                if c == K_CHUNK:
                    ins = dve.tensor_scalar(k32[:, blk(part, BANK)], banks[n % 4], bk_col[:, 0:1], None, ALU.add)
                elif c == V_CHUNK:
                    ins = dve.tensor_tensor(v32[:, blk(part, S)], banks[n % 4][:, 0:S], bv_row[:, :], ALU.add)
                else:
                    m = c - Q_CHUNK
                    out = q32[:, :].rearrange("p (b n t) -> p b n t", b=B, n=SETS)[:, part * (B // 2):(part + 1) * (B // 2), m, :]
                    ins = dve.tensor_scalar(out, banks[n % 4].rearrange("p (b t) -> p b t", t=S), bq_cols[:, m:m + 1], None, ALU.add)
                ins.then_inc(s["taken"], 1)


def attention_small_heads(nc, C, wkv, wq, wo, bk, bq, bv, bo):
    with ExitStack() as ctx:
        ph = Phase(nc, ctx, "a0")
        q32, k32, v32 = ph.sb("q32", SETS * B * S), ph.sb("k32", B * S), ph.sb("v32", B * S)
        project_small_heads(nc, C, q32, k32, v32, wkv, wq, bk, bq, bv, bo)
        wo_raw, wo_s = ph.sb("wo_raw", SETS * D), ph.split("wo", SETS * D)
        q_s = [ph.split(f"q{p}", SETS * S) for p in (0, 1)]
        k_s = [ph.split(f"k{p}", 2 * S) for p in (0, 1)]
        v_s = [ph.split(f"v{p}", KV0 * S) for p in (0, 1)]
        probs = [ph.sb(f"probs{p}", RW) for p in (0, 1)]
        pT = [ph.split(f"pT{p}", RW) for p in (0, 1)]
        raw_max, neg_max, total = ([ph.sb(f"{n}{p}", RH) for p in (0, 1)] for n in ("raw_max", "neg_max", "total"))
        oT, keep = ph.split("oT", SETS * S), ph.sb("keep", 2)
        s = ph.sems("wo_in wo_hi wo_lo keep zeroed q_hi q_lo k_hi k_lo v_hi v_lo s_mm raw_max neg_max exped inverse probs"
                    " pT_mm pT_hi pT_lo av_mm oT_hi oT_lo o_mm added")
        bank_s = [C.ps[:, 2 * BANK * p:2 * BANK * (p + 1)] for p in (0, 1)]
        bank_pT, bank_oT, bank_out = C.ps[:, 4 * BANK:6 * BANK], C.ps[:, 6 * BANK:7 * BANK], C.ps[:, 7 * BANK:8 * BANK]
        SCALE = HD0 ** -0.5
        block = ctx.enter_context(nc.Block())

        def items(eng, step):
            for r in range(ROUNDS):
                step(0, r, 0)
            with eng.Fori(0, B // 2 - 1) as pair:
                for n in (1, 2):
                    for r in range(ROUNDS):
                        step(pair * 2 + n, r, n % 2)
            for r in range(ROUNDS):
                step(B - 1, r, 1)

        def exists(i):
            return not (isinstance(i, int) and i >= B)

        def diagonal(tile):
            whole = tile[:, :]
            return bass.AP(whole.tensor, whole.offset, [whole.ap[0], [S + HD0, KV0], [1, HD0]])

        @block.sync
        def _(sp):
            sp.dma_start(wo_raw[:, :], wo).then_inc(s["wo_in"], 16)

        @block.gpsimd
        def _(pool):
            def normalise(R, p):
                pool.wait_ge(s["inverse"], R + 1)
                v = probs[p][:, :].rearrange("p (h t) -> p h t", h=RH)
                pool.tensor_tensor(v, v, along_last(total[p][:, :], S), ALU.mult).then_inc(s["probs"], 1)
            normalise(0, 0)

            def step(i, r, p):
                if r < ROUNDS - 1 or exists(i + 1):
                    normalise(i * ROUNDS + r + 1, (r + 1) % 2)
            items(pool, step)

        @block.tensor
        def _(pe):
            def scores(i, r, p):
                R = i * ROUNDS + r
                if r == 0:
                    pe.wait_ge(s["q_lo"], i + 1)
                    pe.wait_ge(s["k_lo"], 2 * (i + 1))
                wait_from_one(pe, s["exped"], RH * (R - 1))
                rows = slice(32 * r, 32 * r + 32)
                for n in range(SETS):
                    last = matmul_split(pe, bank_s[r % 2][:, n * 2 * S:(n + 1) * 2 * S],
                                        tuple(x[rows, n * S:(n + 1) * S] for x in q_s[p]),
                                        tuple(x[rows, :] for x in k_s[p]), True, True)
                last.then_inc(s["s_mm"], 1)

            def turn(i, r):
                R = i * ROUNDS + r
                pe.wait_ge(s["probs"], R + 1)
                wait_from_one(pe, s["pT_lo"], 2 * R)
                for c in (0, 1):
                    for n in range(SETS):
                        last = pe.transpose(bank_pT[:, (c * SETS + n) * S:(c * SETS + n + 1) * S],
                                            probs[r % 2][:, (2 * n + c) * S:(2 * n + c + 1) * S], C.ident[:, :])
                    last.then_inc(s["pT_mm"], 1)

            def mix(i, r, p):
                R = i * ROUNDS + r
                if r == 0:
                    pe.wait_ge(s["v_lo"], i + 1)
                    wait_from_one(pe, s["oT_lo"], i)
                for c in (0, 1):
                    pe.wait_ge(s["pT_lo"], 2 * R + c + 1)
                    kv = 2 * r + c
                    last = matmul_split(pe, bank_oT, tuple(x[:, kv * S:(kv + 1) * S] for x in v_s[p]),
                                        tuple(x[:, c * BANK:(c + 1) * BANK] for x in pT[r % 2]), kv == 0, kv == KV0 - 1)
                last.then_inc(s["av_mm"], 1)

            def project_out(i):
                pe.wait_ge(s["oT_lo"], i + 1)
                wait_from_one(pe, s["added"], i)
                matmul_tiles(pe, bank_out, [tuple(x[:, n * S:(n + 1) * S] for x in oT) for n in range(SETS)],
                             [tuple(x[:, n * D:(n + 1) * D] for x in wo_s) for n in range(SETS)]).then_inc(s["o_mm"], 1)
            pe.wait_ge(s["zeroed"], 4)
            scores(0, 0, 0)
            scores(0, 1, 0)
            pe.wait_ge(s["wo_lo"], 1)

            def step(i, r, p):
                if r < ROUNDS - 2:
                    scores(i, r + 2, p)
                elif exists(i + 1):
                    scores(i + 1, r + 2 - ROUNDS, 1 - p)
                if r > 0:
                    mix(i, r - 1, p)
                elif not (isinstance(i, int) and i == 0):
                    mix(i - 1, ROUNDS - 1, 1 - p)
                turn(i, r)
                if r == 1 and not (isinstance(i, int) and i == 0):
                    project_out(i - 1)
            items(pe, step)
            mix(B - 1, ROUNDS - 1, 1)
            project_out(B - 1)

        @block.scalar
        def _(act):
            def stage_qk(i, p):
                wait_from_one(act, s["s_mm"], ROUNDS * (i - 1))
                act.activation(q_s[p][0][:, :], q32[:, bass.ds((i % B) * (SETS * S), SETS * S)], ACT.Copy).then_inc(s["q_hi"], 1)
                for c in (0, 1):
                    act.activation(k_s[p][0][:, c * S:(c + 1) * S], k32[:, bass.ds((i % B) * S, S)], ACT.Copy,
                                   scale=keep[:, c:c + 1]).then_inc(s["k_hi"], 1)

            def stage_v(i, p):
                wait_from_one(act, s["av_mm"], ROUNDS * (i - 1))
                v = v32[:, bass.ds((i % B) * S, S)].rearrange("p (k d) -> p k d", k=KV0)
                act.activation(diagonal(v_s[p][0]), v, ACT.Copy).then_inc(s["v_hi"], 1)

            def exps(R, p):
                act.wait_ge(s["neg_max"], R + 1)
                wait_from_one(act, s["pT_mm"], 2 * (R - 1))
                wait_from_one(act, s["probs"], R - 1)
                for h in range(RH):
                    act.activation(probs[p][:, h * S:(h + 1) * S], bank_s[p][:, h * S:(h + 1) * S], ACT.Exp,
                                   bias=neg_max[p][:, h:h + 1], scale=SCALE, accum_out=total[p][:, h:h + 1]).then_inc(s["exped"], 1)

            def split_pT(R, p):
                wait_from_one(act, s["av_mm"], R - 1)
                for c in (0, 1):
                    act.wait_ge(s["pT_mm"], 2 * R + c + 1)
                    at = slice(c * BANK, (c + 1) * BANK)
                    act.activation(pT[p][0][:, at], bank_pT[:, at], ACT.Copy).then_inc(s["pT_hi"], 1)

            def split_oT(i):
                act.wait_ge(s["av_mm"], ROUNDS * (i + 1))
                wait_from_one(act, s["o_mm"], i)
                act.activation(oT[0][:, :], bank_oT, ACT.Copy).then_inc(s["oT_hi"], 1)
            act.wait_ge(s["keep"], 1)
            stage_qk(0, 0)
            act.wait_ge(s["zeroed"], 4)
            stage_v(0, 0)
            act.wait_ge(s["wo_in"], 16)
            act.activation(wo_s[0][:, :], wo_raw[:, :], ACT.Copy).then_inc(s["wo_hi"], 1)
            exps(0, 0)

            def step(i, r, p):
                R = i * ROUNDS + r
                if not (isinstance(R, int) and R == 0):
                    split_pT(R - 1, (r - 1) % 2)
                if r == 0 and exists(i + 1):
                    stage_qk(i + 1, 1 - p)
                if r < ROUNDS - 1 or exists(i + 1):
                    exps(R + 1, (r + 1) % 2)
                if r == 0 and not (isinstance(i, int) and i == 0):
                    split_oT(i - 1)
                if r == 2 and exists(i + 1):
                    stage_v(i + 1, 1 - p)
            items(act, step)
            split_pT(B * ROUNDS - 1, 1)
            split_oT(B - 1)

        @block.vector
        def _(dve):
            def stage_qk(i, p):
                dve.wait_ge(s["q_hi"], i + 1)
                minus(dve, q_s[p][1][:, :], q32[:, bass.ds((i % B) * (SETS * S), SETS * S)], q_s[p][0][:, :]).then_inc(s["q_lo"], 1)
                dve.wait_ge(s["k_hi"], 2 * (i + 1))
                for c in (0, 1):
                    hi, lo = (x[:, c * S:(c + 1) * S] for x in k_s[p])
                    dve.scalar_tensor_tensor(lo, k32[:, bass.ds((i % B) * S, S)], keep[:, c:c + 1], hi.bitcast(F32), ALU.mult,
                                             ALU.subtract).then_inc(s["k_lo"], 1)

            def stage_v(i, p):
                dve.wait_ge(s["v_hi"], i + 1)
                v = v32[:, bass.ds((i % B) * S, S)].rearrange("p (k d) -> p k d", k=KV0)
                minus(dve, diagonal(v_s[p][1]), v, diagonal(v_s[p][0])).then_inc(s["v_lo"], 1)

            def maxima(R, p):
                dve.wait_ge(s["s_mm"], R + 1)
                wait_from_one(dve, s["neg_max"], R - 1)
                dve.tensor_reduce(raw_max[p][:, :], bank_s[p].rearrange("p (h t) -> p h t", h=RH), AX.X, ALU.max).then_inc(s["raw_max"], 1)
                dve.wait_ge(s["raw_max"], R + 1)
                wait_from_one(dve, s["exped"], RH * (R - 1))
                dve.tensor_scalar(neg_max[p][:, :], raw_max[p][:, :], -SCALE, None, ALU.mult).then_inc(s["neg_max"], 1)

            def invert(R, p):
                dve.wait_ge(s["exped"], RH * (R + 1))
                dve.reciprocal(total[p][:, :], total[p][:, :]).then_inc(s["inverse"], 1)

            def split_pT(R, p):
                for c in (0, 1):
                    at = slice(c * BANK, (c + 1) * BANK)
                    dve.wait_ge(s["pT_hi"], 2 * R + c + 1)
                    minus(dve, pT[p][1][:, at], bank_pT[:, at], pT[p][0][:, at]).then_inc(s["pT_lo"], 1)

            def split_oT(i):
                dve.wait_ge(s["oT_hi"], i + 1)
                minus(dve, oT[1][:, :], bank_oT, oT[0][:, :]).then_inc(s["oT_lo"], 1)

            def add_out(i):
                dve.wait_ge(s["o_mm"], i + 1)
                x_i = C.x[:, blk(i, D)]
                dve.tensor_tensor(x_i, x_i, bank_out, ALU.add).then_inc(s["added"], 1)
            dve.tensor_reduce(keep[:, :], C.ident[:, :].rearrange("p (a c r) -> p c a r", c=2, r=HD0), AX.XY,
                              ALU.add).then_inc(s["keep"], 1)
            for p in (0, 1):
                for half in (0, 1):
                    dve.tensor_scalar(v_s[p][half][:, :], C.ones[:, 0:1].to_broadcast([128, KV0 * S]), 0.0, None, ALU.mult)\
                        .then_inc(s["zeroed"], 1)
            dve.wait_ge(s["keep"], 1)
            dve.wait_ge(s["zeroed"], 4)
            stage_qk(0, 0)
            stage_v(0, 0)
            dve.wait_ge(s["wo_hi"], 1)
            minus(dve, wo_s[1][:, :], wo_raw[:, :], wo_s[0][:, :]).then_inc(s["wo_lo"], 1)
            maxima(0, 0)
            maxima(1, 1)
            invert(0, 0)

            def step(i, r, p):
                R = i * ROUNDS + r
                if not (isinstance(R, int) and R == 0):
                    split_pT(R - 1, (r - 1) % 2)
                if r == 0 and exists(i + 1):
                    stage_qk(i + 1, 1 - p)
                if r == 2 and not (isinstance(i, int) and i == 0):
                    add_out(i - 1)
                if r < ROUNDS - 2 or exists(i + 1):
                    maxima(R + 2, r % 2)
                if r < ROUNDS - 1 or exists(i + 1):
                    invert(R + 1, (r + 1) % 2)
                if r == 0 and not (isinstance(i, int) and i == 0):
                    split_oT(i - 1)
                if r == 2 and exists(i + 1):
                    stage_v(i + 1, 1 - p)
            items(dve, step)
            split_pT(B * ROUNDS - 1, 1)
            split_oT(B - 1)
            add_out(B - 1)



def attention_transposed(nc, C, context):
    with ExitStack() as ctx:
        ph = Phase(nc, ctx, "a3")
        t = NormBuffers(ph)
        xT = [ph.split(f"xT{p}", D) for p in (0, 1)]
        c_raw = [ph.sb(f"c_raw{p}", D) for p in (0, 1)]
        c_s = [ph.split(f"c{p}", D) for p in (0, 1)]
        probs = [ph.sb(f"probs{p}", S) for p in (0, 1)]
        total = [ph.sb(f"total{p}", 1) for p in (0, 1)]
        raw_max, neg_max = ph.sb("raw_max", 1), ph.sb("neg_max", 1)
        p_s = [ph.split(f"p{p}", S) for p in (0, 1)]
        s = ph.sems(NORM_SEMS + " c_in c_hi c_lo s_mm raw_max neg_max exped inverse probs p_hi p_lo o_mm added")
        bank_xT, bank_out = C.ps[:, 0:BANK], C.ps[:, 3 * BANK:4 * BANK]
        bank_s = [C.ps[:, (1 + p) * BANK:(1 + p) * BANK + S] for p in (0, 1)]
        SCALE = S ** -0.5
        block = ctx.enter_context(nc.Block())

        def x_of(i):
            return C.x[:, blk(i, D)]

        @block.sync
        def _(sp):
            for i in range(B):
                wait_from_one(sp, s["c_lo"], i - 1)
                wait_from_one(sp, s["c_in"], 16 * i)
                sp.dma_start(c_raw[i % 2][:, :], context[i]).then_inc(s["c_in"], 16)

        @block.gpsimd
        def _(pool):
            def front(i, p):
                pool.wait_ge(s["c_hi"], i + 1)
                minus(pool, c_s[p][1][:, :], c_raw[p][:, :], c_s[p][0][:, :]).then_inc(s["c_lo"], 1)
            norm_gpsimd(pool, C, s, t)
            in_pairs(pool, front, lambda i, p: None)

        @block.tensor
        def _(pe):
            def front(i, p):
                norm_tensor(pe, C, s, t.xn[:, :], bank_xT, i)
                pe.wait_ge(s["xT_lo"], i + 1)
                wait_from_one(pe, s["exped"], i - 1)
                lhs = [tuple(h[:, k * S:(k + 1) * S] for h in xT[p]) for k in range(KT)]
                rhs = [tuple(h[:, bass.ds(i * S + k * B * S, S)] for h in C.cT) for k in range(KT)]
                matmul_tiles(pe, bank_s[p], lhs, rhs).then_inc(s["s_mm"], 1)

            def back(i, p):
                pe.wait_ge(s["p_lo"], i + 1)
                pe.wait_ge(s["c_lo"], i + 1)
                wait_from_one(pe, s["added"], i)
                matmul_split(pe, bank_out, tuple(h[:, :] for h in p_s[p]), tuple(h[:, :] for h in c_s[p]),
                             True, True).then_inc(s["o_mm"], 1)
            in_pairs(pe, front, back)

        @block.scalar
        def _(act):
            def front(i, p):
                act.wait_ge(s["c_in"], 16 * (i + 1))
                wait_from_one(act, s["o_mm"], i - 1)
                act.activation(c_s[p][0][:, :], c_raw[p][:, :], ACT.Copy).then_inc(s["c_hi"], 1)
                act.wait_ge(s["xnT"], i + 1)
                wait_from_one(act, s["s_mm"], i - 1)
                act.activation(xT[p][0][:, :], bank_xT, ACT.Copy).then_inc(s["xT_hi"], 1)
                act.wait_ge(s["neg_max"], i + 1)
                wait_from_one(act, s["p_lo"], i - 1)
                act.activation(probs[p][:, :], bank_s[p], ACT.Exp, bias=neg_max[:, 0:1], scale=SCALE,
                               accum_out=total[p][:, :]).then_inc(s["exped"], 1)

            def back(i, p):
                act.wait_ge(s["probs"], i + 1)
                wait_from_one(act, s["o_mm"], i)
                act.activation(p_s[p][0][:, :], probs[p][:, :], ACT.Copy).then_inc(s["p_hi"], 1)
            in_pairs(act, front, back)

        @block.vector
        def _(dve):
            def front(i, p):
                dve.wait_ge(s["xT_hi"], i + 1)
                minus(dve, xT[p][1][:, :], bank_xT, xT[p][0][:, :]).then_inc(s["xT_lo"], 1)
                next_norm_vector(dve, C, s, t, i)
                dve.wait_ge(s["s_mm"], i + 1)
                dve.tensor_reduce(raw_max[:, :], bank_s[p], AX.X, ALU.max).then_inc(s["raw_max"], 1)
                dve.wait_ge(s["raw_max"], i + 1)
                wait_from_one(dve, s["exped"], i)
                dve.tensor_scalar(neg_max[:, :], raw_max[:, :], -SCALE, None, ALU.mult).then_inc(s["neg_max"], 1)

            def back(i, p):
                dve.wait_ge(s["exped"], i + 1)
                dve.reciprocal(total[p][:, :], total[p][:, :]).then_inc(s["inverse"], 1)
                dve.wait_ge(s["inverse"], i + 1)
                dve.tensor_scalar(probs[p][:, :], probs[p][:, :], total[p][:, 0:1], None, ALU.mult).then_inc(s["probs"], 1)
                dve.wait_ge(s["p_hi"], i + 1)
                minus(dve, p_s[p][1][:, :], probs[p][:, :], p_s[p][0][:, :]).then_inc(s["p_lo"], 1)
                dve.wait_ge(s["o_mm"], i + 1)
                dve.tensor_tensor(x_of(i), x_of(i), bank_out, ALU.add).then_inc(s["added"], 1)
            moments_vector(dve, C, s, t)
            in_pairs(dve, front, back)


E3 = 64
TOP = 8


def bias_experts(nc, C, w_router, router_bias, expert_bias, out):
    with ExitStack() as ctx:
        ph = Phase(nc, ctx, "f3")
        t = NormBuffers(ph)
        xT = [ph.split(f"xT{p}", D) for p in (0, 1)]
        xn_all = ph.sb("xn_all", B * D)
        router_raw, router = ph.sb("router_raw", KT * E3), ph.split("router", KT * E3)
        eb_raw, eb = ph.sb("eb_raw", D, rows=E3), ph.split("eb", D, rows=E3)
        row = ph.sb("row", E3)
        scores, most = ph.sb("scores", B * E3), ph.sb("most", B)
        current, rest, top = ph.sb("current", E3), ph.sb("rest", E3), ph.sb("top", TOP)
        w_sum = [ph.sb(f"w_sum{p}", 1) for p in (0, 1)]
        taken = ph.sb("taken", 128)
        wT = [ph.split(f"wT{p}", S, rows=E3) for p in (0, 1)]
        delta = ph.sb("delta", D)
        s = ph.sems(NORM_SEMS + " w_in row_in w_hi w_lo xn_kept logits_mm scores chain below exped padded current"
                    " top taken w_sum takenT wT_hi wT_lo up_mm delta added stored")
        bank_xT, bank_l, bank_wT, bank_up = (C.ps[:, blk(k, BANK)] for k in range(4))
        block = ctx.enter_context(nc.Block())

        def x_of(i):
            return C.x[:, blk(i, D)]

        def nothing(i, p):
            pass

        @block.sync
        def _(sp):
            sp.dma_start(router_raw[:, :], w_router).then_inc(s["w_in"], 16)
            sp.dma_start(eb_raw[:, :], expert_bias).then_inc(s["w_in"], 16)
            sp.dma_start(row[:, :], router_bias.partition_broadcast(128)).then_inc(s["row_in"], 16)
            with sp.Fori(0, B) as i:
                sp.wait_ge(s["added"], i + 1)
                sp.dma_start(out[bass.ds(i, 1)].rearrange("a p d -> p (a d)"), x_of(i)).then_inc(s["stored"], 16)
            sp.wait_ge(s["stored"], 16 * B)

        @block.gpsimd
        def _(pool):
            pool.memset(taken[:, E3:128], 0.0).then_inc(s["padded"], 1)
            norm_gpsimd(pool, C, s, t)

        @block.tensor
        def _(pe):
            pe.wait_ge(s["w_lo"], 2)

            def back(i, p):
                pe.wait_ge(s["xT_lo"], i + 1)
                wait_from_one(pe, s["scores"], i)
                matmul_tiles(pe, bank_l[:, 0:E3], [tuple(h[:, k * S:(k + 1) * S] for h in xT[p]) for k in range(KT)],
                             [tuple(h[:, k * E3:(k + 1) * E3] for h in router) for k in range(KT)]).then_inc(s["logits_mm"], 1)

            in_pairs(pe, lambda i, p: norm_tensor(pe, C, s, t.xn[:, :], bank_xT, i), back)
            pe.wait_ge(s["padded"], 1)

            def front2(i, p):
                pe.wait_ge(s["taken"], i + 1)
                wait_from_one(pe, s["wT_lo"], i)
                pe.transpose(bank_wT[:, 0:S], taken[:, :], C.ident[:, :]).then_inc(s["takenT"], 1)

            def back2(i, p):
                pe.wait_ge(s["wT_lo"], i + 1)
                wait_from_one(pe, s["delta"], i)
                matmul_split(pe, bank_up, tuple(h[:, :] for h in wT[p]), tuple(h[:, :] for h in eb), True, True)\
                    .then_inc(s["up_mm"], 1)
            in_pairs(pe, front2, back2)

        @block.scalar
        def _(act):
            act.wait_ge(s["w_in"], 32)
            act.activation(router[0][:, :], router_raw[:, :], ACT.Copy).then_inc(s["w_hi"], 1)
            act.activation(eb[0][:, :], eb_raw[:, :], ACT.Copy).then_inc(s["w_hi"], 1)

            def front(i, p):
                act.wait_ge(s["xn"], i + 1)
                act.activation(xn_all[:, blk(i, D)], t.xn[:, :], ACT.Copy).then_inc(s["xn_kept"], 1)
                act.wait_ge(s["xnT"], i + 1)
                wait_from_one(act, s["logits_mm"], i - 1)
                act.activation(xT[p][0][:, :], bank_xT, ACT.Copy).then_inc(s["xT_hi"], 1)
            in_pairs(act, front, nothing)
            act.wait_ge(s["below"], 1)
            act.activation(scores[:, :], scores[:, :], ACT.Exp).then_inc(s["exped"], 1)

            def front2(i, p):
                act.wait_ge(s["takenT"], i + 1)
                wait_from_one(act, s["up_mm"], i - 1)
                act.activation(wT[p][0][:, :], bank_wT[0:E3, 0:S], ACT.Copy).then_inc(s["wT_hi"], 1)
            in_pairs(act, front2, nothing)

        @block.vector
        def _(dve):
            n_link = [0]

            def link(ins):
                n_link[0] += 1
                ins.then_inc(s["chain"], 1)
                dve.wait_ge(s["chain"], n_link[0])
            dve.wait_ge(s["w_hi"], 1)
            minus(dve, router[1][:, :], router_raw[:, :], router[0][:, :]).then_inc(s["w_lo"], 1)
            dve.wait_ge(s["w_hi"], 2)
            minus(dve, eb[1][:, :], eb_raw[:, :], eb[0][:, :]).then_inc(s["w_lo"], 1)
            dve.wait_ge(s["row_in"], 16)
            moments_vector(dve, C, s, t)

            def front(i, p):
                dve.wait_ge(s["xT_hi"], i + 1)
                minus(dve, xT[p][1][:, :], bank_xT, xT[p][0][:, :]).then_inc(s["xT_lo"], 1)
                dve.wait_ge(s["xn_kept"], i + 1)
                next_norm_vector(dve, C, s, t, i)

            def back(i, p):
                dve.wait_ge(s["logits_mm"], i + 1)
                dve.tensor_tensor(scores[:, blk(i, E3)], bank_l[:, 0:E3], row[:, :], ALU.add).then_inc(s["scores"], 1)
            in_pairs(dve, front, back)
            dve.wait_ge(s["scores"], B)
            s3 = by_sequence(scores[:, :])
            link(dve.tensor_reduce(most[:, :], s3, AX.X, ALU.max))
            dve.tensor_tensor(s3, s3, along_last(most[:, :], E3), ALU.subtract).then_inc(s["below"], 1)
            dve.wait_ge(s["exped"], 1)
            link(dve.tensor_reduce(most[:, :], s3, AX.X, ALU.add))
            link(dve.reciprocal(most[:, :], most[:, :]))
            link(dve.tensor_tensor(s3, s3, along_last(most[:, :], E3), ALU.mult))
            dve.wait_ge(s["xn_kept"], B)

            def front2(i, p):
                dve.tensor_copy(current[:, :], scores[:, blk(i, E3)]).then_inc(s["current"], 1)
                dve.drain()
                dve.max(top[:, :], current[:, :])
                dve.drain()
                dve.match_replace(rest[:, :], top[:, :], current[:, :], 0.0).then_inc(s["top"], 1)
                dve.wait_ge(s["top"], i + 1)
                wait_from_one(dve, s["takenT"], i)
                dve.tensor_tensor(taken[:, 0:E3], current[:, :], rest[:, :], ALU.subtract).then_inc(s["taken"], 1)
                dve.tensor_reduce(w_sum[p][:, :], top[:, :], AX.X, ALU.add).then_inc(s["w_sum"], 1)
                dve.wait_ge(s["wT_hi"], i + 1)
                minus(dve, wT[p][1][:, :], bank_wT[0:E3, 0:S], wT[p][0][:, :]).then_inc(s["wT_lo"], 1)

            def back2(i, p):
                dve.wait_ge(s["up_mm"], i + 1)
                dve.wait_ge(s["w_sum"], i + 1)
                wait_from_one(dve, s["added"], i)
                dve.scalar_tensor_tensor(delta[:, :], xn_all[:, blk(i, D)], w_sum[p][:, 0:1], bank_up, ALU.mult,
                                         ALU.add).then_inc(s["delta"], 1)
                dve.wait_ge(s["delta"], i + 1)
                dve.tensor_tensor(x_of(i), x_of(i), delta[:, :], ALU.add).then_inc(s["added"], 1)
            in_pairs(dve, front2, back2)



class Core:

    def __init__(self, nc, ctx):
        def sb(name, cols):
            return ctx.enter_context(nc.sbuf_tensor(name, [128, cols], F32))
        self.x = sb("x", B * D)
        self.ident, self.ones, self.neg_half = sb("ident", 128), sb("ones", 128), sb("neg_half", 8)
        self.ln_eps, self.falling = sb("ln_eps", 1), sb("falling", E)
        self.to_exp = sb("to_exp", B * E)
        self.ps = ctx.enter_context(nc.psum_tensor("ps", [128, 8 * BANK], F32))


def build(nc, A, out):
    with ExitStack() as ctx:
        def sb(name, cols, dt=F32):
            return ctx.enter_context(nc.sbuf_tensor(name, [128, cols], dt))
        C = Core(nc, ctx)
        set_up(nc, C, A["x"])
        C.cT = tuple(sb(f"cT_{h}", KT * B * S, F32R) for h in ("hi", "lo"))
        context_transposed(nc, C, A["cT"])
        attention_small_heads(nc, C, A["L0_wkv"], A["L0_wq"], A["L0_wo"], A["L0_bk"], A["L0_bq"], A["L0_xattn_bv"],
                              A["L0_xattn_bo"])
        ffn_phase(nc, C, "f0", GateNet, A["L0_main"], A["L0_side"], A["L0_up"], 1.0 / R,
                  extra=[A[n] for n in ("L0_ffn_gb1", "L0_ffn_ln_gamma", "L0_ffn_ln_beta", "L0_gw2", "L0_ffn_gb2")])
        attention_phase(nc, C, "a1", A["L1_wkv"], A["L1_wq"], A["L1_wo"], q_norm=A["L1_xattn_q_norm_w"],
                        k_norm=A["L1_xattn_k_norm_w"], mask=A["mask"])
        ffn_phase(nc, C, "f1", TopTwo, A["L1_main"], A["L1_side"], A["L1_up"], 1.0, bias=A["L1_ffn_b_base"])
        attention_phase(nc, C, "a2", A["L2_wkv"], A["L2_wq"], A["L2_wo"], bq=A["L2_bq"], bk=A["L2_bk"],
                        bv=A["L2_bv"], bo=A["L2_xattn_bo"])
        ffn_phase(nc, C, "f2", MeanRoute, A["L2_main"], A["L2_side"], A["L2_up"], 2.0, bias=A["L2_ffn_b"],
                  extra=[A["L2_ffn_router_b"]])
        attention_transposed(nc, C, A["context"])
        bias_experts(nc, C, A["L3_router"], A["L3_ffn_router_bias"], A["L3_ffn_expert_bias"], out)


def kernel(**inputs):
    import numpy as np
    import concourse.bacc as bacc
    from concourse.bass_utils import run_bass_kernel_spmd

    def tiled(w):
        return np.ascontiguousarray(w.reshape(KT, 128, -1).transpose(1, 0, 2).reshape(128, -1))

    I = {k: np.asarray(v) for k, v in inputs.items()}
    A = {"x": I["x"]}
    for n, main, a, gate, up in (
            ("L0", I["L0_ffn_weight"].T, I["L0_ffn_lora_A"].transpose(1, 0, 2).reshape(D, ER), I["L0_ffn_gw1"].T,
             I["L0_ffn_lora_B"].reshape(ER, D)),
            ("L1", I["L1_ffn_W_base"].T, I["L1_ffn_A"].reshape(ER, D).T, I["L1_ffn_W_gate"].T,
             I["L1_ffn_B"].transpose(0, 2, 1).reshape(ER, D)),
            ("L2", I["L2_ffn_W"].T, I["L2_ffn_A"].reshape(ER, D).T, I["L2_ffn_router_W"].T,
             I["L2_ffn_B"].transpose(0, 2, 1).reshape(ER, D))):
        A[n + "_main"] = tiled(main)
        A[n + "_side"] = tiled(np.concatenate([a, gate], axis=1))
        A[n + "_up"] = np.ascontiguousarray(up)
    A["L0_gw2"] = I["L0_ffn_gw2"].reshape(-1)
    for n in ("L0_ffn_gb1", "L0_ffn_ln_gamma", "L0_ffn_ln_beta", "L0_ffn_gb2", "L1_ffn_b_base", "L2_ffn_b",
              "L2_ffn_router_b"):
        A[n] = I[n]

    def sets(w):
        return w.reshape(KV0, SETS, HD0, -1).transpose(1, 0, 2, 3).reshape(SETS, KV0 * HD0, -1)

    def chunks(w):
        return w.reshape(KT, 128, -1, 128).transpose(2, 1, 0, 3).reshape(-1, 128, CHUNK)
    A["L0_wq"] = chunks(sets(I["L0_xattn_Wq"].T).reshape(D, D).T)
    A["L0_wkv"] = chunks(np.concatenate([I["L0_xattn_Wk"], I["L0_xattn_Wv"]], axis=1))
    A["L0_wo"] = sets(I["L0_xattn_Wo"]).transpose(1, 0, 2).reshape(128, SETS * D)
    A["L0_bq"] = sets(I["L0_xattn_bq"]).reshape(SETS, 128).T
    A["L0_bk"] = I["L0_xattn_bk"].reshape(128, 1)
    A["context"] = I["ctx_4096"]
    A["L3_router"] = tiled(I["L3_ffn_router_weight"].T)
    for n in ("L0_xattn_bv", "L0_xattn_bo", "L3_ffn_router_bias", "L3_ffn_expert_bias"):
        A[n] = I[n]

    A["cT"] = tiled(I["ctx_4096"].reshape(B * S, D).T)
    A["mask"] = I["mask_1x1xSxS2_ff0"].reshape(S, S)

    def heads_apart(w, n):
        return w.reshape(KT, 128, GROUPS, n, HD).transpose(2, 3, 1, 0, 4).reshape(GROUPS, n, 128, CHUNK)

    def v_and_k(k, v):
        return np.concatenate([heads_apart(v, 1), heads_apart(k, 1)], axis=1)

    def columns(b):
        return b.reshape(-1, HD).T
    A["L1_wq"] = heads_apart(I["L1_xattn_Wq"].T, HQ)
    A["L1_wkv"] = v_and_k(I["L1_xattn_Wk"].T, I["L1_xattn_Wv"].T)
    A["L1_wo"] = I["L1_xattn_Wo"].T.reshape(GROUPS, HQ, HD, D)
    A["L1_xattn_q_norm_w"], A["L1_xattn_k_norm_w"] = columns(I["L1_xattn_q_norm_w"]), columns(I["L1_xattn_k_norm_w"])
    A["L2_wq"] = heads_apart(I["L2_xattn_Wq"], HQ)
    wkv, bkv = I["L2_xattn_Wkv"], I["L2_xattn_bkv"]
    A["L2_wkv"] = v_and_k(wkv[:, :GROUPS * HD], wkv[:, GROUPS * HD:])
    A["L2_wo"] = I["L2_xattn_Wo"].reshape(GROUPS, HQ, HD, D)
    A["L2_bq"], A["L2_bk"], A["L2_bv"] = columns(I["L2_xattn_bq"]), columns(bkv[:GROUPS * HD]), columns(bkv[GROUPS * HD:])
    for n in ("L2_xattn_bo",):
        A[n] = I[n]

    nc = bacc.Bacc("TRN2", target_bir_lowering=False, num_devices=1)
    A = {n: np.ascontiguousarray(a) for n, a in A.items()}
    aps = {n: nc.dram_tensor(f"in_{n}", a.shape, mybir.dt.from_np(a.dtype), kind="ExternalInput").ap() for n, a in A.items()}
    out = nc.dram_tensor("out", (B, S, D), F32, kind="ExternalOutput").ap()
    build(nc, aps, out)
    return run_bass_kernel_spmd(nc, [{f"in_{n}": a for n, a in A.items()}], core_ids=[0]).results[0]["out"]
```

```python
import concourse.bass as bass
from concourse import mybir
from contextlib import ExitStack

F32 = mybir.dt.float32
F32R = mybir.dt.float32r
ALU = mybir.AluOpType
ACT = mybir.ActivationFunctionType
AX = mybir.AxisListType

B = 8
S = 128
D = 512
KT = D // 128
BANK = 512
LN_EPS = 1e-5
NEVER = -3.0e38


def blk(i, width):
    return bass.ds(i * width, width)


def wait_from_one(eng, sem, value):
    if not (isinstance(value, int) and value <= 0):
        eng.wait_ge(sem, value)


def in_pairs(eng, front, back):
    front(0, 0)
    front(1, 1)
    back(0, 0)
    with eng.Fori(0, B // 2 - 2) as pair:
        i = pair * 2 + 1
        for n in (0, 1):
            front(i + n + 1, n)
            back(i + n, 1 - n)
    for i in (B - 2, B - 1):
        front(i, i % 2)
        back(i - 1, (i - 1) % 2)
    back(B - 1, 1)


def nothing(i, p):
    pass


def matmul_split(pe, out, lhs, rhs, start, stop):
    (lhs_hi, lhs_lo), (rhs_hi, rhs_lo) = lhs, rhs
    pe.matmul(out, lhs_lo, rhs_hi, start=start, stop=False)
    pe.matmul(out, lhs_hi, rhs_lo, start=False, stop=False)
    return pe.matmul(out, lhs_hi, rhs_hi, start=False, stop=stop)


def matmul_tiles(pe, out, lhs_tiles, rhs_tiles):
    n = len(lhs_tiles)
    for k in range(n):
        last = matmul_split(pe, out, lhs_tiles[k], rhs_tiles[k], k == 0, k == n - 1)
    return last


def minus(eng, out_lo, value, hi):
    return eng.tensor_tensor(out_lo, value, hi.bitcast(F32), ALU.subtract)


class Phase:

    def __init__(self, nc, ctx, tag):
        self.nc, self.ctx, self.tag, self.used = nc, ctx, tag, []
        ctx.callback(self.clear)

    def clear(self):
        self.nc.clear_and_free_semaphores(self.used)
        self.nc.all_engine_barrier()

    def sb(self, name, cols, dt=F32, rows=128):
        return self.ctx.enter_context(self.nc.sbuf_tensor(f"{self.tag}_{name}", [rows, cols], dt))

    def split(self, name, cols, rows=128):
        return (self.sb(name + "_hi", cols, F32R, rows), self.sb(name + "_lo", cols, F32R, rows))

    def sem(self, name):
        self.used.append(self.nc.alloc_semaphore(name=f"{self.tag}_{name}"))
        return self.used[-1]

    def sems(self, names):
        return {n: self.sem(n) for n in names.split()}



NORM_SEMS = "stats moments veps rstd xn xnT xT_hi xT_lo"


class NormBuffers:
    def __init__(self, ph):
        self.stats, self.moments = ph.sb("stats", B * 6), ph.sb("moments", B * 2)
        self.veps, self.rstd = ph.sb("veps", B), ph.sb("rstd", B)
        self.xn = [ph.sb(f"xn{p}", D) for p in (0, 1)]


def moments_vector(dve, C, s, t, meanwhile=None):
    for i in range(B):
        dve.bn_stats(t.stats[:, blk(i, 6)], C.x[:, blk(i, D)]).then_inc(s["stats"], 1)
    dve.drain()
    for i in range(B):
        dve.bn_aggr(t.moments[:, 2 * i:2 * i + 2], t.stats[:, 6 * i:6 * i + 6]).then_inc(s["moments"], 1)
    if meanwhile:
        meanwhile()
    dve.wait_ge(s["rstd"], 1)
    norm_vector(dve, C, s, t, 0, 0)


def norm_vector(dve, C, s, t, i, p):
    wait_from_one(dve, s["xnT"], i - 1)
    dve.tensor_scalar(t.xn[p][:, :], C.x[:, blk(i, D)], t.moments[:, blk(i * 2, 1)], t.rstd[:, blk(i, 1)], ALU.subtract,
                      ALU.mult).then_inc(s["xn"], 1)


def next_norm_vector(dve, C, s, t, i, p):
    if not (isinstance(i, int) and i == B - 1):
        norm_vector(dve, C, s, t, i + 1, 1 - p)


def norm_gpsimd(pool, C, s, t):
    pool.wait_ge(s["moments"], B)
    variance = t.moments[:, :].rearrange("p (b c) -> p b c", c=2)[:, :, 1]
    pool.tensor_tensor(t.veps[:, :], variance, C.ln_eps[:, 0:1].to_broadcast([128, B]), ALU.add).then_inc(s["veps"], 1)
    pool.wait_ge(s["veps"], 1)
    pool.tensor_tensor(t.rstd[:, :], t.veps[:, :], C.neg_half[:, 0:B], ALU.pow).then_inc(s["rstd"], 1)


def norm_tensor(pe, C, s, xn, bank, i):
    pe.wait_ge(s["xn"], i + 1)
    wait_from_one(pe, s["xT_lo"], i - 1)
    for k in range(KT):
        last = pe.transpose(bank[:, k * 128:(k + 1) * 128], xn[:, k * 128:(k + 1) * 128], C.ident[:, :])
    last.then_inc(s["xnT"], 1)


def tiles_of(bank):
    return bank.rearrange("p (k t) -> p k t", k=KT)



def set_up(nc, C, x_dram, cT_dram):
    with ExitStack() as ctx:
        ph = Phase(nc, ctx, "setup")
        raw = ph.sb("raw", KT * B * S)
        s = ph.sems("zeroed const x_in loaded0 loaded1 loaded2 loaded3 hi lo")
        block = ctx.enter_context(nc.Block())

        @block.sync
        def _(sp):
            for k in range(KT):
                sp.dma_start(raw[:, blk(k, B * S)], cT_dram[:, blk(k, B * S)]).then_inc(s[f"loaded{k}"], 16)
            sp.wait_ge(s["x_in"], 16 * B)

        @block.scalar
        def _(act):
            for b in range(B):
                act.dma_start(C.x[:, blk(b, D)], x_dram[b]).then_inc(s["x_in"], 16)
            for k in range(KT):
                act.wait_ge(s[f"loaded{k}"], 16)
                act.activation(C.cT[0][:, blk(k, B * S)], raw[:, blk(k, B * S)], ACT.Copy).then_inc(s["hi"], 1)

        @block.vector
        def _(dve):
            for k in range(KT):
                dve.wait_ge(s["hi"], k + 1)
                minus(dve, C.cT[1][:, blk(k, B * S)], raw[:, blk(k, B * S)], C.cT[0][:, blk(k, B * S)]).then_inc(s["lo"], 1)

        @block.gpsimd
        def _(pool):
            pool.memset(C.ident[:, :], 0.0).then_inc(s["zeroed"], 1)
            pool.memset(C.neg_half[:, :], -0.5).then_inc(s["zeroed"], 1)
            pool.memset(C.ones[:, :], 1.0).then_inc(s["zeroed"], 1)
            pool.memset(C.ln_eps[:, :], LN_EPS).then_inc(s["zeroed"], 1)
            for e in range(8):
                pool.memset(C.falling[:, e:e + 1], float(8 - e)).then_inc(s["zeroed"], 1)
            pool.wait_ge(s["zeroed"], 12)
            pool.affine_select(out=C.ident[:, :], in_=C.ident[:, :], compare_op=ALU.not_equal, fill=1.0,
                               base=0, pattern=[[-1, 128]], channel_multiplier=1).then_inc(s["const"], 1)
            pool.wait_ge(s["const"], 1)



E = 8
R = 16
ER = E * R
GATE_HID = 32
CAPACITY = int(3.0 * B * S / E)
MEAN_FROM, MEAN_TO = 107, S - 1


def by_sequence(tile):
    return tile.rearrange("p (b c) -> p b c", b=B)


def along_last(v, n):
    return v.unsqueeze(2).to_broadcast([128, v.shape[1], n])


def along_sequences(v):
    return v.unsqueeze(1).to_broadcast([128, B, v.shape[1]])


def best_expert(link, dve, C, gates, onehot, best, rank):
    g3, o3 = by_sequence(gates), by_sequence(onehot)
    link(dve.tensor_reduce(best, g3, AX.X, ALU.max))
    link(dve.tensor_tensor(o3, g3, along_last(best, E), ALU.is_equal))
    link(dve.tensor_tensor(o3, o3, along_sequences(C.falling[:, :]), ALU.mult))
    link(dve.tensor_reduce(rank, o3, AX.X, ALU.max))
    link(dve.tensor_tensor(o3, o3, along_last(rank, E), ALU.is_equal))


class TopTwo:
    G = E
    N_ROWS = 0

    def __init__(self, ph, C, extra):
        self.C, self.extra = C, extra
        self.gates, self.first, self.second, self.rest = (
            ph.sb(n, B * E) for n in ("gates", "first", "second", "rest"))
        self.best, self.next, self.rank, self.share = (ph.sb(n, B) for n in ("best", "next", "rank", "share"))
        self.ratio = C.to_exp[:, 0:B]
        self.ahead, self.exped = ph.sem("ahead"), ph.sem("exped")
        self.route = self.first

    def load(self, sp, sem):
        pass

    def gpsimd(self, pool):
        pass

    def tensor(self, pe, bank):
        pass

    def scalar(self, act):
        act.wait_ge(self.ahead, 1)
        act.activation(self.ratio, self.ratio, ACT.Exp).then_inc(self.exped, 1)

    def pick(self, dve, link):
        best_expert(link, dve, self.C, self.gates[:, :], self.first[:, :], self.best[:, :], self.rank[:, :])
        link(dve.scalar_tensor_tensor(self.rest[:, :], self.first[:, :], NEVER, self.gates[:, :], ALU.mult, ALU.add))
        best_expert(link, dve, self.C, self.rest[:, :], self.second[:, :], self.next[:, :], self.rank[:, :])
        dve.tensor_tensor(self.ratio, self.next[:, :], self.best[:, :], ALU.subtract).then_inc(self.ahead, 1)
        dve.wait_ge(self.exped, 1)
        link(dve.tensor_scalar(self.share[:, :], self.ratio, 1.0, None, ALU.add))
        link(dve.reciprocal(self.share[:, :], self.share[:, :]))
        link(dve.tensor_tensor(self.ratio, self.ratio, self.share[:, :], ALU.mult))

    def weigh(self, dve, link):
        for onehot, w in ((self.first, self.share[:, :]), (self.second, self.ratio)):
            o3 = by_sequence(onehot[:, :])
            link(dve.tensor_tensor(o3, o3, along_last(w, E), ALU.mult))
        link(dve.tensor_tensor(self.first[:, :], self.first[:, :], self.second[:, :], ALU.add))

    def vector(self, dve, link, gate_out, bank, rows_loaded):
        link(dve.tensor_copy(by_sequence(self.gates[:, :]), gate_out))
        self.pick(dve, link)
        self.weigh(dve, link)


class GateNet(TopTwo):
    G = GATE_HID
    N_ROWS = 5

    def __init__(self, ph, C, extra):
        super().__init__(ph, C, extra)
        n = GATE_HID
        self.rows = [ph.sb(f"row{k}", w) for k, w in enumerate((n, n, n, E * n, E))]
        self.hid, self.dev = ph.sb("hid", B * n), ph.sb("dev", B * n)
        self.stat, self.inv = ph.sb("stat", B), ph.sb("inv", B)
        self.products = ph.sb("products", B * E * n)
        self.counts, self.allowed = ph.sb("counts", 2 * E), ph.sb("allowed", 2 * E)
        self.var, self.inverted, self.counted, self.summed = (
            ph.sem(n) for n in ("var", "inverted", "counted", "summed"))

    def load(self, sp, sem):
        for dst, src in zip(self.rows, self.extra):
            sp.dma_start(dst[:, :], src.partition_broadcast(128)).then_inc(sem, 16)

    def gpsimd(self, pool):
        pool.wait_ge(self.var, 1)
        pool.tensor_tensor(self.inv[:, :], self.stat[:, :], self.C.neg_half[:, 0:B], ALU.pow).then_inc(self.inverted, 1)

    def tensor(self, pe, bank):
        pe.wait_ge(self.counted, 1)
        pe.matmul(bank[:, 0:2 * E], self.C.ones[:, :], self.counts[:, :], start=True, stop=True).then_inc(self.summed, 1)

    def vector(self, dve, link, gate_out, bank, rows_loaded):
        b1, gamma, beta, w2, b2 = (r[:, :] for r in self.rows)
        hid, dev = by_sequence(self.hid[:, :]), by_sequence(self.dev[:, :])
        stat, n = self.stat[:, :], GATE_HID
        dve.wait_ge(rows_loaded, 16 * self.N_ROWS)
        link(dve.tensor_tensor(hid, gate_out, along_sequences(b1), ALU.add))
        link(dve.tensor_reduce(stat, hid, AX.X, ALU.add))
        link(dve.tensor_scalar(stat, stat, 1.0 / n, None, ALU.mult))
        link(dve.tensor_tensor(hid, hid, along_last(stat, n), ALU.subtract))
        link(dve.tensor_tensor(dev, hid, hid, ALU.mult))
        link(dve.tensor_reduce(stat, dev, AX.X, ALU.add))
        dve.tensor_scalar(stat, stat, 1.0 / n, LN_EPS, ALU.mult, ALU.add).then_inc(self.var, 1)
        dve.wait_ge(self.inverted, 1)
        link(dve.tensor_tensor(hid, hid, along_last(self.inv[:, :], n), ALU.mult))
        link(dve.tensor_tensor(hid, hid, along_sequences(gamma), ALU.mult))
        link(dve.tensor_tensor(hid, hid, along_sequences(beta), ALU.add))
        link(dve.tensor_scalar(self.hid[:, :], self.hid[:, :], 0.0, None, ALU.max))
        for b in range(B):
            p3 = self.products[:, b * E * n:(b + 1) * E * n].rearrange("p (e c) -> p e c", e=E)
            h3 = self.hid[:, b * n:(b + 1) * n].unsqueeze(1).to_broadcast([128, E, n])
            link(dve.tensor_tensor(p3, h3, w2.rearrange("p (e c) -> p e c", e=E), ALU.mult))
        link(dve.tensor_reduce(self.gates[:, :], self.products[:, :].rearrange("p (g c) -> p g c", c=n), AX.X, ALU.add))
        g3 = by_sequence(self.gates[:, :])
        link(dve.tensor_tensor(g3, g3, along_sequences(b2), ALU.add))
        self.pick(dve, link)
        link(dve.tensor_reduce(self.counts[:, 0:E], self.first[:, :].rearrange("p (b e) -> p e b", b=B), AX.X, ALU.add))
        dve.tensor_reduce(self.counts[:, E:2 * E], self.second[:, :].rearrange("p (b e) -> p e b", b=B), AX.X,
                          ALU.add).then_inc(self.counted, 1)
        dve.wait_ge(self.summed, 1)
        link(dve.tensor_scalar(self.allowed[:, :], bank[:, 0:2 * E], float(CAPACITY), None, ALU.is_le))
        for k, onehot in enumerate((self.first, self.second)):
            o3 = by_sequence(onehot[:, :])
            link(dve.tensor_tensor(o3, o3, along_sequences(self.allowed[:, k * E:(k + 1) * E]), ALU.mult))
        self.weigh(dve, link)


class MeanRoute:
    G = E
    N_ROWS = 1

    def __init__(self, ph, C, extra):
        self.C, self.extra = C, extra
        self.row, self.average = ph.sb("row", E), ph.sb("average", S)
        self.gates, self.route, self.most = ph.sb("gates", B * E), C.to_exp, ph.sb("most", B)
        self.masked, self.copied, self.averaged, self.below, self.exped = (
            ph.sem(n) for n in ("masked", "copied", "averaged", "below", "exped"))

    def load(self, sp, sem):
        sp.dma_start(self.row[:, :], self.extra[0].partition_broadcast(128)).then_inc(sem, 16)

    def gpsimd(self, pool):
        a = self.average[:, :]
        pool.memset(a, 1.0 / (MEAN_TO - MEAN_FROM)).then_inc(self.masked, 1)
        pool.wait_ge(self.masked, 1)
        pool.affine_select(out=a, in_=a, compare_op=ALU.is_ge, fill=0.0, base=-MEAN_FROM, pattern=[[0, S]],
                           channel_multiplier=1).then_inc(self.masked, 1)
        pool.wait_ge(self.masked, 2)
        pool.affine_select(out=a, in_=a, compare_op=ALU.is_ge, fill=0.0, base=MEAN_TO - 1, pattern=[[0, S]],
                           channel_multiplier=-1).then_inc(self.masked, 1)

    def tensor(self, pe, bank):
        pe.wait_ge(self.copied, 1)
        pe.wait_ge(self.masked, 3)
        pe.matmul(bank[:, 0:B * E], self.average[:, :], self.gates[:, :], start=True, stop=True).then_inc(self.averaged, 1)

    def scalar(self, act):
        act.wait_ge(self.below, 1)
        act.activation(self.route[:, :], self.route[:, :], ACT.Exp).then_inc(self.exped, 1)

    def vector(self, dve, link, gate_out, bank, rows_loaded):
        r3, most = by_sequence(self.route[:, :]), self.most[:, :]
        dve.tensor_copy(by_sequence(self.gates[:, :]), gate_out).then_inc(self.copied, 1)
        dve.wait_ge(rows_loaded, 16)
        dve.wait_ge(self.averaged, 1)
        link(dve.tensor_tensor(r3, by_sequence(bank[:, 0:B * E]), along_sequences(self.row[:, :]), ALU.add))
        link(dve.tensor_reduce(most, r3, AX.X, ALU.max))
        dve.tensor_tensor(r3, r3, along_last(most, E), ALU.subtract).then_inc(self.below, 1)
        dve.wait_ge(self.exped, 1)
        link(dve.tensor_reduce(most, r3, AX.X, ALU.add))
        link(dve.reciprocal(most, most))
        link(dve.tensor_tensor(r3, r3, along_last(most, E), ALU.mult))


def ffn_phase(nc, C, tag, Route, w_main, w_side, w_up, scale, bias=None, extra=None):
    SIDE = ER + Route.G
    with ExitStack() as ctx:
        ph = Phase(nc, ctx, tag)
        t = NormBuffers(ph)
        xT = [ph.split(f"xT{p}", D) for p in (0, 1)]
        raw = [ph.sb(n, c) for n, c in (("main_raw", KT * D), ("side_raw", KT * SIDE), ("up_raw", D))]
        main, side, up = (ph.split(n, c) for n, c in (("main", KT * D), ("side", KT * SIDE), ("up", D)))
        HALVES = (slice(0, KT * D // 2), slice(KT * D // 2, KT * D))
        parts = (("main_loaded0", raw[0], main, HALVES[0]), ("main_loaded1", raw[0], main, HALVES[1]),
                 ("side_loaded", raw[1], side, slice(0, KT * SIDE)), ("up_loaded", raw[2], up, slice(0, D)))
        kept = ph.sb("kept", B * SIDE)
        bias_row = ph.sb("bias", D) if bias is not None else None
        routed, rT = ph.sb("routed", B * ER), ph.split("rT", B * S)
        s = ph.sems(NORM_SEMS + " main_loaded0 main_loaded1 side_loaded up_loaded rows bias_loaded w_hi w_lo biased main_mm side_mm added kept"
                    " chain routed routedT rT_hi rT_lo up_mm summed_up")
        route = Route(ph, C, extra)
        bank_main, bank_side = (C.ps[:, blk(k, BANK)] for k in (0, 1))
        bank_xT, bank_rT, bank_up = ([C.ps[:, blk(k + p, BANK)] for p in (0, 1)] for k in (2, 4, 6))
        bank_route = bank_main
        block = ctx.enter_context(nc.Block())

        def x_of(i):
            return C.x[:, blk(i, D)]

        def tiles(pair, n):
            return [tuple(h[:, k * n:(k + 1) * n] for h in pair) for k in range(KT)]

        @block.sync
        def _(sp):
            sp.dma_start(raw[0][:, HALVES[0]], w_main[:, HALVES[0]]).then_inc(s["main_loaded0"], 16)
            sp.dma_start(raw[2][:, :], w_up).then_inc(s["up_loaded"], 16)
            if bias is not None:
                sp.dma_start(bias_row[:, :], bias.partition_broadcast(128)).then_inc(s["bias_loaded"], 16)
            route.load(sp, s["rows"])

        @block.gpsimd
        def _(pool):
            norm_gpsimd(pool, C, s, t)
            if bias is not None:
                pool.wait_ge(s["bias_loaded"], 16)
                with pool.Fori(0, B) as i:
                    pool.wait_ge(s["xn"], i + 1)
                    pool.tensor_tensor(x_of(i), x_of(i), bias_row[:, :], ALU.add).then_inc(s["biased"], 1)
            route.gpsimd(pool)

        @block.tensor
        def _(pe):
            def front(i, p):
                norm_tensor(pe, C, s, t.xn[p][:, :], bank_xT[p], i)

            def back(i, p):
                lhs = tiles(xT[p], S)
                pe.wait_ge(s["w_lo"], 3)
                pe.wait_ge(s["xT_lo"], i + 1)
                wait_from_one(pe, s["added"], i)
                matmul_tiles(pe, bank_main, lhs, tiles(main, D)).then_inc(s["main_mm"], 1)
                wait_from_one(pe, s["kept"], i)
                matmul_tiles(pe, bank_side[:, 0:SIDE], lhs, tiles(side, SIDE)).then_inc(s["side_mm"], 1)
            in_pairs(pe, front, back)
            route.tensor(pe, bank_route)

            for h in (0, 1):
                pe.wait_ge(s["routed"], h + 1)
                for j in range(B // 2):
                    last = pe.transpose(bank_rT[h][:, j * S:(j + 1) * S], routed[:, (h * (B // 2) + j) * ER:][:, 0:ER],
                                        C.ident[:, :])
                last.then_inc(s["routedT"], 1)
            pe.wait_ge(s["w_lo"], 4)
            for i in range(B):
                if i % (B // 2) == 0:
                    pe.wait_ge(s["rT_lo"], i // (B // 2) + 1)
                wait_from_one(pe, s["summed_up"], i - 1)
                matmul_split(pe, bank_up[i % 2], tuple(x[:, i * S:(i + 1) * S] for x in rT),
                             (up[0][:, :], up[1][:, :]), True, True).then_inc(s["up_mm"], 1)

        @block.scalar
        def _(act):
            act.dma_start(raw[0][:, HALVES[1]], w_main[:, HALVES[1]]).then_inc(s["main_loaded1"], 16)
            act.dma_start(raw[1][:, :], w_side).then_inc(s["side_loaded"], 16)
            for name, r, pair, cols in parts:
                act.wait_ge(s[name], 16)
                act.activation(pair[0][:, cols], r[:, cols], ACT.Copy).then_inc(s["w_hi"], 1)

            def front(i, p):
                act.wait_ge(s["xnT"], i + 1)
                wait_from_one(act, s["side_mm"], i - 1)
                act.activation(xT[p][0][:, :], bank_xT[p], ACT.Copy).then_inc(s["xT_hi"], 1)
            in_pairs(act, front, lambda i, p: None)
            route.scalar(act)

            for h in (0, 1):
                act.wait_ge(s["routedT"], h + 1)
                act.activation(rT[0][:, h * BANK:(h + 1) * BANK], bank_rT[h], ACT.Copy).then_inc(s["rT_hi"], 1)

        @block.vector
        def _(dve):
            n_link = [0]

            def link(ins):
                n_link[0] += 1
                ins.then_inc(s["chain"], 1)
                dve.wait_ge(s["chain"], n_link[0])

            def split_low(n):
                name, r, pair, cols = parts[n]
                dve.wait_ge(s["w_hi"], n + 1)
                minus(dve, pair[1][:, cols], r[:, cols], pair[0][:, cols]).then_inc(s["w_lo"], 1)

            def split_first_weights():
                for n in range(3):
                    split_low(n)
            moments_vector(dve, C, s, t, split_first_weights)

            def front(i, p):
                next_norm_vector(dve, C, s, t, i, p)
                dve.wait_ge(s["xT_hi"], i + 1)
                minus(dve, xT[p][1][:, :], bank_xT[p], xT[p][0][:, :]).then_inc(s["xT_lo"], 1)

            def back(i, p):
                dve.wait_ge(s["main_mm"], i + 1)
                if bias is not None:
                    dve.wait_ge(s["biased"], i + 1)
                dve.tensor_tensor(x_of(i), x_of(i), bank_main, ALU.add).then_inc(s["added"], 1)
                dve.wait_ge(s["side_mm"], i + 1)
                dve.tensor_copy(kept[:, blk(i, SIDE)], bank_side[:, 0:SIDE]).then_inc(s["kept"], 1)
            in_pairs(dve, front, back)
            split_low(3)
            dve.wait_ge(s["kept"], B)
            dve.wait_ge(s["added"], B)
            route.vector(dve, link, by_sequence(kept[:, :])[:, :, ER:SIDE], bank_route, s["rows"])

            for h in (0, 1):
                part = slice(h * (B // 2), (h + 1) * (B // 2))
                dve.tensor_tensor(by_sequence(routed[:, :])[:, part].rearrange("p b (e r) -> p b e r", e=E),
                                  by_sequence(kept[:, :])[:, part, 0:ER].rearrange("p b (e r) -> p b e r", e=E),
                                  by_sequence(route.route[:, :])[:, part].unsqueeze(3).to_broadcast([128, B // 2, E, R]),
                                  ALU.mult).then_inc(s["routed"], 1)
            for h in (0, 1):
                at = slice(h * BANK, (h + 1) * BANK)
                dve.wait_ge(s["rT_hi"], h + 1)
                minus(dve, rT[1][:, at], bank_rT[h], rT[0][:, at]).then_inc(s["rT_lo"], 1)
            for i in range(B):
                dve.wait_ge(s["up_mm"], i + 1)
                dve.scalar_tensor_tensor(x_of(i), bank_up[i % 2], scale, x_of(i), ALU.mult, ALU.add).then_inc(s["summed_up"], 1)



HQ = 4
HD = 128
GROUPS = 8
UNIT = 4
CHUNK = KT * HD
QK_EPS = 1e-5


def norm_all(nc, C, tag, xT, bias=None, prefetch=None):
    with ExitStack() as ctx:
        ph = Phase(nc, ctx, tag)
        t = NormBuffers(ph)
        s = ph.sems(NORM_SEMS + " bias_loaded biased")
        bias_row = ph.sb("bias", D) if bias is not None else None
        bank = [C.ps[:, blk(p, BANK)] for p in (0, 1)]
        block = ctx.enter_context(nc.Block())

        def xT_of(half, i):
            return half[:, :].rearrange("p (k t) -> p k t", k=KT)[:, :, blk(i, S)]

        @block.sync
        def _(sp):
            if bias is not None:
                sp.dma_start(bias_row[:, :], bias.partition_broadcast(128)).then_inc(s["bias_loaded"], 16)
            if prefetch:
                prefetch(sp)

        @block.gpsimd
        def _(pool):
            norm_gpsimd(pool, C, s, t)
            if bias is not None:
                pool.wait_ge(s["bias_loaded"], 16)
                with pool.Fori(0, B) as i:
                    pool.wait_ge(s["xn"], i + 1)
                    pool.tensor_tensor(C.x[:, blk(i, D)], C.x[:, blk(i, D)], bias_row[:, :], ALU.add).then_inc(s["biased"], 1)

        @block.tensor
        def _(pe):
            in_pairs(pe, lambda i, p: norm_tensor(pe, C, s, t.xn[p][:, :], bank[p], i), nothing)

        @block.scalar
        def _(act):
            def front(i, p):
                act.wait_ge(s["xnT"], i + 1)
                act.activation(xT_of(xT[0], i), tiles_of(bank[p]), ACT.Copy).then_inc(s["xT_hi"], 1)
            in_pairs(act, front, nothing)

        @block.vector
        def _(dve):
            def front(i, p):
                next_norm_vector(dve, C, s, t, i, p)
                dve.wait_ge(s["xT_hi"], i + 1)
                minus(dve, xT_of(xT[1], i), tiles_of(bank[p]), xT_of(xT[0], i)).then_inc(s["xT_lo"], 1)
            moments_vector(dve, C, s, t)
            in_pairs(dve, front, nothing)


def attention_phase(nc, C, tag, wkv, wq, wo, q_norm=None, k_norm=None, mask=None, bq=None, bk=None, bv=None, bo=None):
    normed = q_norm is not None
    with ExitStack() as ctx:
        ph = Phase(nc, ctx, tag)
        xT = ph.split("xT", KT * B * S)
        raw = [ph.sb(f"raw{k}", CHUNK) for k in (0, 1)]
        s = ph.sems("raw_in0 raw_in1 chunk_hi wo_hi split0 split1 columns k_mm k_hi k_lo kn q_mm q32 q_hi q_lo vT_mm vT v_mm v_hi v_lo"
                    " s_mm raw_max neg_max exped inverse probs pT_mm pT_hi pT_lo av_mm o32 oT_hi oT_lo o_mm added")

        if normed:
            mask_t, weight, q_col = ph.sb("mask", S), ph.sb("weight", 1), ph.sb("q_col", 1)
            small_loads = ((weight, k_norm), (q_col, q_norm), (mask_t, mask))
        else:
            bq_cols, bk_cols, bv_cols = ph.sb("bq_cols", GROUPS * HQ), ph.sb("bk_cols", GROUPS), ph.sb("bv_cols", GROUPS)
            small_loads = ((bq_cols, bq), (bk_cols, bk), (bv_cols, bv))

        def prefetch(sp):
            for dst, src in small_loads:
                sp.dma_start(dst[:, :], src).then_inc(s["columns"], 16)
            sp.dma_start(raw[0][:, :], wkv[0, 0]).then_inc(s["raw_in0"], 16)
            sp.dma_start(raw[1][:, :], wq[0, 0]).then_inc(s["raw_in1"], 16)
        norm_all(nc, C, tag + "n", xT, bo, prefetch)
        wk_s, wq_s = ph.split("wk", CHUNK), ph.split("wq", HQ * CHUNK)
        wv_s, wo_s = ph.split("wv", CHUNK), ph.split("wo", 2 * HQ * D)
        kT, qT = [ph.split(f"kT{p}", UNIT * S) for p in (0, 1)], [ph.split(f"qT{p}", HQ * UNIT * S) for p in (0, 1)]
        vT, v_s = ph.sb("vT", UNIT * S), [ph.split(f"v{p}", HD) for p in (0, 1)]
        probs, pT, oT = ph.sb("probs", HQ * S), ph.split("pT", HQ * S), ph.split("oT", HQ * S)
        neg_max, total = ph.sb("neg_max", HQ), ph.sb("total", HQ)
        kn = ph.sb("kn", UNIT * S)
        if normed:
            squares, k_squares = ph.sb("squares", UNIT * S), ph.sb("k_squares", UNIT * S)
            k_scale, k_diagonal = ph.sb("k_scale", UNIT), k_squares
            eps = ph.sb("eps", 1)
            q_scale = [ph.sb(f"q_scale{p}", HQ * UNIT) for p in (0, 1)]
            sn = ph.sems("weight eps squares qs_mm q_eps q_scale k_squares k_copied k_eps k_scale k_diagonal kb_mm masked")
        else:
            q32, o32 = ph.sb("q32", UNIT * S), ph.sb("o32", HQ * S)
        bank_k, bank_q, bank_v, bank_s0, bank_s1, bank_pT, bank_o, bank_out = (C.ps[:, blk(k, BANK)] for k in range(8))
        bank_s = (bank_s0, bank_s1)
        q_sums, k_sums = bank_v[:, 2 * HD:2 * HD + UNIT], bank_v[:, 2 * HD + UNIT:2 * HD + 2 * UNIT]
        SCALE = HD ** -0.5
        KEYS_AT = 2
        block = ctx.enter_context(nc.Block())

        def head(tile, h, width=128):
            return tile[:, h * width:(h + 1) * width]

        def heads(tile):
            return tile.rearrange("p (h c) -> p h c", h=HQ)

        def ahead(g, b, n):
            return (g + (b + n) // B, (b + n) % B)

        def number(g, b):
            return g * B + b

        def steps(eng, step):
            for b in range(B):
                step(0, b)
            with eng.Fori(1, GROUPS - 2) as g:
                for b in range(B):
                    step(g, b)
            for g in (GROUPS - 2, GROUPS - 1):
                for b in range(B):
                    step(g, b)

        def q_bank(P):
            return bank_out if isinstance(P, int) and P in (1, 3) else bank_q

        def exists(g):
            return not (isinstance(g, int) and g >= GROUPS)

        K_CHUNK, Q_CHUNK, V_CHUNK, O_CHUNK, CHUNKS = 0, 1, 5, 6, 10

        def home(c):
            pair, at = (wk_s, 0) if c == K_CHUNK else (wv_s, 0) if c == V_CHUNK else (wq_s, (c - Q_CHUNK) * CHUNK)
            return tuple(x[:, at:at + CHUNK] for x in pair)

        def nth(g, c):
            return g * (CHUNKS // 2) + c // 2 + 1

        def chunk_in(eng, g, c):
            eng.wait_ge(s[f"raw_in{c % 2}"], 16 * nth(g, c))

        def chunk_split(eng, g, c):
            eng.wait_ge(s[f"split{c % 2}"], nth(g, c))

        @block.sync
        def _(sp):
            def load_chunk(g, c):
                wait_from_one(sp, s[f"split{c % 2}"], nth(g, c) - 1)
                src = (wkv[bass.ds(g, 1), 0] if c == K_CHUNK else wkv[bass.ds(g, 1), 1] if c == V_CHUNK
                       else wq[bass.ds(g, 1), c - Q_CHUNK] if c < O_CHUNK else wo[bass.ds(g, 1), c - O_CHUNK])
                sp.dma_start(raw[c % 2][:, :], src.rearrange("a p c -> p (a c)")).then_inc(s[f"raw_in{c % 2}"], 16)

            for n in range(2, GROUPS * CHUNKS):
                load_chunk(n // CHUNKS, n % CHUNKS)

        @block.gpsimd
        def _(pool):
            if normed:
                pool.memset(eps[:, :], HD * QK_EPS).then_inc(sn["eps"], 1)
                pool.wait_ge(sn["eps"], 1)

            def split_chunk(g, c):
                hi, lo = home(c)
                chunk_in(pool, g, c)
                pool.tensor_tensor(hi, raw[c % 2][:, :], C.ones[:, 0:1].to_broadcast([128, CHUNK]), ALU.mult).then_inc(s["chunk_hi"], 1)
                pool.wait_ge(s["chunk_hi"], O_CHUNK * g + c + 1)
                minus(pool, lo, raw[c % 2][:, :], hi).then_inc(s[f"split{c % 2}"], 1)

            def normalise(t):
                pool.wait_ge(s["inverse"], t + 1)
                pool.tensor_tensor(heads(probs[:, :]), heads(probs[:, :]), along_last(total[:, :], S), ALU.mult).then_inc(s["probs"], 1)

            def query_scale(P, unit, h):
                pool.wait_ge(sn["q_eps"], P + 1)
                out = q_scale[unit][:, h * UNIT:(h + 1) * UNIT]
                pool.tensor_tensor(out, out, C.neg_half[:, 0:UNIT], ALU.pow).then_inc(sn["q_scale"], 1)

            def key_scale(u):
                pool.wait_ge(sn["k_eps"], u + 1)
                pool.tensor_tensor(k_scale[:, :], k_scale[:, :], C.neg_half[:, 0:UNIT], ALU.pow).then_inc(sn["k_scale"], 1)
            if normed:
                for P in range(UNIT):
                    query_scale(P, 0, P)
                    if P == 0:
                        key_scale(0)
            normalise(0)
            pool.wait_ge(s["q_mm"], UNIT + 1)
            split_chunk(1, K_CHUNK)
            split_chunk(1, Q_CHUNK)

            def step(g, b):
                t = number(g, b)
                gp, bp = ahead(g, b, 5)
                if normed and exists(ahead(g, b, 4)[0]):
                    query_scale(t + 4, (b + 4) // UNIT % 2, (b + 4) % UNIT)
                    if (b + 4) % UNIT == 0:
                        key_scale(g * 2 + (b + 4) // UNIT)
                if exists(gp + 1):
                    if bp == 4:
                        pool.wait_ge(s["q_mm"], t + 6)
                        split_chunk(gp + 1, K_CHUNK)
                    if bp >= 4:
                        pool.wait_ge(s["q_mm"], t + 6)
                        split_chunk(gp + 1, Q_CHUNK + bp - 4)
                if b == 3 and exists(g + 1):
                    pool.wait_ge(s["vT_mm"], g * 2 + 2)
                    split_chunk(g + 1, V_CHUNK)
                if exists(ahead(g, b, 1)[0]):
                    normalise(t + 1)
            steps(pool, step)

        @block.tensor
        def _(pe):
            def project(P, g, b):
                unit, h = b // UNIT, b % UNIT
                if h == 0:
                    if b == 0:
                        chunk_split(pe, g, K_CHUNK)
                    wait_from_one(pe, s["vT"], g * 2 + unit)
                    matmul_tiles(pe, bank_k, [tuple(head(x, k) for x in wk_s) for k in range(KT)],
                                 tokens(C.cT, unit)).then_inc(s["k_mm"], 1)
                if unit == 0:
                    chunk_split(pe, g, Q_CHUNK + h)
                wait_from_one(pe, s["q_lo"], P - 1 if isinstance(P, int) and P <= UNIT else P)
                matmul_tiles(pe, q_bank(P), [tuple(head(x, h * KT + k) for x in wq_s) for k in range(KT)],
                             tokens(xT, unit)).then_inc(s["q_mm"], 1)

            def tokens(pair, unit):
                return [tuple(x[:, k * B * S + unit * UNIT * S:k * B * S + (unit + 1) * UNIT * S] for x in pair) for k in range(KT)]

            def sums(P, g, b, n_v):
                pe.wait_ge(sn["squares"], P + 1)
                wait_from_one(pe, sn["q_eps"], P)
                wait_from_one(pe, s["v_lo"], n_v)
                for j in range(UNIT):
                    last = pe.matmul(q_sums[:, j:j + 1], head(squares, j), C.ones[:, 0:1], start=True, stop=True)
                if b % UNIT == 0:
                    pe.wait_ge(sn["k_squares"], g * 2 + b // UNIT + 1)
                    for j in range(UNIT):
                        last = pe.matmul(k_sums[:, j:j + 1], head(k_squares, j), C.ones[:, 0:1], start=True, stop=True)
                last.then_inc(sn["qs_mm"], 1)
                if b % UNIT == 1:
                    pe.wait_ge(sn["k_diagonal"], g * 2 + b // UNIT + 1)
                    pe.wait_ge(sn["k_copied"], g * 2 + b // UNIT + 1)
                    pe.matmul(bank_k, C.ones[:, :], k_diagonal[:, :], start=True, stop=True).then_inc(sn["kb_mm"], 1)

            def scores(t, g, b):
                unit, j = b // UNIT, b % UNIT
                if j == 0:
                    pe.wait_ge(s["k_lo"], g * 2 + unit + 1)
                    pe.wait_ge(s["q_lo"], UNIT * (g * 2 + unit + 1))
                wait_from_one(pe, sn["masked"] if normed else s["exped"], HQ * (t - 1))
                for h in range(HQ):
                    last = matmul_split(pe, head(bank_s[b % 2], h), tuple(head(x, h * UNIT + j) for x in qT[unit]),
                                        tuple(head(x, j) for x in kT[unit]), True, True)
                last.then_inc(s["s_mm"], 1)

            def project_values(g, unit):
                if unit == 0:
                    chunk_split(pe, g, V_CHUNK)
                pe.wait_ge(s["kn"], g * 2 + unit + 1)
                matmul_tiles(pe, bank_k, [tuple(head(x, k) for x in wv_s) for k in range(KT)],
                             tokens(C.cT, unit)).then_inc(s["vT_mm"], 1)

            def values(t, g, b):
                unit, j = b // UNIT, b % UNIT
                if j == 0:
                    pe.wait_ge(s["vT"], g * 2 + unit + 1)
                wait_from_one(pe, s["v_lo"], t)
                if normed and exists(ahead(g, b, 3)[0]):
                    wait_from_one(pe, sn["q_eps"], t + UNIT)
                pe.transpose(bank_v[:, 0:HD], head(vT, j), C.ident[:, :]).then_inc(s["v_mm"], 1)

            def project_out(t, g, b):
                pe.wait_ge(s["oT_lo"], t + 1)
                if b == 0:
                    for h in (HQ - 2, HQ - 1):
                        chunk_split(pe, g, O_CHUNK + h)
                wait_from_one(pe, s["added"], t)
                turn = g % 2 if isinstance(g, int) else pe.snap(g % 2)
                matmul_tiles(pe, bank_out, [tuple(head(x, h) for x in oT) for h in range(HQ)],
                             [tuple(x[:, bass.ds(turn * (HQ * D) + h * D, D)] for x in wo_s) for h in range(HQ)])\
                    .then_inc(s["o_mm"], 1)
            for P in range(UNIT + 1):
                if P == UNIT:
                    project_values(0, 0)
                project(P, 0, P)
                if normed and P < UNIT:
                    sums(P, 0, P, 0)
            scores(0, 0, 0)
            values(0, 0, 0)
            if normed:
                sums(UNIT, 0, UNIT, 1)

            def step(g, b):
                t = number(g, b)
                next_item, piece = ahead(g, b, 1), ahead(g, b, 5)
                if exists(next_item[0]):
                    scores(t + 1, *next_item)
                if exists(piece[0]):
                    project(t + 5, *piece)
                pe.wait_ge(s["probs"], t + 1)
                wait_from_one(pe, s["pT_lo"], t)
                for h in range(HQ):
                    last = pe.transpose(head(bank_pT, h), head(probs, h), C.ident[:, :])
                last.then_inc(s["pT_mm"], 1)
                if exists(next_item[0]):
                    values(t + 1, *next_item)
                if not (isinstance(t, int) and t == 0):
                    project_out(t - 1, *ahead(g, b, -1))
                if exists(piece[0]) and piece[1] % UNIT == UNIT - 1:
                    project_values(piece[0], piece[1] // UNIT)
                pe.wait_ge(s["pT_lo"], t + 1)
                pe.wait_ge(s["v_lo"], t + 1)
                wait_from_one(pe, s["oT_lo"], t)
                matmul_split(pe, bank_o, tuple(x[:, :] for x in v_s[b % 2]), tuple(x[:, :] for x in pT),
                             True, True).then_inc(s["av_mm"], 1)
                if normed and exists(piece[0]):
                    sums(t + 5, *piece, t + 2)
            steps(pe, step)
            project_out(GROUPS * B - 1, GROUPS - 1, B - 1)

        @block.scalar
        def _(act):
            def split_first(c):
                chunk_in(act, 0, c)
                act.activation(home(c)[0], raw[c % 2][:, :], ACT.Copy).then_inc(s["chunk_hi"], 1)

            def split_wo(g, h):
                chunk_in(act, g, O_CHUNK + h)
                wait_from_one(act, s["o_mm"], B * (g - 1))
                hi = wo_s[0][:, bass.ds((g % 2) * (HQ * D) + h * D, D)]
                act.activation(hi, raw[h % 2][:, :], ACT.Copy).then_inc(s["wo_hi"], 1)

            def keys(u):
                if normed:
                    act.wait_ge(s["k_mm"], u + 1)
                    wait_from_one(act, s["kn"], u)
                    act.activation(k_squares[:, :], bank_k, ACT.Square).then_inc(sn["k_squares"], 1)

            def split_keys(u, unit):
                act.wait_ge(s["kn"], u + 1)
                wait_from_one(act, s["s_mm"], UNIT * (u - 1))
                act.activation(kT[unit][0][:, :], kn[:, :], ACT.Copy).then_inc(s["k_hi"], 1)

            def queries(P, g, b):
                unit, h = b // UNIT, b % UNIT
                act.wait_ge(s["q_mm"] if normed else s["q32"], P + 1)
                if h == 0:
                    wait_from_one(act, s["s_mm"], UNIT * (g * 2 + unit - 1))
                out = head(qT[unit][0], h, UNIT * S)
                if normed:
                    act.activation(out, q_bank(P), ACT.Copy).then_inc(s["q_hi"], 1)
                    wait_from_one(act, sn["qs_mm"], P)
                    act.activation(squares[:, :], q_bank(P), ACT.Square).then_inc(sn["squares"], 1)
                else:
                    act.activation(out, q32[:, :], ACT.Copy).then_inc(s["q_hi"], 1)

            def exps(t, b):
                act.wait_ge(s["neg_max"], t + 1)
                if not normed:
                    wait_from_one(act, s["pT_mm"], t)
                src = probs if normed else bank_s[b % 2]
                for h in range(HQ):
                    act.activation(head(probs, h), head(src, h), ACT.Exp, bias=neg_max[:, h:h + 1],
                                   scale=1.0 if normed else SCALE, accum_out=total[:, h:h + 1]).then_inc(s["exped"], 1)

            def split_v(t, b):
                act.wait_ge(s["v_mm"], t + 1)
                wait_from_one(act, s["av_mm"], t - 1)
                act.activation(v_s[b % 2][0][:, :], bank_v[:, 0:HD], ACT.Copy).then_inc(s["v_hi"], 1)

            def split_oT(t):
                act.wait_ge(s["av_mm"] if normed else s["o32"], t + 1)
                wait_from_one(act, s["o_mm"], t)
                act.activation(oT[0][:, :], bank_o if normed else o32[:, :], ACT.Copy).then_inc(s["oT_hi"], 1)
            for c in range(O_CHUNK):
                split_first(c)
                if c > Q_CHUNK:
                    P = c - Q_CHUNK - 1
                    if P == 0:
                        keys(0)
                    queries(P, 0, P)
                    if P == KEYS_AT:
                        split_keys(0, 0)
            keys(1)
            queries(UNIT, 0, UNIT)
            for h in range(HQ):
                split_wo(0, h)
            split_v(0, 0)
            exps(0, 0)

            def step(g, b):
                t = number(g, b)
                gp, bp = piece = ahead(g, b, 5)
                if not (isinstance(t, int) and t == 0):
                    split_oT(t - 1)
                if 3 <= b < 3 + HQ and exists(g + 1):
                    split_wo(g + 1, b - 3)
                if exists(gp):
                    u = gp * 2 + bp // UNIT
                    if bp % UNIT == 0:
                        keys(u)
                    if bp % UNIT == KEYS_AT:
                        split_keys(u, bp // UNIT)
                act.wait_ge(s["pT_mm"], t + 1)
                wait_from_one(act, s["av_mm"], t)
                act.activation(pT[0][:, :], bank_pT, ACT.Copy).then_inc(s["pT_hi"], 1)
                if exists(ahead(g, b, 1)[0]):
                    split_v(t + 1, (b + 1) % B)
                if exists(gp):
                    queries(t + 5, gp, bp)
                if exists(ahead(g, b, 1)[0]):
                    exps(t + 1, (b + 1) % B)
            steps(act, step)
            split_oT(GROUPS * B - 1)

        @block.vector
        def _(dve):
            def split_first(c):
                dve.wait_ge(s["chunk_hi"], c + 1)
                hi, lo = home(c)
                minus(dve, lo, raw[c % 2][:, :], hi).then_inc(s[f"split{c % 2}"], 1)

            def split_wo(g, h):
                dve.wait_ge(s["wo_hi"], HQ * g + h + 1)
                hi, lo = (x[:, bass.ds((g % 2) * (HQ * D) + h * D, D)] for x in wo_s)
                minus(dve, lo, raw[h % 2][:, :], hi).then_inc(s[f"split{h % 2}"], 1)

            def keys(u, g, b):
                if normed:
                    dve.wait_ge(sn["k_squares"], u + 1)
                    wait_from_one(dve, s["k_lo"], u)
                    dve.tensor_copy(kn[:, :], bank_k).then_inc(sn["k_copied"], 1)
                else:
                    dve.wait_ge(s["k_mm"], u + 1)
                    wait_from_one(dve, s["k_lo"], u)
                    dve.tensor_scalar(kn[:, :], bank_k, bk_cols[:, bass.ds(g, 1)], None, ALU.add).then_inc(s["kn"], 1)

            def take_values(u):
                dve.wait_ge(s["vT_mm"], u + 1)
                wait_from_one(dve, s["v_mm"], u * UNIT)
                dve.tensor_copy(vT[:, :], bank_k).then_inc(s["vT"], 1)

            def key_eps(u):
                dve.wait_ge(sn["qs_mm"], UNIT * u + 1)
                dve.tensor_scalar(k_scale[:, :], k_sums, HD * QK_EPS, None, ALU.add).then_inc(sn["k_eps"], 1)

            def key_diagonal(u):
                dve.wait_ge(sn["k_scale"], u + 1)
                dve.tensor_tensor(k_diagonal[:, :].rearrange("p (j t) -> p j t", j=UNIT), along_last(k_scale[:, :], S),
                                  C.ident[:, :].unsqueeze(1).to_broadcast([128, UNIT, S]), ALU.mult).then_inc(sn["k_diagonal"], 1)

            def scale_keys(u):
                dve.wait_ge(sn["kb_mm"], u + 1)
                dve.wait_ge(sn["k_copied"], u + 1)
                dve.scalar_tensor_tensor(kn[:, :], kn[:, :], weight[:, 0:1], bank_k, ALU.mult, ALU.mult).then_inc(s["kn"], 1)

            def split_keys(u, unit):
                dve.wait_ge(s["k_hi"], u + 1)
                minus(dve, kT[unit][1][:, :], kn[:, :], kT[unit][0][:, :]).then_inc(s["k_lo"], 1)

            def queries(P, g, b):
                unit, h = b // UNIT, b % UNIT
                hi, lo = (head(x, h, UNIT * S) for x in qT[unit])
                if normed:
                    dve.wait_ge(sn["squares"], P + 1)
                    minus(dve, lo, q_bank(P), hi).then_inc(s["q_lo"], 1)
                else:
                    dve.wait_ge(s["q_hi"], P + 1)
                    minus(dve, lo, q32[:, :], hi).then_inc(s["q_lo"], 1)

            def bias_queries(P, g, h):
                dve.wait_ge(s["q_mm"], P + 1)
                wait_from_one(dve, s["q_lo"], P)
                dve.tensor_scalar(q32[:, :], q_bank(P), bq_cols[:, bass.ds(g * HQ + h, 1)], None, ALU.add).then_inc(s["q32"], 1)

            def query_eps(P, g, b):
                unit, h = b // UNIT, b % UNIT
                dve.wait_ge(sn["qs_mm"], P + 1)
                if h == 0:
                    wait_from_one(dve, sn["masked"], HQ * UNIT * (g * 2 + unit - 1))
                dve.tensor_scalar(q_scale[unit][:, h * UNIT:(h + 1) * UNIT], q_sums, HD * QK_EPS, None, ALU.add).then_inc(sn["q_eps"], 1)

            def add_mask(t, b):
                unit, j = b // UNIT, b % UNIT
                dve.wait_ge(s["s_mm"], t + 1)
                if j == 0:
                    pieces = t + UNIT
                    dve.wait_ge(sn["q_scale"], pieces)
                wait_from_one(dve, s["pT_mm"], t)
                for h in range(HQ):
                    at = h * UNIT + j
                    dve.scalar_tensor_tensor(head(probs, h), head(bank_s[b % 2], h), q_scale[unit][:, at:at + 1], mask_t[:, :],
                                             ALU.mult, ALU.add).then_inc(sn["masked"], 1)

            def maximum(t, b):
                wait_from_one(dve, s["exped"], HQ * t)
                if normed:
                    dve.wait_ge(sn["masked"], HQ * (t + 1))
                    dve.tensor_reduce(neg_max[:, :], heads(probs[:, :]), AX.X, ALU.max, negate=True).then_inc(s["neg_max"], 1)
                else:
                    dve.wait_ge(s["s_mm"], t + 1)
                    dve.tensor_reduce(neg_max[:, :], heads(bank_s[b % 2]), AX.X, ALU.max).then_inc(s["raw_max"], 1)
                    dve.wait_ge(s["raw_max"], t + 1)
                    dve.tensor_scalar(neg_max[:, :], neg_max[:, :], -SCALE, None, ALU.mult).then_inc(s["neg_max"], 1)

            def invert(t):
                dve.wait_ge(s["exped"], HQ * (t + 1))
                dve.reciprocal(total[:, :], total[:, :]).then_inc(s["inverse"], 1)

            def split_v(t, b):
                dve.wait_ge(s["v_hi"], t + 1)
                minus(dve, v_s[b % 2][1][:, :], bank_v[:, 0:HD], v_s[b % 2][0][:, :]).then_inc(s["v_lo"], 1)

            def split_oT(t):
                dve.wait_ge(s["oT_hi"], t + 1)
                minus(dve, oT[1][:, :], bank_o if normed else o32[:, :], oT[0][:, :]).then_inc(s["oT_lo"], 1)

            def bias_out(t, g):
                dve.wait_ge(s["av_mm"], t + 1)
                wait_from_one(dve, s["oT_lo"], t)
                dve.tensor_scalar(o32[:, :], bank_o, bv_cols[:, bass.ds(g, 1)], None, ALU.add).then_inc(s["o32"], 1)

            def add_out(t, b):
                dve.wait_ge(s["o_mm"], t + 1)
                x_b = C.x[:, blk(b, D)]
                dve.tensor_tensor(x_b, x_b, bank_out, ALU.add).then_inc(s["added"], 1)
            dve.wait_ge(s["columns"], 48)
            if normed:
                dve.scalar_tensor_tensor(weight[:, :], weight[:, :], HD ** 0.5, q_col[:, :], ALU.mult, ALU.mult).then_inc(sn["weight"], 1)
                dve.wait_ge(sn["weight"], 1)
            for c in range(O_CHUNK):
                split_first(c)
                if c > Q_CHUNK:
                    P = c - Q_CHUNK - 1
                    if P == 0:
                        keys(0, 0, 0)
                    if not normed:
                        bias_queries(P, 0, P)
                    queries(P, 0, P)
                    if P == KEYS_AT and not normed:
                        split_keys(0, 0)
                    if normed:
                        if P == 0:
                            key_eps(0)
                        query_eps(P, 0, P)
                        if P == 1:
                            key_diagonal(0)
                        if P == KEYS_AT:
                            scale_keys(0)
                            split_keys(0, 0)
            take_values(0)
            keys(1, 0, UNIT)
            if not normed:
                bias_queries(UNIT, 0, 0)
            queries(UNIT, 0, UNIT)
            for h in range(HQ):
                split_wo(0, h)
            if normed:
                add_mask(0, 0)
            maximum(0, 0)
            split_v(0, 0)
            invert(0)

            def step(g, b):
                t = number(g, b)
                gp, bp = ahead(g, b, 5)
                u = gp * 2 + bp // UNIT
                before = ahead(g, b, 4)
                if not (isinstance(t, int) and t == 0):
                    split_oT(t - 1)
                if 3 <= b < 3 + HQ and exists(g + 1):
                    split_wo(g + 1, b - 3)
                if normed and exists(before[0]):
                    if before[1] % UNIT == 0:
                        key_eps(before[0] * 2 + before[1] // UNIT)
                    query_eps(t + 4, *before)
                if exists(gp):
                    if bp % UNIT == 0:
                        keys(u, gp, bp)
                    if normed and bp % UNIT == 2:
                        scale_keys(u)
                    if not normed:
                        bias_queries(t + 5, gp, bp % UNIT)
                dve.wait_ge(s["pT_hi"], t + 1)
                minus(dve, pT[1][:, :], bank_pT, pT[0][:, :]).then_inc(s["pT_lo"], 1)
                more = exists(ahead(g, b, 1)[0])
                if more:
                    split_v(t + 1, (b + 1) % B)
                if exists(gp):
                    queries(t + 5, gp, bp)
                    if normed and bp % UNIT == 1:
                        key_diagonal(u)
                if more:
                    if normed:
                        add_mask(t + 1, (b + 1) % B)
                    maximum(t + 1, (b + 1) % B)
                if exists(gp):
                    if bp % UNIT == KEYS_AT:
                        split_keys(u, bp // UNIT)
                    if bp % UNIT == UNIT - 1:
                        take_values(u)
                if not normed:
                    bias_out(t, g)
                if more:
                    invert(t + 1)
                if not (isinstance(t, int) and t == 0):
                    add_out(t - 1, (b - 1) % B)
            steps(dve, step)
            split_oT(GROUPS * B - 1)
            add_out(GROUPS * B - 1, B - 1)



HD0 = 16
KV0 = 8
SETS = 4
ROUNDS = KV0 // 2
RH = 2 * SETS
RW = RH * S


def project_small_heads(nc, C, q32, k32, v32, wkv, wq, bk, bq, bv, bo):
    with ExitStack() as ctx:
        ph = Phase(nc, ctx, "p0")
        xT = ph.split("xT", KT * B * S)
        raw, w_s = ph.sb("raw", (2 + SETS) * CHUNK), ph.split("w", (2 + SETS) * CHUNK)
        bk_col, bq_cols, bv_row = ph.sb("bk", 1), ph.sb("bq", SETS), ph.sb("bv", S)
        s = ph.sems("w_in bias_in w_hi w_lo mm taken")
        banks = [C.ps[:, blk(k, BANK)] for k in range(4)]
        K_CHUNK, V_CHUNK, Q_CHUNK = 0, 1, 2
        products = [(K_CHUNK, h) for h in (0, 1)] + [(V_CHUNK, b) for b in range(B)] + \
            [(Q_CHUNK + n, h) for n in range(SETS) for h in (0, 1)]

        def chunk(tile, c):
            return tile[:, c * CHUNK:(c + 1) * CHUNK]

        def load_weights(sp):
            for c in range(2 + SETS):
                src = wkv[c] if c < Q_CHUNK else wq[c - Q_CHUNK]
                sp.dma_start(chunk(raw, c), src).then_inc(s["w_in"], 16)
            sp.dma_start(bk_col[:, :], bk).then_inc(s["bias_in"], 16)
            sp.dma_start(bq_cols[:, :], bq).then_inc(s["bias_in"], 16)
            sp.dma_start(bv_row[:, :], bv.partition_broadcast(128)).then_inc(s["bias_in"], 16)
        norm_all(nc, C, "p0n", xT, bo, load_weights)
        block = ctx.enter_context(nc.Block())

        @block.scalar
        def _(act):
            act.wait_ge(s["w_in"], 16 * (2 + SETS))
            for c in range(2 + SETS):
                act.activation(chunk(w_s[0], c), chunk(raw, c), ACT.Copy).then_inc(s["w_hi"], 1)

        @block.tensor
        def _(pe):
            for n, (c, part) in enumerate(products):
                pe.wait_ge(s["w_lo"], c + 1)
                wait_from_one(pe, s["taken"], n - 3)
                if c == V_CHUNK:
                    lhs = [tuple(x[:, k * B * S + part * S:k * B * S + (part + 1) * S] for x in C.cT) for k in range(KT)]
                    rhs = [tuple(chunk(x, c)[:, k * S:(k + 1) * S] for x in w_s) for k in range(KT)]
                    out = banks[n % 4][:, 0:S]
                else:
                    lhs = [tuple(chunk(x, c)[:, k * S:(k + 1) * S] for x in w_s) for k in range(KT)]
                    moving = C.cT if c == K_CHUNK else xT
                    rhs = [tuple(x[:, k * B * S + part * BANK:k * B * S + (part + 1) * BANK] for x in moving) for k in range(KT)]
                    out = banks[n % 4]
                matmul_tiles(pe, out, lhs, rhs).then_inc(s["mm"], 1)

        @block.vector
        def _(dve):
            for c in range(2 + SETS):
                dve.wait_ge(s["w_hi"], c + 1)
                minus(dve, chunk(w_s[1], c), chunk(raw, c), chunk(w_s[0], c)).then_inc(s["w_lo"], 1)
            dve.wait_ge(s["bias_in"], 48)
            for n, (c, part) in enumerate(products):
                dve.wait_ge(s["mm"], n + 1)
                if c == K_CHUNK:
                    ins = dve.tensor_scalar(k32[:, blk(part, BANK)], banks[n % 4], bk_col[:, 0:1], None, ALU.add)
                elif c == V_CHUNK:
                    ins = dve.tensor_tensor(v32[:, blk(part, S)], banks[n % 4][:, 0:S], bv_row[:, :], ALU.add)
                else:
                    m = c - Q_CHUNK
                    out = q32[:, :].rearrange("p (b n t) -> p b n t", b=B, n=SETS)[:, part * (B // 2):(part + 1) * (B // 2), m, :]
                    ins = dve.tensor_scalar(out, banks[n % 4].rearrange("p (b t) -> p b t", t=S), bq_cols[:, m:m + 1], None, ALU.add)
                ins.then_inc(s["taken"], 1)


def attention_small_heads(nc, C, wkv, wq, wo, bk, bq, bv, bo):
    with ExitStack() as ctx:
        ph = Phase(nc, ctx, "a0")
        q32, k32, v32 = ph.sb("q32", SETS * B * S), ph.sb("k32", B * S), ph.sb("v32", B * S)
        project_small_heads(nc, C, q32, k32, v32, wkv, wq, bk, bq, bv, bo)
        wo_raw, wo_s = ph.sb("wo_raw", SETS * D), ph.split("wo", SETS * D)
        q_s = [ph.split(f"q{p}", SETS * S) for p in (0, 1)]
        k_s = [ph.split(f"k{p}", 2 * S) for p in (0, 1)]
        v_s = [ph.split(f"v{p}", KV0 * S) for p in (0, 1)]
        probs = [ph.sb(f"probs{p}", RW) for p in (0, 1)]
        pT = [ph.split(f"pT{p}", RW) for p in (0, 1)]
        raw_max, neg_max, total = ([ph.sb(f"{n}{p}", RH) for p in (0, 1)] for n in ("raw_max", "neg_max", "total"))
        oT, keep = ph.split("oT", SETS * S), ph.sb("keep", 2)
        s = ph.sems("wo_in wo_hi wo_lo keep zeroed q_hi q_lo k_hi k_lo v_hi v_lo s_mm raw_max neg_max exped inverse probs"
                    " pT_mm pT_hi pT_lo av_mm oT_hi oT_lo o_mm added")
        bank_s = [C.ps[:, 2 * BANK * p:2 * BANK * (p + 1)] for p in (0, 1)]
        bank_pT, bank_oT, bank_out = C.ps[:, 4 * BANK:6 * BANK], C.ps[:, 6 * BANK:7 * BANK], C.ps[:, 7 * BANK:8 * BANK]
        SCALE = HD0 ** -0.5
        block = ctx.enter_context(nc.Block())

        def items(eng, step):
            for r in range(ROUNDS):
                step(0, r, 0)
            with eng.Fori(0, B // 2 - 1) as pair:
                for n in (1, 2):
                    for r in range(ROUNDS):
                        step(pair * 2 + n, r, n % 2)
            for r in range(ROUNDS):
                step(B - 1, r, 1)

        def exists(i):
            return not (isinstance(i, int) and i >= B)

        def diagonal(tile):
            whole = tile[:, :]
            return bass.AP(whole.tensor, whole.offset, [whole.ap[0], [S + HD0, KV0], [1, HD0]])

        @block.sync
        def _(sp):
            sp.dma_start(wo_raw[:, :], wo).then_inc(s["wo_in"], 16)

        @block.gpsimd
        def _(pool):
            def normalise(R, p):
                pool.wait_ge(s["inverse"], R + 1)
                v = probs[p][:, :].rearrange("p (h t) -> p h t", h=RH)
                pool.tensor_tensor(v, v, along_last(total[p][:, :], S), ALU.mult).then_inc(s["probs"], 1)
            normalise(0, 0)

            def step(i, r, p):
                if r < ROUNDS - 1 or exists(i + 1):
                    normalise(i * ROUNDS + r + 1, (r + 1) % 2)
            items(pool, step)

        @block.tensor
        def _(pe):
            def scores(i, r, p):
                R = i * ROUNDS + r
                if r == 0:
                    pe.wait_ge(s["q_lo"], i + 1)
                    pe.wait_ge(s["k_lo"], 2 * (i + 1))
                wait_from_one(pe, s["exped"], RH * (R - 1))
                rows = slice(32 * r, 32 * r + 32)
                for n in range(SETS):
                    last = matmul_split(pe, bank_s[r % 2][:, n * 2 * S:(n + 1) * 2 * S],
                                        tuple(x[rows, n * S:(n + 1) * S] for x in q_s[p]),
                                        tuple(x[rows, :] for x in k_s[p]), True, True)
                last.then_inc(s["s_mm"], 1)

            def turn(i, r):
                R = i * ROUNDS + r
                pe.wait_ge(s["probs"], R + 1)
                wait_from_one(pe, s["pT_lo"], 2 * R)
                for c in (0, 1):
                    for n in range(SETS):
                        last = pe.transpose(bank_pT[:, (c * SETS + n) * S:(c * SETS + n + 1) * S],
                                            probs[r % 2][:, (2 * n + c) * S:(2 * n + c + 1) * S], C.ident[:, :])
                    last.then_inc(s["pT_mm"], 1)

            def mix(i, r, p):
                R = i * ROUNDS + r
                if r == 0:
                    pe.wait_ge(s["v_lo"], i + 1)
                    wait_from_one(pe, s["oT_lo"], i)
                for c in (0, 1):
                    pe.wait_ge(s["pT_lo"], 2 * R + c + 1)
                    kv = 2 * r + c
                    last = matmul_split(pe, bank_oT, tuple(x[:, kv * S:(kv + 1) * S] for x in v_s[p]),
                                        tuple(x[:, c * BANK:(c + 1) * BANK] for x in pT[r % 2]), kv == 0, kv == KV0 - 1)
                last.then_inc(s["av_mm"], 1)

            def project_out(i):
                pe.wait_ge(s["oT_lo"], i + 1)
                wait_from_one(pe, s["added"], i)
                matmul_tiles(pe, bank_out, [tuple(x[:, n * S:(n + 1) * S] for x in oT) for n in range(SETS)],
                             [tuple(x[:, n * D:(n + 1) * D] for x in wo_s) for n in range(SETS)]).then_inc(s["o_mm"], 1)
            pe.wait_ge(s["zeroed"], 4)
            scores(0, 0, 0)
            scores(0, 1, 0)
            pe.wait_ge(s["wo_lo"], 1)

            def step(i, r, p):
                if r < ROUNDS - 2:
                    scores(i, r + 2, p)
                elif exists(i + 1):
                    scores(i + 1, r + 2 - ROUNDS, 1 - p)
                if r > 0:
                    mix(i, r - 1, p)
                elif not (isinstance(i, int) and i == 0):
                    mix(i - 1, ROUNDS - 1, 1 - p)
                turn(i, r)
                if r == 1 and not (isinstance(i, int) and i == 0):
                    project_out(i - 1)
            items(pe, step)
            mix(B - 1, ROUNDS - 1, 1)
            project_out(B - 1)

        @block.scalar
        def _(act):
            def stage_qk(i, p):
                wait_from_one(act, s["s_mm"], ROUNDS * (i - 1))
                act.activation(q_s[p][0][:, :], q32[:, bass.ds((i % B) * (SETS * S), SETS * S)], ACT.Copy).then_inc(s["q_hi"], 1)
                for c in (0, 1):
                    act.activation(k_s[p][0][:, c * S:(c + 1) * S], k32[:, bass.ds((i % B) * S, S)], ACT.Copy,
                                   scale=keep[:, c:c + 1]).then_inc(s["k_hi"], 1)

            def stage_v(i, p):
                wait_from_one(act, s["av_mm"], ROUNDS * (i - 1))
                v = v32[:, bass.ds((i % B) * S, S)].rearrange("p (k d) -> p k d", k=KV0)
                act.activation(diagonal(v_s[p][0]), v, ACT.Copy).then_inc(s["v_hi"], 1)

            def exps(R, p):
                act.wait_ge(s["neg_max"], R + 1)
                wait_from_one(act, s["pT_mm"], 2 * (R - 1))
                wait_from_one(act, s["probs"], R - 1)
                for h in range(RH):
                    act.activation(probs[p][:, h * S:(h + 1) * S], bank_s[p][:, h * S:(h + 1) * S], ACT.Exp,
                                   bias=neg_max[p][:, h:h + 1], scale=SCALE, accum_out=total[p][:, h:h + 1]).then_inc(s["exped"], 1)

            def split_pT(R, p):
                wait_from_one(act, s["av_mm"], R - 1)
                for c in (0, 1):
                    act.wait_ge(s["pT_mm"], 2 * R + c + 1)
                    at = slice(c * BANK, (c + 1) * BANK)
                    act.activation(pT[p][0][:, at], bank_pT[:, at], ACT.Copy).then_inc(s["pT_hi"], 1)

            def split_oT(i):
                act.wait_ge(s["av_mm"], ROUNDS * (i + 1))
                wait_from_one(act, s["o_mm"], i)
                act.activation(oT[0][:, :], bank_oT, ACT.Copy).then_inc(s["oT_hi"], 1)
            act.wait_ge(s["keep"], 1)
            stage_qk(0, 0)
            act.wait_ge(s["zeroed"], 4)
            stage_v(0, 0)
            act.wait_ge(s["wo_in"], 16)
            act.activation(wo_s[0][:, :], wo_raw[:, :], ACT.Copy).then_inc(s["wo_hi"], 1)
            exps(0, 0)

            def step(i, r, p):
                R = i * ROUNDS + r
                if not (isinstance(R, int) and R == 0):
                    split_pT(R - 1, (r - 1) % 2)
                if r == 0 and exists(i + 1):
                    stage_qk(i + 1, 1 - p)
                if r < ROUNDS - 1 or exists(i + 1):
                    exps(R + 1, (r + 1) % 2)
                if r == 0 and not (isinstance(i, int) and i == 0):
                    split_oT(i - 1)
                if r == 2 and exists(i + 1):
                    stage_v(i + 1, 1 - p)
            items(act, step)
            split_pT(B * ROUNDS - 1, 1)
            split_oT(B - 1)

        @block.vector
        def _(dve):
            def stage_qk(i, p):
                dve.wait_ge(s["q_hi"], i + 1)
                minus(dve, q_s[p][1][:, :], q32[:, bass.ds((i % B) * (SETS * S), SETS * S)], q_s[p][0][:, :]).then_inc(s["q_lo"], 1)
                dve.wait_ge(s["k_hi"], 2 * (i + 1))
                for c in (0, 1):
                    hi, lo = (x[:, c * S:(c + 1) * S] for x in k_s[p])
                    dve.scalar_tensor_tensor(lo, k32[:, bass.ds((i % B) * S, S)], keep[:, c:c + 1], hi.bitcast(F32), ALU.mult,
                                             ALU.subtract).then_inc(s["k_lo"], 1)

            def stage_v(i, p):
                dve.wait_ge(s["v_hi"], i + 1)
                v = v32[:, bass.ds((i % B) * S, S)].rearrange("p (k d) -> p k d", k=KV0)
                minus(dve, diagonal(v_s[p][1]), v, diagonal(v_s[p][0])).then_inc(s["v_lo"], 1)

            def maxima(R, p):
                dve.wait_ge(s["s_mm"], R + 1)
                wait_from_one(dve, s["neg_max"], R - 1)
                dve.tensor_reduce(raw_max[p][:, :], bank_s[p].rearrange("p (h t) -> p h t", h=RH), AX.X, ALU.max).then_inc(s["raw_max"], 1)
                dve.wait_ge(s["raw_max"], R + 1)
                wait_from_one(dve, s["exped"], RH * (R - 1))
                dve.tensor_scalar(neg_max[p][:, :], raw_max[p][:, :], -SCALE, None, ALU.mult).then_inc(s["neg_max"], 1)

            def invert(R, p):
                dve.wait_ge(s["exped"], RH * (R + 1))
                dve.reciprocal(total[p][:, :], total[p][:, :]).then_inc(s["inverse"], 1)

            def split_pT(R, p):
                for c in (0, 1):
                    at = slice(c * BANK, (c + 1) * BANK)
                    dve.wait_ge(s["pT_hi"], 2 * R + c + 1)
                    minus(dve, pT[p][1][:, at], bank_pT[:, at], pT[p][0][:, at]).then_inc(s["pT_lo"], 1)

            def split_oT(i):
                dve.wait_ge(s["oT_hi"], i + 1)
                minus(dve, oT[1][:, :], bank_oT, oT[0][:, :]).then_inc(s["oT_lo"], 1)

            def add_out(i):
                dve.wait_ge(s["o_mm"], i + 1)
                x_i = C.x[:, blk(i, D)]
                dve.tensor_tensor(x_i, x_i, bank_out, ALU.add).then_inc(s["added"], 1)
            dve.tensor_reduce(keep[:, :], C.ident[:, :].rearrange("p (a c r) -> p c a r", c=2, r=HD0), AX.XY,
                              ALU.add).then_inc(s["keep"], 1)
            for p in (0, 1):
                for half in (0, 1):
                    dve.tensor_scalar(v_s[p][half][:, :], C.ones[:, 0:1].to_broadcast([128, KV0 * S]), 0.0, None, ALU.mult)\
                        .then_inc(s["zeroed"], 1)
            dve.wait_ge(s["keep"], 1)
            dve.wait_ge(s["zeroed"], 4)
            stage_qk(0, 0)
            stage_v(0, 0)
            dve.wait_ge(s["wo_hi"], 1)
            minus(dve, wo_s[1][:, :], wo_raw[:, :], wo_s[0][:, :]).then_inc(s["wo_lo"], 1)
            maxima(0, 0)
            maxima(1, 1)
            invert(0, 0)

            def step(i, r, p):
                R = i * ROUNDS + r
                if not (isinstance(R, int) and R == 0):
                    split_pT(R - 1, (r - 1) % 2)
                if r == 0 and exists(i + 1):
                    stage_qk(i + 1, 1 - p)
                if r == 2 and not (isinstance(i, int) and i == 0):
                    add_out(i - 1)
                if r < ROUNDS - 2 or exists(i + 1):
                    maxima(R + 2, r % 2)
                if r < ROUNDS - 1 or exists(i + 1):
                    invert(R + 1, (r + 1) % 2)
                if r == 0 and not (isinstance(i, int) and i == 0):
                    split_oT(i - 1)
                if r == 2 and exists(i + 1):
                    stage_v(i + 1, 1 - p)
            items(dve, step)
            split_pT(B * ROUNDS - 1, 1)
            split_oT(B - 1)
            add_out(B - 1)



def attention_transposed(nc, C, context):
    with ExitStack() as ctx:
        ph = Phase(nc, ctx, "a3")
        xT = ph.split("xT", KT * B * S)
        norm_all(nc, C, "a3n", xT)
        c_raw, c_s = ph.sb("c_raw", B * D), ph.split("c", B * D)
        probs, p_s = ph.sb("probs", B * S), ph.split("p", B * S)
        most, total = ph.sb("most", B), ph.sb("total", B)
        s = ph.sems("c_in0 c_in1 c_hi c_lo s_mm most below exped total inverse probs p_hi p_lo o_mm added")
        bank_s, bank_out = ([C.ps[:, blk(k + h, BANK)] for h in (0, 1)] for k in (0, 2))
        HALF = B // 2
        SCALE = S ** -0.5
        block = ctx.enter_context(nc.Block())

        def half(tile, h):
            n = tile.shape[1] // 2
            return tile[:, h * n:(h + 1) * n]

        def by_item(v):
            return v.rearrange("p (b c) -> p b c", b=HALF)

        def spread(v):
            return v.unsqueeze(2).to_broadcast([128, HALF, S])

        @block.sync
        def _(sp):
            for h in (0, 1):
                sp.dma_start(by_item(half(c_raw, h)), context[h * HALF:(h + 1) * HALF].rearrange("b p d -> p b d"))\
                    .then_inc(s[f"c_in{h}"], 16)

        @block.tensor
        def _(pe):
            for i in range(B):
                last = matmul_tiles(pe, bank_s[i // HALF][:, i % HALF * S:(i % HALF + 1) * S],
                                    *([tuple(x[:, k * B * S + i * S:k * B * S + (i + 1) * S] for x in pair) for k in range(KT)]
                                      for pair in (xT, C.cT)))
                if i % HALF == HALF - 1:
                    last.then_inc(s["s_mm"], 1)
            for i in range(B):
                if i % HALF == 0:
                    pe.wait_ge(s["p_lo"], i // HALF + 1)
                    pe.wait_ge(s["c_lo"], i // HALF + 1)
                wait_from_one(pe, s["added"], i - 1)
                matmul_split(pe, bank_out[i % 2], tuple(x[:, i * S:(i + 1) * S] for x in p_s),
                             tuple(x[:, i * D:(i + 1) * D] for x in c_s), True, True).then_inc(s["o_mm"], 1)

        @block.scalar
        def _(act):
            def split_p(h):
                act.wait_ge(s["probs"], h + 1)
                act.activation(half(p_s[0], h), half(probs, h), ACT.Copy).then_inc(s["p_hi"], 1)

            for h in (0, 1):
                act.wait_ge(s[f"c_in{h}"], 16)
                act.activation(half(c_s[0], h), half(c_raw, h), ACT.Copy).then_inc(s["c_hi"], 1)
            for h in (0, 1):
                act.wait_ge(s["below"], h + 1)
                act.activation(half(probs, h), half(probs, h), ACT.Exp, scale=SCALE).then_inc(s["exped"], 1)
                if h == 1:
                    split_p(0)
            split_p(1)

        @block.vector
        def _(dve):
            def below(h):
                dve.wait_ge(s["s_mm"], h + 1)
                dve.tensor_reduce(half(most, h), by_item(bank_s[h]), AX.X, ALU.max).then_inc(s["most"], 1)
                dve.wait_ge(s["most"], h + 1)
                dve.tensor_tensor(by_item(half(probs, h)), by_item(bank_s[h]), spread(half(most, h)), ALU.subtract)\
                    .then_inc(s["below"], 1)

            def split_context(h):
                dve.wait_ge(s["c_hi"], h + 1)
                minus(dve, half(c_s[1], h), half(c_raw, h), half(c_s[0], h)).then_inc(s["c_lo"], 1)

            def normalise(h):
                dve.wait_ge(s["exped"], h + 1)
                dve.tensor_reduce(half(total, h), by_item(half(probs, h)), AX.X, ALU.add).then_inc(s["total"], 1)
                dve.wait_ge(s["total"], h + 1)
                dve.reciprocal(half(total, h), half(total, h)).then_inc(s["inverse"], 1)
                dve.wait_ge(s["inverse"], h + 1)
                dve.tensor_tensor(by_item(half(probs, h)), by_item(half(probs, h)), spread(half(total, h)), ALU.mult)\
                    .then_inc(s["probs"], 1)

            def split(h):
                dve.wait_ge(s["p_hi"], h + 1)
                minus(dve, half(p_s[1], h), half(probs, h), half(p_s[0], h)).then_inc(s["p_lo"], 1)

            def add_out(i):
                dve.wait_ge(s["o_mm"], i + 1)
                x_i = C.x[:, blk(i, D)]
                dve.tensor_tensor(x_i, x_i, bank_out[i % 2], ALU.add).then_inc(s["added"], 1)
            split_context(0)
            below(0)
            normalise(0)
            below(1)
            split(0)
            split_context(1)
            normalise(1)
            for i in range(HALF):
                add_out(i)
                if i == 0:
                    split(1)
            for i in range(HALF, B):
                add_out(i)


E3 = 64
TOP = 8


def bias_experts(nc, C, w_router, router_bias, expert_bias, out):
    with ExitStack() as ctx:
        ph = Phase(nc, ctx, "f3")
        t = NormBuffers(ph)
        xT = [ph.split(f"xT{p}", D) for p in (0, 1)]
        xn_all = ph.sb("xn_all", B * D)
        router_raw, router = ph.sb("router_raw", KT * E3), ph.split("router", KT * E3)
        eb_raw, eb = ph.sb("eb_raw", D), ph.split("eb", D)
        row = ph.sb("row", E3)
        scores, most = ph.sb("scores", B * E3), ph.sb("most", B)
        taken, top, w_sum = ph.sb("taken", B * E3), ph.sb("top", B * TOP), ph.sb("w_sum", B)
        wT = ph.split("wT", B // 2 * S)
        delta = [ph.sb(f"delta{p}", D) for p in (0, 1)]
        s = ph.sems(NORM_SEMS + " w_in row_in w_hi w_lo xn_kept logits_mm scores chain below exped top rest taken w_sum"
                    " takenT wT_hi wT_lo up_mm delta added stored")
        bank_l, bank_wT = (C.ps[:, blk(k, BANK)] for k in (0, 1))
        bank_xT, bank_up = ([C.ps[:, blk(k + p, BANK)] for p in (0, 1)] for k in (2, 4))
        block = ctx.enter_context(nc.Block())

        def x_of(i):
            return C.x[:, blk(i, D)]

        @block.sync
        def _(sp):
            sp.dma_start(router_raw[:, :], w_router).then_inc(s["w_in"], 16)
            for p in (0, 1):
                sp.dma_start(eb_raw[p * E3:(p + 1) * E3, :], expert_bias).then_inc(s["w_in"], 16)
            sp.dma_start(row[:, :], router_bias.partition_broadcast(128)).then_inc(s["row_in"], 16)
            with sp.Fori(0, B) as i:
                sp.wait_ge(s["added"], i + 1)
                sp.dma_start(out[bass.ds(i, 1)].rearrange("a p d -> p (a d)"), x_of(i)).then_inc(s["stored"], 16)
            sp.wait_ge(s["stored"], 16 * B)

        @block.gpsimd
        def _(pool):
            norm_gpsimd(pool, C, s, t)
            for i in range(B):
                pool.wait_ge(s["delta"], i + 1)
                pool.tensor_tensor(x_of(i), x_of(i), delta[i % 2][:, :], ALU.add).then_inc(s["added"], 1)

        @block.tensor
        def _(pe):
            def back(i, p):
                pe.wait_ge(s["w_lo"], 2)
                pe.wait_ge(s["xT_lo"], i + 1)
                wait_from_one(pe, s["scores"], i)
                matmul_tiles(pe, bank_l[:, 0:E3], [tuple(h[:, k * S:(k + 1) * S] for h in xT[p]) for k in range(KT)],
                             [tuple(h[:, k * E3:(k + 1) * E3] for h in router) for k in range(KT)]).then_inc(s["logits_mm"], 1)

            in_pairs(pe, lambda i, p: norm_tensor(pe, C, s, t.xn[p][:, :], bank_xT[p], i), back)
            pe.wait_ge(s["taken"], 1)
            for k in range(B // 2):
                last = pe.transpose(bank_wT[:, k * S:(k + 1) * S], taken[:, k * 2 * E3:(k + 1) * 2 * E3], C.ident[:, :])
            last.then_inc(s["takenT"], 1)
            pe.wait_ge(s["wT_lo"], 1)
            for i in range(B):
                rows, at = slice(i % 2 * E3, (i % 2 + 1) * E3), slice(i // 2 * S, (i // 2 + 1) * S)
                wait_from_one(pe, s["delta"], i - 1)
                matmul_split(pe, bank_up[i % 2], tuple(x[rows, at] for x in wT), tuple(x[rows, :] for x in eb), True, True)\
                    .then_inc(s["up_mm"], 1)

        @block.scalar
        def _(act):
            act.wait_ge(s["w_in"], 48)
            act.activation(router[0][:, :], router_raw[:, :], ACT.Copy).then_inc(s["w_hi"], 1)
            act.activation(eb[0][:, :], eb_raw[:, :], ACT.Copy).then_inc(s["w_hi"], 1)

            def front(i, p):
                act.wait_ge(s["xn"], i + 1)
                act.activation(xn_all[:, blk(i, D)], t.xn[p][:, :], ACT.Copy).then_inc(s["xn_kept"], 1)
                act.wait_ge(s["xnT"], i + 1)
                wait_from_one(act, s["logits_mm"], i - 1)
                act.activation(xT[p][0][:, :], bank_xT[p], ACT.Copy).then_inc(s["xT_hi"], 1)
            in_pairs(act, front, nothing)
            act.wait_ge(s["below"], 1)
            act.activation(scores[:, :], scores[:, :], ACT.Exp).then_inc(s["exped"], 1)

            act.wait_ge(s["takenT"], 1)
            act.activation(wT[0][:, :], bank_wT, ACT.Copy).then_inc(s["wT_hi"], 1)

        @block.vector
        def _(dve):
            n_link = [0]

            def link(ins):
                n_link[0] += 1
                ins.then_inc(s["chain"], 1)
                dve.wait_ge(s["chain"], n_link[0])

            def split_weights():
                dve.wait_ge(s["w_hi"], 1)
                minus(dve, router[1][:, :], router_raw[:, :], router[0][:, :]).then_inc(s["w_lo"], 1)
                dve.wait_ge(s["w_hi"], 2)
                minus(dve, eb[1][:, :], eb_raw[:, :], eb[0][:, :]).then_inc(s["w_lo"], 1)
                dve.wait_ge(s["row_in"], 16)
            moments_vector(dve, C, s, t, split_weights)

            def front(i, p):
                wait_from_one(dve, s["xn_kept"], i)
                next_norm_vector(dve, C, s, t, i, p)
                dve.wait_ge(s["xT_hi"], i + 1)
                minus(dve, xT[p][1][:, :], bank_xT[p], xT[p][0][:, :]).then_inc(s["xT_lo"], 1)

            def back(i, p):
                dve.wait_ge(s["logits_mm"], i + 1)
                dve.tensor_tensor(scores[:, blk(i, E3)], bank_l[:, 0:E3], row[:, :], ALU.add).then_inc(s["scores"], 1)
            in_pairs(dve, front, back)
            dve.wait_ge(s["scores"], B)
            s3 = by_sequence(scores[:, :])
            link(dve.tensor_reduce(most[:, :], s3, AX.X, ALU.max))
            dve.tensor_tensor(s3, s3, along_last(most[:, :], E3), ALU.subtract).then_inc(s["below"], 1)
            dve.wait_ge(s["exped"], 1)
            link(dve.tensor_reduce(most[:, :], s3, AX.X, ALU.add))
            link(dve.reciprocal(most[:, :], most[:, :]))
            link(dve.tensor_tensor(s3, s3, along_last(most[:, :], E3), ALU.mult))
            dve.wait_ge(s["xn_kept"], B)

            def of(tile, i, width):
                return tile[:, i * width:(i + 1) * width]
            for i in range(B):
                dve.max(of(top, i, TOP), of(scores, i, E3)).then_inc(s["top"], 1)
            dve.drain()
            for i in range(B):
                dve.match_replace(of(taken, i, E3), of(top, i, TOP), of(scores, i, E3), 0.0).then_inc(s["rest"], 1)
            dve.wait_ge(s["top"], B)
            dve.tensor_reduce(w_sum[:, :], by_sequence(top[:, :]), AX.X, ALU.add).then_inc(s["w_sum"], 1)
            dve.wait_ge(s["rest"], B)
            dve.tensor_tensor(taken[:, :], scores[:, :], taken[:, :], ALU.subtract).then_inc(s["taken"], 1)
            dve.wait_ge(s["wT_hi"], 1)
            minus(dve, wT[1][:, :], bank_wT, wT[0][:, :]).then_inc(s["wT_lo"], 1)
            dve.wait_ge(s["w_sum"], 1)
            for i in range(B):
                dve.wait_ge(s["up_mm"], i + 1)
                wait_from_one(dve, s["added"], i - 1)
                dve.scalar_tensor_tensor(delta[i % 2][:, :], xn_all[:, blk(i, D)], w_sum[:, i:i + 1], bank_up[i % 2], ALU.mult,
                                         ALU.add).then_inc(s["delta"], 1)




class Core:

    def __init__(self, nc, ctx):
        def sb(name, cols):
            return ctx.enter_context(nc.sbuf_tensor(name, [128, cols], F32))
        self.x = sb("x", B * D)
        self.ident, self.ones, self.neg_half = sb("ident", 128), sb("ones", 128), sb("neg_half", 8)
        self.ln_eps, self.falling = sb("ln_eps", 1), sb("falling", E)
        self.to_exp = sb("to_exp", B * E)
        self.cT = tuple(ctx.enter_context(nc.sbuf_tensor(f"cT_{h}", [128, KT * B * S], F32R)) for h in ("hi", "lo"))
        self.ps = ctx.enter_context(nc.psum_tensor("ps", [128, 8 * BANK], F32))


def build(nc, A, out):
    with ExitStack() as ctx:
        C = Core(nc, ctx)
        set_up(nc, C, A["x"], A["cT"])
        attention_small_heads(nc, C, A["L0_wkv"], A["L0_wq"], A["L0_wo"], A["L0_bk"], A["L0_bq"], A["L0_xattn_bv"],
                              A["L0_xattn_bo"])
        ffn_phase(nc, C, "f0", GateNet, A["L0_main"], A["L0_side"], A["L0_up"], 1.0 / R,
                  extra=[A[n] for n in ("L0_ffn_gb1", "L0_ffn_ln_gamma", "L0_ffn_ln_beta", "L0_gw2", "L0_ffn_gb2")])
        attention_phase(nc, C, "a1", A["L1_wkv"], A["L1_wq"], A["L1_wo"], q_norm=A["L1_xattn_q_norm_w"],
                        k_norm=A["L1_xattn_k_norm_w"], mask=A["mask"])
        ffn_phase(nc, C, "f1", TopTwo, A["L1_main"], A["L1_side"], A["L1_up"], 1.0, bias=A["L1_ffn_b_base"])
        attention_phase(nc, C, "a2", A["L2_wkv"], A["L2_wq"], A["L2_wo"], bq=A["L2_bq"], bk=A["L2_bk"],
                        bv=A["L2_bv"], bo=A["L2_xattn_bo"])
        ffn_phase(nc, C, "f2", MeanRoute, A["L2_main"], A["L2_side"], A["L2_up"], 2.0, bias=A["L2_ffn_b"],
                  extra=[A["L2_ffn_router_b"]])
        attention_transposed(nc, C, A["context"])
        bias_experts(nc, C, A["L3_router"], A["L3_ffn_router_bias"], A["L3_ffn_expert_bias"], out)


def kernel(**inputs):
    import numpy as np
    import concourse.bacc as bacc
    from concourse.bass_utils import run_bass_kernel_spmd

    def tiled(w):
        return np.ascontiguousarray(w.reshape(KT, 128, -1).transpose(1, 0, 2).reshape(128, -1))

    I = {k: np.asarray(v) for k, v in inputs.items()}
    A = {"x": I["x"]}
    for n, main, a, gate, up in (
            ("L0", I["L0_ffn_weight"].T, I["L0_ffn_lora_A"].transpose(1, 0, 2).reshape(D, ER), I["L0_ffn_gw1"].T,
             I["L0_ffn_lora_B"].reshape(ER, D)),
            ("L1", I["L1_ffn_W_base"].T, I["L1_ffn_A"].reshape(ER, D).T, I["L1_ffn_W_gate"].T,
             I["L1_ffn_B"].transpose(0, 2, 1).reshape(ER, D)),
            ("L2", I["L2_ffn_W"].T, I["L2_ffn_A"].reshape(ER, D).T, I["L2_ffn_router_W"].T,
             I["L2_ffn_B"].transpose(0, 2, 1).reshape(ER, D))):
        A[n + "_main"] = tiled(main)
        A[n + "_side"] = tiled(np.concatenate([a, gate], axis=1))
        A[n + "_up"] = np.ascontiguousarray(up)
    A["L0_gw2"] = I["L0_ffn_gw2"].reshape(-1)
    for n in ("L0_ffn_gb1", "L0_ffn_ln_gamma", "L0_ffn_ln_beta", "L0_ffn_gb2", "L1_ffn_b_base", "L2_ffn_b",
              "L2_ffn_router_b"):
        A[n] = I[n]

    def sets(w):
        return w.reshape(KV0, SETS, HD0, -1).transpose(1, 0, 2, 3).reshape(SETS, KV0 * HD0, -1)

    def chunks(w):
        return w.reshape(KT, 128, -1, 128).transpose(2, 1, 0, 3).reshape(-1, 128, CHUNK)
    A["L0_wq"] = chunks(sets(I["L0_xattn_Wq"].T).reshape(D, D).T)
    A["L0_wkv"] = chunks(np.concatenate([I["L0_xattn_Wk"], I["L0_xattn_Wv"]], axis=1))
    A["L0_wo"] = sets(I["L0_xattn_Wo"]).transpose(1, 0, 2).reshape(128, SETS * D)
    A["L0_bq"] = sets(I["L0_xattn_bq"]).reshape(SETS, 128).T
    A["L0_bk"] = I["L0_xattn_bk"].reshape(128, 1)
    A["context"] = I["ctx_4096"]
    A["L3_router"] = tiled(I["L3_ffn_router_weight"].T)
    for n in ("L0_xattn_bv", "L0_xattn_bo", "L3_ffn_router_bias", "L3_ffn_expert_bias"):
        A[n] = I[n]

    A["cT"] = tiled(I["ctx_4096"].reshape(B * S, D).T)
    A["mask"] = I["mask_1x1xSxS2_ff0"].reshape(S, S)

    def heads_apart(w, n):
        return w.reshape(KT, 128, GROUPS, n, HD).transpose(2, 3, 1, 0, 4).reshape(GROUPS, n, 128, CHUNK)

    def k_and_v(k, v):
        return np.concatenate([heads_apart(k, 1), heads_apart(v, 1)], axis=1)

    def columns(b):
        return b.reshape(-1, HD).T
    A["L1_wq"] = heads_apart(I["L1_xattn_Wq"].T, HQ)
    A["L1_wkv"] = k_and_v(I["L1_xattn_Wk"].T, I["L1_xattn_Wv"].T)
    A["L1_wo"] = I["L1_xattn_Wo"].T.reshape(GROUPS, HQ, HD, D)
    A["L1_xattn_q_norm_w"], A["L1_xattn_k_norm_w"] = columns(I["L1_xattn_q_norm_w"]), columns(I["L1_xattn_k_norm_w"])
    A["L2_wq"] = heads_apart(I["L2_xattn_Wq"], HQ)
    wkv, bkv = I["L2_xattn_Wkv"], I["L2_xattn_bkv"]
    A["L2_wkv"] = k_and_v(wkv[:, :GROUPS * HD], wkv[:, GROUPS * HD:])
    A["L2_wo"] = I["L2_xattn_Wo"].reshape(GROUPS, HQ, HD, D)
    A["L2_bq"], A["L2_bk"], A["L2_bv"] = columns(I["L2_xattn_bq"]), columns(bkv[:GROUPS * HD]), columns(bkv[GROUPS * HD:])
    for n in ("L2_xattn_bo",):
        A[n] = I[n]

    nc = bacc.Bacc("TRN2", target_bir_lowering=False, num_devices=1)
    A = {n: np.ascontiguousarray(a) for n, a in A.items()}
    aps = {n: nc.dram_tensor(f"in_{n}", a.shape, mybir.dt.from_np(a.dtype), kind="ExternalInput").ap() for n, a in A.items()}
    out = nc.dram_tensor("out", (B, S, D), F32, kind="ExternalOutput").ap()
    build(nc, aps, out)
    return run_bass_kernel_spmd(nc, [{f"in_{n}": a for n, a in A.items()}], core_ids=[0]).results[0]["out"]
```
